# Optimizing a Trainium2 kernel written in Bass

```python
import numpy as np
import jax
import jax.numpy as jnp

def _softmax(x, axis=-1):
    return jax.nn.softmax(x, axis=axis)

def _gelu(x):
    return jax.nn.gelu(x, approximate=True)

def _silu(x):
    return jax.nn.silu(x)

def _sigmoid(x):
    return jax.nn.sigmoid(x)

def _layernorm(x, axis=-1, eps=1e-05):
    m = jnp.mean(x, axis=axis, keepdims=True)
    v = jnp.var(x, axis=axis, keepdims=True)
    return (x - m) / jnp.sqrt(v + eps)

def _scatter_add(tgt, idx, src, axis=0):
    return tgt.at[idx].add(src)

def _segment_sum(src, seg, n):
    return jax.ops.segment_sum(src, seg, n)
kernel_name = 'mk_recurrent_d2_jaxref_r8_8aaf3b'

def setup_inputs(seed: int=0):
    np.random.seed(seed)
    _w = jnp.asarray

    def _L0_attn_setup():
        import jax, jax.numpy as jnp
        import numpy as np
        D = 128
        H = 16
        KVH = 4
        HD = D // H
        LAT = 32
        WIN = 32
        B, S = (1, 256)
        BASE_G, BASE_L = (1000000.0, 10000.0)
        EPS = 1e-06

        def rmsnorm(x, w):
            return x * jax.lax.rsqrt(jnp.mean(x * x, axis=-1, keepdims=True) + EPS) * w

        def qk_norm(x):
            return x * jax.lax.rsqrt(jnp.mean(x * x, axis=-1, keepdims=True) + EPS)

        def rope(x, base):
            s, hd = (x.shape[-2], x.shape[-1])
            inv_freq = 1.0 / base ** (jnp.arange(0, hd, 2, dtype=jnp.float32) / hd)
            freqs = jnp.arange(s, dtype=jnp.float32)[:, None] * inv_freq[None, :]
            cos, sin = (jnp.cos(freqs), jnp.sin(freqs))
            xe, xo = (x[..., ::2], x[..., 1::2])
            out = jnp.stack([xe * cos - xo * sin, xe * sin + xo * cos], axis=-1)
            return out.reshape(x.shape)

        def split_heads(x, n_heads):
            b, s, _ = x.shape
            return x.reshape(b, s, n_heads, HD).transpose(0, 2, 1, 3)

        def repeat_kv(x):
            return jnp.repeat(x, H // KVH, axis=1)

        def sdpa(q, k, v, mask):
            scores = jnp.einsum('bhqd,bhkd->bhqk', q, k) / np.sqrt(HD).astype(np.float32)
            scores = jnp.where(mask, scores, jnp.float32(-1e+30))
            probs = jax.nn.softmax(scores, axis=-1)
            return jnp.einsum('bhqk,bhkd->bhqd', probs, v)

        def merge_heads(x):
            b, h, s, hd = x.shape
            return x.transpose(0, 2, 1, 3).reshape(b, s, h * hd)

        def global_latent_attn(x, wq, w_kv_down, w_k_up, w_v_up, wo):
            q = split_heads(x @ wq, H)
            latent = x @ w_kv_down
            k = split_heads(latent @ w_k_up, KVH)
            v = split_heads(latent @ w_v_up, KVH)
            q, k = (rope(q, BASE_G), rope(k, BASE_G))
            q, k = (qk_norm(q), qk_norm(k))
            k, v = (repeat_kv(k), repeat_kv(v))
            i = jnp.arange(x.shape[1])
            causal = i[:, None] >= i[None, :]
            return merge_heads(sdpa(q, k, v, causal)) @ wo

        def local_gqa_attn(x, wq, wk, wv, wo):
            q = split_heads(x @ wq, H)
            k = split_heads(x @ wk, KVH)
            v = split_heads(x @ wv, KVH)
            q, k = (rope(q, BASE_L), rope(k, BASE_L))
            q, k = (qk_norm(q), qk_norm(k))
            k, v = (repeat_kv(k), repeat_kv(v))
            i = jnp.arange(x.shape[1])
            diff = i[:, None] - i[None, :]
            mask = (diff >= 0) & (diff < WIN)
            return merge_heads(sdpa(q, k, v, mask)) @ wo
        key = jax.random.key(seed)
        ks = jax.random.split(key, 12)
        std = 0.02
        return {'hidden': jax.random.normal(ks[0], (B, S, D), dtype=jnp.float32), 'norm1_w': jnp.ones((D,), jnp.float32), 'norm2_w': jnp.ones((D,), jnp.float32), 'g_wq': jax.random.normal(ks[1], (D, H * HD), jnp.float32) * std, 'g_kv_down': jax.random.normal(ks[2], (D, LAT), jnp.float32) * std, 'g_k_up': jax.random.normal(ks[3], (LAT, KVH * HD), jnp.float32) * std, 'g_v_up': jax.random.normal(ks[4], (LAT, KVH * HD), jnp.float32) * std, 'g_wo': jax.random.normal(ks[5], (D, D), jnp.float32) * std, 'l_wq': jax.random.normal(ks[6], (D, H * HD), jnp.float32) * std, 'l_wk': jax.random.normal(ks[7], (D, KVH * HD), jnp.float32) * std, 'l_wv': jax.random.normal(ks[8], (D, KVH * HD), jnp.float32) * std, 'l_wo': jax.random.normal(ks[9], (D, D), jnp.float32) * std}
    _L0_attn_in = _L0_attn_setup()

    def _L0_ffn_setup():
        import jax, jax.numpy as jnp
        import numpy as np
        H, F, E_SHARED, E_ROUTED, K = (128, 512, 1, 8, 2)

        def _expert(x, w_up, w_down):
            h = jax.nn.gelu(jnp.einsum('bsh,hf->bsf', x, w_up), approximate=False)
            return jnp.einsum('bsf,fh->bsh', h, w_down)
        key = jax.random.key(seed)
        ks = jax.random.split(key, 6)
        x = jax.random.normal(ks[0], (4, 256, H), dtype=jnp.float32)
        s = 0.02
        shared_up = jax.random.normal(ks[1], (E_SHARED, H, F), dtype=jnp.float32) * s
        shared_down = jax.random.normal(ks[2], (E_SHARED, F, H), dtype=jnp.float32) * s
        routed_up = jax.random.normal(ks[3], (E_ROUTED, H, F), dtype=jnp.float32) * s
        routed_down = jax.random.normal(ks[4], (E_ROUTED, F, H), dtype=jnp.float32) * s
        router_w = jax.random.normal(ks[5], (H, E_ROUTED), dtype=jnp.float32) * s
        return {'x': x, 'shared_up': shared_up, 'shared_down': shared_down, 'routed_up': routed_up, 'routed_down': routed_down, 'router_w': router_w}
    _L0_ffn_in = _L0_ffn_setup()

    def _L1_attn_setup():
        import jax, jax.numpy as jnp
        import numpy as np
        B, S, D, H, R = (8, 128, 128, 8, 32)
        DH = D // H

        def _lowrank(xh, U, V, b):
            t = jnp.einsum('bshd,hrd->bshr', xh, V)
            return jnp.einsum('bshr,hdr->bshd', t, U) + b
        key = jax.random.key(seed)
        ks = jax.random.split(key, 10)
        p = lambda k, shape: jax.random.normal(k, shape, dtype=jnp.float32) * 0.02
        return {'x': jax.random.normal(ks[0], (B, S, D), dtype=jnp.float32), 'Uq': p(ks[1], (H, DH, R)), 'Vq': p(ks[2], (H, R, DH)), 'bq': p(ks[3], (H, DH)), 'Uk': p(ks[4], (H, DH, R)), 'Vk': p(ks[5], (H, R, DH)), 'bk': p(ks[6], (H, DH)), 'Uv': p(ks[7], (H, DH, R)), 'Vv': p(ks[8], (H, R, DH)), 'bv': p(ks[9], (H, DH))}
    _L1_attn_in = _L1_attn_setup()

    def _L1_ffn_setup():
        import jax, jax.numpy as jnp
        import numpy as np
        HIDDEN_SIZE = 128
        NUM_EXPERTS = 8
        MOE_INTERMEDIATE_SIZE = 176
        NUM_EXPERTS_PER_TOK = 2
        SHARED_EXPERT_INTERMEDIATE_SIZE = 352
        B, T = (2, 128)
        W_SCALE = 0.02
        key = jax.random.key(seed)
        ks = jax.random.split(key, 8)
        H, E, I, SI = (HIDDEN_SIZE, NUM_EXPERTS, MOE_INTERMEDIATE_SIZE, SHARED_EXPERT_INTERMEDIATE_SIZE)
        return {'x': jax.random.normal(ks[0], (B, T, H), jnp.float32), 'gate_w': jax.random.normal(ks[1], (E, H), jnp.float32) * W_SCALE, 'experts_gate_up': jax.random.normal(ks[2], (E, 2 * I, H), jnp.float32) * W_SCALE, 'experts_down': jax.random.normal(ks[3], (E, H, I), jnp.float32) * W_SCALE, 'shared_gate_w': jax.random.normal(ks[4], (SI, H), jnp.float32) * W_SCALE, 'shared_up_w': jax.random.normal(ks[5], (SI, H), jnp.float32) * W_SCALE, 'shared_down_w': jax.random.normal(ks[6], (H, SI), jnp.float32) * W_SCALE, 'shared_expert_gate_w': jax.random.normal(ks[7], (1, H), jnp.float32) * W_SCALE}
    _L1_ffn_in = _L1_ffn_setup()
    _d = {'L0_attn_hidden': _L0_attn_in['hidden'], 'L0_attn_norm1_w': _L0_attn_in['norm1_w'], 'L0_attn_norm2_w': _L0_attn_in['norm2_w'], 'L0_attn_g_wq': _L0_attn_in['g_wq'], 'L0_attn_g_kv_down': _L0_attn_in['g_kv_down'], 'L0_attn_g_k_up': _L0_attn_in['g_k_up'], 'L0_attn_g_v_up': _L0_attn_in['g_v_up'], 'L0_attn_g_wo': _L0_attn_in['g_wo'], 'L0_attn_l_wq': _L0_attn_in['l_wq'], 'L0_attn_l_wk': _L0_attn_in['l_wk'], 'L0_attn_l_wv': _L0_attn_in['l_wv'], 'L0_attn_l_wo': _L0_attn_in['l_wo'], 'L0_ffn_shared_up': _L0_ffn_in['shared_up'], 'L0_ffn_shared_down': _L0_ffn_in['shared_down'], 'L0_ffn_routed_up': _L0_ffn_in['routed_up'], 'L0_ffn_routed_down': _L0_ffn_in['routed_down'], 'L0_ffn_router_w': _L0_ffn_in['router_w'], 'L1_attn_Uq': _L1_attn_in['Uq'], 'L1_attn_Vq': _L1_attn_in['Vq'], 'L1_attn_bq': _L1_attn_in['bq'], 'L1_attn_Uk': _L1_attn_in['Uk'], 'L1_attn_Vk': _L1_attn_in['Vk'], 'L1_attn_bk': _L1_attn_in['bk'], 'L1_attn_Uv': _L1_attn_in['Uv'], 'L1_attn_Vv': _L1_attn_in['Vv'], 'L1_attn_bv': _L1_attn_in['bv'], 'L1_ffn_gate_w': _L1_ffn_in['gate_w'], 'L1_ffn_experts_gate_up': _L1_ffn_in['experts_gate_up'], 'L1_ffn_experts_down': _L1_ffn_in['experts_down'], 'L1_ffn_shared_gate_w': _L1_ffn_in['shared_gate_w'], 'L1_ffn_shared_up_w': _L1_ffn_in['shared_up_w'], 'L1_ffn_shared_down_w': _L1_ffn_in['shared_down_w'], 'L1_ffn_shared_expert_gate_w': _L1_ffn_in['shared_expert_gate_w']}
    _x0 = _d['L0_attn_hidden']
    _d['L0_attn_hidden'] = jax.random.normal(jax.random.fold_in(jax.random.key(seed), 1), (1, 2048, 128), dtype=_x0.dtype)
    del _x0
    return _d

def reference(L0_attn_hidden, L0_attn_norm1_w, L0_attn_norm2_w, L0_attn_g_wq, L0_attn_g_kv_down, L0_attn_g_k_up, L0_attn_g_v_up, L0_attn_g_wo, L0_attn_l_wq, L0_attn_l_wk, L0_attn_l_wv, L0_attn_l_wo, L0_ffn_shared_up, L0_ffn_shared_down, L0_ffn_routed_up, L0_ffn_routed_down, L0_ffn_router_w, L1_attn_Uq, L1_attn_Vq, L1_attn_bq, L1_attn_Uk, L1_attn_Vk, L1_attn_bk, L1_attn_Uv, L1_attn_Vv, L1_attn_bv, L1_ffn_gate_w, L1_ffn_experts_gate_up, L1_ffn_experts_down, L1_ffn_shared_gate_w, L1_ffn_shared_up_w, L1_ffn_shared_down_w, L1_ffn_shared_expert_gate_w):

    def _L0_attn_ref(hidden, norm1_w, norm2_w, g_wq, g_kv_down, g_k_up, g_v_up, g_wo, l_wq, l_wk, l_wv, l_wo):
        import jax, jax.numpy as jnp
        import numpy as np
        D = 128
        H = 16
        KVH = 4
        HD = D // H
        LAT = 32
        WIN = 32
        B, S = (1, 256)
        BASE_G, BASE_L = (1000000.0, 10000.0)
        EPS = 1e-06

        def rmsnorm(x, w):
            return x * jax.lax.rsqrt(jnp.mean(x * x, axis=-1, keepdims=True) + EPS) * w

        def qk_norm(x):
            return x * jax.lax.rsqrt(jnp.mean(x * x, axis=-1, keepdims=True) + EPS)

        def rope(x, base):
            s, hd = (x.shape[-2], x.shape[-1])
            inv_freq = 1.0 / base ** (jnp.arange(0, hd, 2, dtype=jnp.float32) / hd)
            freqs = jnp.arange(s, dtype=jnp.float32)[:, None] * inv_freq[None, :]
            cos, sin = (jnp.cos(freqs), jnp.sin(freqs))
            xe, xo = (x[..., ::2], x[..., 1::2])
            out = jnp.stack([xe * cos - xo * sin, xe * sin + xo * cos], axis=-1)
            return out.reshape(x.shape)

        def split_heads(x, n_heads):
            b, s, _ = x.shape
            return x.reshape(b, s, n_heads, HD).transpose(0, 2, 1, 3)

        def repeat_kv(x):
            return jnp.repeat(x, H // KVH, axis=1)

        def sdpa(q, k, v, mask):
            scores = jnp.einsum('bhqd,bhkd->bhqk', q, k) / np.sqrt(HD).astype(np.float32)
            scores = jnp.where(mask, scores, jnp.float32(-1e+30))
            probs = jax.nn.softmax(scores, axis=-1)
            return jnp.einsum('bhqk,bhkd->bhqd', probs, v)

        def merge_heads(x):
            b, h, s, hd = x.shape
            return x.transpose(0, 2, 1, 3).reshape(b, s, h * hd)

        def global_latent_attn(x, wq, w_kv_down, w_k_up, w_v_up, wo):
            q = split_heads(x @ wq, H)
            latent = x @ w_kv_down
            k = split_heads(latent @ w_k_up, KVH)
            v = split_heads(latent @ w_v_up, KVH)
            q, k = (rope(q, BASE_G), rope(k, BASE_G))
            q, k = (qk_norm(q), qk_norm(k))
            k, v = (repeat_kv(k), repeat_kv(v))
            i = jnp.arange(x.shape[1])
            causal = i[:, None] >= i[None, :]
            return merge_heads(sdpa(q, k, v, causal)) @ wo

        def local_gqa_attn(x, wq, wk, wv, wo):
            q = split_heads(x @ wq, H)
            k = split_heads(x @ wk, KVH)
            v = split_heads(x @ wv, KVH)
            q, k = (rope(q, BASE_L), rope(k, BASE_L))
            q, k = (qk_norm(q), qk_norm(k))
            k, v = (repeat_kv(k), repeat_kv(v))
            i = jnp.arange(x.shape[1])
            diff = i[:, None] - i[None, :]
            mask = (diff >= 0) & (diff < WIN)
            return merge_heads(sdpa(q, k, v, mask)) @ wo
        x = hidden
        x = x + global_latent_attn(rmsnorm(x, norm1_w), g_wq, g_kv_down, g_k_up, g_v_up, g_wo)
        x = x + local_gqa_attn(rmsnorm(x, norm2_w), l_wq, l_wk, l_wv, l_wo)
        return x

    def _L0_ffn_ref(x, shared_up, shared_down, routed_up, routed_down, router_w):
        import jax, jax.numpy as jnp
        import numpy as np
        H, F, E_SHARED, E_ROUTED, K = (128, 512, 1, 8, 2)

        def _expert(x, w_up, w_down):
            h = jax.nn.gelu(jnp.einsum('bsh,hf->bsf', x, w_up), approximate=False)
            return jnp.einsum('bsf,fh->bsh', h, w_down)
        shared_out = jnp.zeros_like(x)
        for i in range(E_SHARED):
            shared_out = shared_out + _expert(x, shared_up[i], shared_down[i])
        probs = jax.nn.softmax(jnp.einsum('bsh,he->bse', x, router_w), axis=-1)
        top_k_prob, top_k_idx = jax.lax.top_k(probs, K)
        onehot = jax.nn.one_hot(top_k_idx, E_ROUTED, dtype=x.dtype)
        gates = jnp.einsum('bsk,bske->bse', top_k_prob, onehot)
        routed_out = jnp.zeros_like(x)
        for e in range(E_ROUTED):
            y = _expert(x, routed_up[e], routed_down[e])
            routed_out = routed_out + gates[..., e:e + 1] * y
        return shared_out + routed_out + x

    def _L1_attn_ref(x, Uq, Vq, bq, Uk, Vk, bk, Uv, Vv, bv):
        import jax, jax.numpy as jnp
        import numpy as np
        B, S, D, H, R = (8, 128, 128, 8, 32)
        DH = D // H

        def _lowrank(xh, U, V, b):
            t = jnp.einsum('bshd,hrd->bshr', xh, V)
            return jnp.einsum('bshr,hdr->bshd', t, U) + b
        b_, s_, _ = x.shape
        xh = x.reshape(b_, s_, H, DH)
        q = _lowrank(xh, Uq, Vq, bq)
        k = _lowrank(xh, Uk, Vk, bk)
        v = _lowrank(xh, Uv, Vv, bv)
        scores = jnp.einsum('bqhd,bkhd->bhqk', q, k) / DH ** 0.5
        attn = jax.nn.softmax(scores, axis=-1)
        out = jnp.einsum('bhqk,bkhd->bqhd', attn, v)
        return out.reshape(b_, s_, D)

    def _L1_ffn_ref(x, gate_w, experts_gate_up, experts_down, shared_gate_w, shared_up_w, shared_down_w, shared_expert_gate_w):
        import jax, jax.numpy as jnp
        import numpy as np
        HIDDEN_SIZE = 128
        NUM_EXPERTS = 8
        MOE_INTERMEDIATE_SIZE = 176
        NUM_EXPERTS_PER_TOK = 2
        SHARED_EXPERT_INTERMEDIATE_SIZE = 352
        B, T = (2, 128)
        W_SCALE = 0.02
        Bx, Tx, H = x.shape
        E = gate_w.shape[0]
        I = experts_down.shape[2]
        x_flat = x.reshape(Bx * Tx, H)
        logits = x_flat @ gate_w.T
        scores = jax.nn.softmax(logits, axis=-1)
        _, topk_ids = jax.lax.top_k(scores, NUM_EXPERTS_PER_TOK)
        in_topk = jax.nn.one_hot(topk_ids, E, dtype=x.dtype).sum(axis=1)
        w = scores * in_topk
        gu = jnp.einsum('nh,eih->nei', x_flat, experts_gate_up)
        g, u = (gu[..., :I], gu[..., I:])
        h = jax.nn.silu(g) * u
        expert_out = jnp.einsum('nei,ehi->neh', h, experts_down)
        out = jnp.einsum('neh,ne->nh', expert_out, w)
        shared = jax.nn.silu(x_flat @ shared_gate_w.T) * (x_flat @ shared_up_w.T) @ shared_down_w.T
        shared_weight = jax.nn.sigmoid(x_flat @ shared_expert_gate_w.T)
        out = out + shared_weight * shared
        return out.reshape(Bx, Tx, H)
    x = L0_attn_hidden
    xn = _layernorm(x, axis=-1)
    s = _L0_attn_ref(xn, L0_attn_norm1_w, L0_attn_norm2_w, L0_attn_g_wq, L0_attn_g_kv_down, L0_attn_g_k_up, L0_attn_g_v_up, L0_attn_g_wo, L0_attn_l_wq, L0_attn_l_wk, L0_attn_l_wv, L0_attn_l_wo)
    g = _silu(_L0_ffn_ref(xn, L0_ffn_shared_up, L0_ffn_shared_down, L0_ffn_routed_up, L0_ffn_routed_down, L0_ffn_router_w))
    x = x + s * g
    xn = _layernorm(x, axis=-1)
    s = _L1_attn_ref(xn, L1_attn_Uq, L1_attn_Vq, L1_attn_bq, L1_attn_Uk, L1_attn_Vk, L1_attn_bk, L1_attn_Uv, L1_attn_Vv, L1_attn_bv)
    g = _silu(_L1_ffn_ref(xn, L1_ffn_gate_w, L1_ffn_experts_gate_up, L1_ffn_experts_down, L1_ffn_shared_gate_w, L1_ffn_shared_up_w, L1_ffn_shared_down_w, L1_ffn_shared_expert_gate_w))
    x = x + s * g
    return x

_drawn_inputs = setup_inputs


def setup_inputs(seed=0):
    import zlib

    import numpy as np

    out = dict(_drawn_inputs(seed))
    spreads = {'L0_attn_norm1_w': (1.0, 0.6), 'L0_attn_norm2_w': (1.0, 0.6)}
    factors = {'L0_attn_g_wq': 8.0,
     'L0_attn_g_kv_down': 8.0,
     'L0_attn_g_k_up': 8.0,
     'L0_attn_g_v_up': 8.0,
     'L0_attn_g_wo': 8.0,
     'L0_attn_l_wq': 8.0,
     'L0_attn_l_wk': 8.0,
     'L0_attn_l_wv': 8.0,
     'L0_attn_l_wo': 8.0,
     'L0_ffn_shared_up': 2.685,
     'L0_ffn_routed_up': 8.0,
     'L0_ffn_routed_down': 8.0,
     'L0_ffn_router_w': 8.0,
     'L1_attn_Uq': 8.0,
     'L1_attn_Vq': 8.0,
     'L1_attn_bq': 35.547,
     'L1_attn_Uk': 8.0,
     'L1_attn_Vk': 8.0,
     'L1_attn_Uv': 8.0,
     'L1_attn_Vv': 8.0,
     'L1_attn_bv': 8.0,
     'L1_ffn_gate_w': 8.0,
     'L1_ffn_experts_gate_up': 8.0,
     'L1_ffn_experts_down': 8.0,
     'L1_ffn_shared_gate_w': 8.0,
     'L1_ffn_shared_up_w': 8.0,
     'L1_ffn_shared_down_w': 8.0,
     'L1_ffn_shared_expert_gate_w': 8.0,
     'L1_attn_bk': 8.0}
    for name, (base, spread) in spreads.items():
        noise = np.random.default_rng([zlib.crc32(name.encode()), seed]).standard_normal(out[name].shape)
        drawn = base * np.exp(spread * noise) if base else spread * noise
        out[name] = jnp.asarray(drawn.astype(out[name].dtype))
    for name, factor in factors.items():
        out[name] = (out[name] * factor).astype(out[name].dtype)
    return out
```

```python
from contextlib import ExitStack

import concourse.bass as bass
from concourse import mybir

P = 128
T = 2048
GT = 512
TPG = GT // P
NG = T // GT
NT = T // P
HQ, HKV, HD = 16, 4, 8
HQK = HQ + HKV
H1, HD1 = 8, 16
WIN = 32
LW = P + WIN
NQK = HQK * HD
NQKV = NQK + HKV * HD
KS0 = 9 * HD
KS1 = 6 * HD1
KM1 = KS1 + 2
F0, FC0 = 512, 4
E0 = 8
I1, IC1 = 176, 88
E1 = 10
LN_EPS, RMS_EPS = 1e-5, 1e-6
PRODUCTS1 = ((0, 0), (0, 1), (0, 2), (1, 0), (1, 1), (2, 0))
VW = HD1 + 1


class Chain:

    def __init__(self, eng, sem, start=0):
        self.eng, self.sem, self.start, self.k = eng, sem, start, 0

    def __call__(self, ins):
        ins.then_inc(self.sem, 1)
        self.k += 1
        self.eng.wait_ge(self.sem, self.start + self.k)


def over_groups(eng, step):
    step(0)
    with eng.Fori(1, NG) as it:
        step(it)


def wait_past(eng, sem, n):
    if not (isinstance(n, int) and n == 0):
        eng.wait_ge(sem, n)


class PrepSems:

    def __init__(self, sem, prefix):
        self.cen = sem(prefix + "_cen")
        self.sq = sem(prefix + "_sq")
        self.var = sem(prefix + "_var")
        self.std = sem(prefix + "_std")
        self.xn = sem(prefix + "_xn")
        self.st = sem(prefix + "_st")
        self.xnT = sem(prefix + "_xnT")
        self.xnTc = sem(prefix + "_xnTc")
        self.lg = sem(prefix + "_lg")
        self.lgc = sem(prefix + "_lgc")
        self.sq2 = sem(prefix + "_sq2")
        self.var2 = sem(prefix + "_var2")
        self.std2 = sem(prefix + "_std2")
        self.y = sem(prefix + "_y")
        self.yT = sem(prefix + "_yT")
        self.yTc = sem(prefix + "_yTc")
        self.qkv = sem(prefix + "_qkv")
        self.qkvc = sem(prefix + "_qkvc")
        self.vc = sem(prefix + "_vc")
        self.ro = sem(prefix + "_ro")
        self.sq3 = sem(prefix + "_sq3")
        self.var3 = sem(prefix + "_var3")
        self.std3 = sem(prefix + "_std3")
        self.rn = sem(prefix + "_rn")
        self.h = sem(prefix + "_h")
        self.r1 = sem(prefix + "_r1")
        self.m = sem(prefix + "_m")
        self.l = sem(prefix + "_l")
        self.kp = sem(prefix + "_kp")
        self.pT = sem(prefix + "_pT")
        self.pTc = sem(prefix + "_pTc")
        self.scr = sem(prefix + "_scr")
        self.stk = sem(prefix + "_stk")
        self.dch = sem(prefix + "_dch")
        self.ost = sem(prefix + "_ost")
        self.oT = sem(prefix + "_oT")
        self.oTc = sem(prefix + "_oTc")
        self.op = sem(prefix + "_op")
        self.ores = sem(prefix + "_ores")


class AttSems:

    def __init__(self, sem, prefix):
        self.vst = sem(prefix + "_vst")
        self.score = sem(prefix + "_score")
        self.prob = sem(prefix + "_prob")
        self.mask = sem(prefix + "_mask")
        self.pv = sem(prefix + "_pv")
        self.oT = sem(prefix + "_oT")
        self.fin = sem(prefix + "_fin")
        self.och = sem(prefix + "_och")
        self.o = sem(prefix + "_o")


class MaxSems:

    def __init__(self, sem, prefix):
        self.mx = sem(prefix + "_mx")
        self.mxr = sem(prefix + "_mxr")
        self.mn = sem(prefix + "_mn")
        self.mnT = sem(prefix + "_mnT")
        self.mnTc = sem(prefix + "_mnTc")
        self.row = sem(prefix + "_row")


class MoeSems:

    def __init__(self, sem, prefix):
        self.up = sem(prefix + "_up")
        self.act = sem(prefix + "_act")
        self.hid = sem(prefix + "_hid")
        self.dn = sem(prefix + "_dn")
        self.acc = sem(prefix + "_acc")


class RouteSems:

    def __init__(self, sem, prefix):
        self.ch = sem(prefix + "_ch")
        self.ready = sem(prefix + "_ready")
        self.ex = sem(prefix + "_ex")


def build(nc, A):
    F32, BF = mybir.dt.float32, mybir.dt.bfloat16
    ALU, ACT, AX = mybir.AluOpType, mybir.ActivationFunctionType, mybir.AxisListType
    ds = bass.ds
    V, S_, PE_, G_ = nc.vector, nc.scalar, nc.tensor, nc.gpsimd
    ctx = ExitStack()
    with ctx:
        def sb(name, shape, dt=F32):
            return ctx.enter_context(nc.sbuf_tensor("sb_" + name, shape, dt))

        def sem(name):
            return ctx.enter_context(nc.semaphore(name))

        x_all = sb("x_all", [P, NT, P])
        xnT_all = sb("xnT_all", [P, T])
        s_all = sb("s_all", [P, NT, P])
        o_all = sb("o_all", [P, NT, P])
        acc = sb("acc", [P, NT, P])
        v_all = sb("v_all", [P, NT, 8, VW])
        stack = sb("stack", [P, HQK, T], BF)
        ring = sb("ring", [P, 4, 1024])
        gates = sb("gates", [P, NT, E1])
        ident = sb("ident", [P, P])
        identb = sb("identb", [P, P], BF)
        tri = sb("tri", [P, P])
        band = sb("band", [P, LW])
        cosT = sb("cosT", [P, 2, NT, HD])
        sinT = sb("sinT", [P, 2, NT, HD])
        normw = sb("normw", [P, 2])
        kvdT = sb("kvdT", [32, P])
        kvup = sb("kvup", [32, 2 * HKV * HD])
        wqkv = sb("wqkv", [P, 2, NQKV])
        wo = sb("wo", [P, 2, P])
        rw0 = sb("rw0", [P, E0])
        rw1 = sb("rw1", [P, E0 + 1])
        wl1 = sb("wl1", [P, 3 * P])
        bias1 = sb("bias1", [P, 3 * P])
        wup = sb("wup", [P, 2, F0])
        wdn = sb("wdn", [P, 2, FC0, P])
        vst = sb("vst", [P, 2, 4, 32])
        oT = sb("oT", [P, 2, GT])
        sq = sb("sq", [P, TPG, NQK])
        st4 = sb("st4", [P, 4, TPG])
        xn_st = sb("xn_st", [P, TPG, P])
        aT_st = sb("aT_st", [P, GT])
        yT_st = sb("yT_st", [P, GT])
        qkv_st = sb("qkv_st", [P, TPG, 3 * P])
        y_st = qkv_st[:, :, 2 * P:3 * P]
        rr = sb("rr", [P, 2 * TPG * NQK])
        ro = rr[:, 0:TPG * NQK].rearrange("p (t n) -> p t n", t=TPG)
        rt = rr[:, TPG * NQK:].rearrange("p (t n) -> p t n", t=TPG)
        cen = rr[:, TPG * NQK:TPG * NQK + GT].rearrange("p (t n) -> p t n", t=TPG)
        res1 = rr[:, 0:TPG * 2 * P].rearrange("p (t n) -> p t n", t=TPG)
        st80 = sb("st80", [P, 3, TPG * HQK])
        parts = sb("parts", [P, TPG, 6, P], BF)
        parts0 = parts[:, :, :, :].rearrange("p t a n -> p t (a n)")[:, :, 0:3 * NQK]\
            .rearrange("p t (a n) -> p t a n", a=3)
        parts1 = parts[:, :, :, :].rearrange("p t (a q) n -> p t a (q n)", q=2)
        kparts = sb("kparts", [P, TPG, 3 * 32], BF)
        pT = sb("pT", [P, 6, GT], BF)
        rden = sb("rden", [P, TPG, 4])
        lg = sb("lg", [P, NT, E0 + 1])
        rs = sb("rs", [P, 4, NT])
        top = sb("top", [P, NT, 8])
        pr = sb("pr", [P, NT, 8])
        mxp = sb("mxp", [P, 16, 4])
        mneg = sb("mneg", [P, 2, 16])
        mparts = sb("mparts", [P, 2, 16], BF)
        mT = sb("mT", [32, P], BF)
        zerob = sb("zerob", [P, GT], BF)

        ps = ctx.enter_context(nc.psum_tensor("ps", [P, 8, 512], F32))
        ps_bf = ps[:, :, :].rearrange("p b n -> p (b n)").bitcast(BF)
        scr = nc.dram_tensor("parts_dram", (3, NG, P, 6, GT), BF, kind="Internal").ap()

        q0s, k0s = stack[:, 0:HQ, :], stack[:, HQ:HQK, :]
        q1s, k1s = stack[:, 0:H1, :], stack[:, H1:2 * H1, :]
        lrV = ring[:, 0, 0:3 * 2 * P].rearrange("p (m c n) -> p m c n", m=3, c=2)
        lrU = ring[:, 1, 0:3 * 2 * P].rearrange("p (m c n) -> p m c n", m=3, c=2)

        s_const, s_x, s_identb = sem("s_const"), sem("s_x"), sem("s_identb")
        s_fold, s_foldc, s_vones = sem("s_fold"), sem("s_foldc"), sem("s_vones")
        SG = PrepSems(sem, "p")
        AG, AL, AB = AttSems(sem, "ag"), AttSems(sem, "al"), AttSems(sem, "ab")
        MX = MaxSems(sem, "mx")
        M0, M1 = MoeSems(sem, "m0"), MoeSems(sem, "m1")
        w0, w1 = [sem("w0_0"), sem("w0_1")], [sem("w1_0"), sem("w1_1")]
        s_stk1, s_zero = sem("s_stk1"), sem("s_zero")
        R0, R1 = RouteSems(sem, "r0"), RouteSems(sem, "r1")
        s_cleared, s_silu, s_prod, s_y, s_out = sem("s_cleared"), sem("s_silu"), sem("s_prod"), sem("s_y"), sem("s_out")

        block = ctx.enter_context(nc.Block())

        consts = [(ident[:, :], A.ident), (tri[:, :], A.tri),
                  (band[:, :], A.band), (cosT[:, :, :, :], A.cosT), (sinT[:, :, :, :], A.sinT),
                  (normw[:, :], A.normw), (kvdT[:, :], A.kvdT), (kvup[:, :], A.kvup),
                  (wqkv[:, 0, 0:P], A.g_wq), (wqkv[:, 1, :], A.l_wqkv), (wo[:, :, :], A.wo),
                  (rw0[:, :], A.router0), (rw1[:, :], A.router1), (lrV, A.lrV), (lrU, A.lrU),
                  (bias1[:, :], A.bias1)]
        ALL_CONST = 16 * len(consts)

        def grp(buf, it):
            return buf[:, ds(TPG * it, TPG), :]

        def cols(it):
            return ds(GT * it, GT)

        def dve_rstd(dve, link, src, stat, inv_n, eps, sq_done, var, std_done, n):
            dve.wait_ge(sq_done, n)
            link(V.tensor_reduce(stat[0], src, AX.X, ALU.add))
            V.tensor_scalar(stat[1], stat[0], inv_n, eps, ALU.mult, ALU.add).then_inc(var, 1)
            dve.wait_ge(std_done, n)
            link(V.reciprocal(stat[0], stat[2]))

        STAT4 = (st4[:, 0, :], st4[:, 1, :], st4[:, 2, :])
        SQ_LN = sq[:, :, 0:P]

        def over(stat, n):
            return stat.unsqueeze(2).broadcast_to([P, stat.shape[1], n])

        def dve_layernorm(dve, S, link, n, src, copies, keep=None):
            last = V.tensor_reduce(st4[:, 0, :], src, AX.X, ALU.add)
            if keep is not None:
                last = V.tensor_copy(keep, src)
            link(last)
            link(V.tensor_scalar(st4[:, 1, :], st4[:, 0, :], -1.0 / P, None, ALU.mult))
            V.tensor_tensor(cen, src, over(st4[:, 1, :], P), ALU.add).then_inc(S.cen, 1)
            dve_rstd(dve, link, SQ_LN, STAT4, 1.0 / P, LN_EPS, S.sq, S.var, S.std, n + 1)
            wait_past(dve, S.st, 2 * NG if copies else n)
            wait_past(dve, S.xnT, n)
            V.tensor_tensor(xn_st[:, :, :], cen, over(st4[:, 0, :], P), ALU.mult).then_inc(S.xn, 1)
            dve.wait_ge(S.xn, n + 1)

        def act_layernorm(act, S, n):
            act.wait_ge(S.cen, n + 1)
            S_.activation(SQ_LN, cen, ACT.Square).then_inc(S.sq, 1)
            act.wait_ge(S.var, n + 1)
            S_.activation(st4[:, 2, :], st4[:, 1, :], ACT.Sqrt).then_inc(S.std, 1)

        def dve_rms(dve, S, link, n, src):
            dve_rstd(dve, link, SQ_LN, STAT4, 1.0 / P, RMS_EPS, S.sq2, S.var2, S.std2, n + 1)
            V.tensor_tensor(y_st, src, over(st4[:, 0, :], P), ALU.mult).then_inc(S.y, 1)

        def act_rms(act, S, n, src, ready, at):
            act.wait_ge(ready, at)
            S_.activation(SQ_LN, src, ACT.Square).then_inc(S.sq2, 1)
            act.wait_ge(S.var2, n + 1)
            S_.activation(st4[:, 2, :], st4[:, 1, :], ACT.Sqrt).then_inc(S.std2, 1)

        def pe_transpose(src, bank, done):
            for t in range(TPG):
                last = PE_.transpose(ps[:, bank, t * P:(t + 1) * P], src[:, t, :], ident[:, :])
            last.then_inc(done, 1)

        def pe_qkv0(pe, S, n, layer):
            pe.wait_ge(S.y, n + 1)
            wait_past(pe, S.yTc, n)
            pe_transpose(y_st, 1, S.yT)
            pe.wait_ge(S.yTc, n + 1)
            for t in range(TPG):
                last = PE_.matmul(ps[:, 2 + t // 2, (t % 2) * NQKV:(t % 2 + 1) * NQKV],
                                  yT_st[:, t * P:(t + 1) * P], wqkv[:, layer, :], start=True, stop=True)
            last.then_inc(S.qkv, 1)

        def act_qkv0(act, S, n, it, layer):
            act.wait_ge(S.yT, n + 1)
            S_.activation(yT_st[:, :], ps[:, 1, :], ACT.Copy, scale=normw[:, layer:layer + 1]).then_inc(S.yTc, 1)
            act.wait_ge(S.qkv, n + 1)
            for b in range(2):
                S_.activation(qkv_st[:, 2 * b:2 * b + 2, 0:NQKV],
                              ps[:, 2 + b, 0:2 * NQKV].rearrange("p (t n) -> p t n", t=2),
                              ACT.Copy).then_inc(S.qkvc, 1)
            act.wait_ge(S.qkvc, 2 * n + 2)
            S_.activation(v_all[:, ds(TPG * it, TPG), 0:HKV, 0:HD],
                          qkv_st[:, :, NQK:NQKV].rearrange("p t (h d) -> p t h d", d=HD),
                          ACT.Copy).then_inc(S.vc, 1)

        def dve_rope_split(dve, S, link, n, it, layer):
            dve.wait_ge(S.qkvc, 2 * n + 2)
            full = [P, TPG, HQK, HD]
            half = [P, TPG, HQK, HD // 2]
            x = qkv_st[:, :, 0:NQK].rearrange("p t (h d) -> p t h d", d=HD)
            w = rt.rearrange("p t (h d) -> p t h d", d=HD)
            cs = cosT[:, layer, ds(TPG * it, TPG), :].unsqueeze(2)
            sn = sinT[:, layer, ds(TPG * it, TPG), :].unsqueeze(2)
            V.tensor_tensor(ro.rearrange("p t (h d) -> p t h d", d=HD), x, cs.broadcast_to(full),
                            ALU.mult).then_inc(S.dch, 1)
            V.tensor_tensor(w[:, :, :, 0:HD:2], x[:, :, :, 1:HD:2], sn[:, :, :, 0:HD:2].broadcast_to(half),
                            ALU.mult).then_inc(S.dch, 1)
            link.k += 2
            link(V.tensor_tensor(w[:, :, :, 1:HD:2], x[:, :, :, 0:HD:2],
                                 sn[:, :, :, 1:HD:2].broadcast_to(half), ALU.mult))
            V.tensor_tensor(ro, ro, rt, ALU.add).then_inc(S.ro, 1)
            stat = tuple(st80[:, i, :] for i in range(3))
            dve_rstd(dve, link, sq[:, :, :].rearrange("p t (h d) -> p (t h) d", d=HD), stat,
                     1.0 / HD, RMS_EPS, S.sq3, S.var3, S.std3, n + 1)
            V.tensor_tensor(rt.rearrange("p t (h d) -> p (t h) d", d=HD),
                            ro.rearrange("p t (h d) -> p (t h) d", d=HD),
                            over(st80[:, 0, :], HD), ALU.mult).then_inc(S.rn, 1)
            dve.wait_ge(S.rn, n + 1)
            dve.wait_ge(S.h, n + 1)
            V.tensor_tensor(ro, rt, parts0[:, :, 0, :], ALU.subtract).then_inc(S.r1, 1)
            dve.wait_ge(S.m, n + 1)
            dve.wait_ge(S.r1, n + 1)
            V.tensor_tensor(parts0[:, :, 2, :], ro, parts0[:, :, 1, :], ALU.subtract).then_inc(S.l, 1)
            dve.wait_ge(S.l, n + 1)
            V.tensor_copy(kparts[:, :, :].rearrange("p t (a n) -> p t a n", a=3),
                          parts0[:, :, :, HQ * HD:NQK]).then_inc(S.kp, 1)

        def act_rope_split(act, S, n):
            act.wait_ge(S.ro, n + 1)
            S_.activation(sq[:, :, :], ro, ACT.Square).then_inc(S.sq3, 1)
            act.wait_ge(S.var3, n + 1)
            S_.activation(st80[:, 2, :], st80[:, 1, :], ACT.Sqrt).then_inc(S.std3, 1)
            act.wait_ge(S.rn, n + 1)
            wait_past(act, S.pT, n)
            S_.activation(parts0[:, :, 0, :], rt, ACT.Copy).then_inc(S.h, 1)
            act.wait_ge(S.r1, n + 1)
            S_.activation(parts0[:, :, 1, :], ro, ACT.Copy).then_inc(S.m, 1)
            act.wait_ge(S.pT, n + 1)
            wait_past(act, S.scr, 32 * n)
            S_.activation(pT[:, 0:3, :].rearrange("p a n -> p (a n)"), ps_bf[:, 6 * 1024:6 * 1024 + 3 * GT],
                          ACT.Copy).then_inc(S.pTc, 1)
            S_.activation(pT[0:96, 3, :], ps_bf[0:96, 6 * 1024 + 3 * GT:8 * 1024], ACT.Copy).then_inc(S.pTc, 1)

        def pe_parts0(pe, S, n):
            pe.wait_ge(S.kp, n + 1)
            wait_past(pe, S.pTc, 2 * n)
            for a in range(3):
                for t in range(TPG):
                    at = 6 * 1024 + a * GT + t * P
                    PE_.transpose(ps_bf[:, at:at + P], parts0[:, t, a, 0:P], identb[:, :])
            for t in range(TPG):
                at = 6 * 1024 + 3 * GT + t * P
                last = PE_.transpose(ps_bf[0:96, at:at + P], kparts[:, t, :], identb[:, :])
            last.then_inc(S.pT, 1)

        def sp_stack0(sp, S, n, it, layer, used, total):
            if used is not None:
                sp.wait_ge(used, total)
            sp.wait_ge(S.pTc, 2 * n + 2)
            sp.dma_start(scr[layer, ds(it, 1), :, 0:3, :].rearrange("o p a t -> p (o a) t"), pT[:, 0:3, :]).then_inc(S.scr, 16)
            sp.dma_start(scr[layer, ds(it, 1), 0:96, 3:4, :].rearrange("o p a t -> p (o a) t"), pT[0:96, 3:4, :]).then_inc(S.scr, 16)
            sp.wait_ge(S.scr, 32 * n + 32)
            for a in range(3):
                for b in range(3):
                    r = (3 * a + b) * HD
                    sp.dma_start(q0s[r:r + HD, :, cols(it)],
                                 scr[layer, ds(it, 1), :, a, :].rearrange("o (h d) t -> d (o h) t", d=HD)).then_inc(S.stk, 16)
                    sp.dma_start(k0s[r:r + HD, :, cols(it)],
                                 scr[layer, ds(it, 1), 32 * b:32 * b + 32, 3, :].rearrange("o (h d) t -> d (o h) t", d=HD)).then_inc(S.stk, 16)

        STK0 = 18 * 16

        K_G = 4 + 2 + 5

        def sets0(g):
            return TPG * (g + 1)

        BASE_SET = [0]
        for g in range(NG):
            BASE_SET.append(BASE_SET[-1] + HKV * sets0(g))

        def att0_score(pe, A_, n, g, kv, kb, q0, first):
            w = GT - q0
            for u in range(2):
                if not first:
                    pe.wait_ge(A_.prob, 2 * n + u - 1)
                for j in range(2):
                    h = 4 * kv + 2 * u + j
                    last = PE_.matmul(ps[:, 2 * u + j, 0:w], k0s[0:KS0, kv, bass.ts(kb, P)],
                                      q0s[0:KS0, h, g * GT + q0:(g + 1) * GT], start=True, stop=True)
                last.then_inc(A_.score, 1)

        def att0_pv(pe, A_, n, par, bank, q0, masked, first, last_set):
            w = GT - q0
            pe.wait_ge(A_.vst, n + 1)
            if masked is not None:
                pe.wait_ge(A_.mask, masked)
            else:
                pe.wait_ge(A_.prob, 2 * n + 2)
            for h in range(4):
                last = PE_.matmul(ps[32 * h:32 * h + 32, bank, q0:GT], vst[:, par, 0, :],
                                  ring[:, 2 * par + h // 2, (h % 2) * w:(h % 2) * w + w],
                                  start=first, stop=last_set, skip_group_check=True)
            last.then_inc(A_.pv, 1)

        def plan0():
            for g in range(NG):
                for kv in range(HKV):
                    yield HKV * g + kv, g, kv, BASE_SET[g] + kv * sets0(g)

        def fin_transposes(pe, A_, c, bank):
            pe.wait_ge(A_.oT, c + 1)
            if c >= 1:
                pe.wait_ge(A_.o, c)
            for t in range(TPG):
                last = PE_.transpose(ps[:, bank, t * P:(t + 1) * P], oT[:, c % 2, t * P:(t + 1) * P], ident[:, :])
            last.then_inc(A_.fin, 1)

        def dve_out(dve, A_, c, bank, pv_done):
            dve.wait_ge(A_.pv, pv_done)
            if c >= 2:
                dve.wait_ge(A_.fin, c - 1)
            V.tensor_copy(oT[:, c % 2, :], ps[:, bank, :]).then_inc(A_.oT, 1)

        def dve_normalise(dve, A_, c, bank, g, col, hd):
            dve.wait_ge(A_.fin, c + 1)
            src = ps[:, bank, :].rearrange("p (t h d) -> p t h d", t=TPG, h=4)
            if c:
                dve.wait_ge(A_.o, c)
            V.reciprocal(rden[:, :, :], src[:, :, :, hd]).then_inc(A_.och, 1)
            dve.wait_ge(A_.och, c + 1)
            V.tensor_tensor(
                o_all[:, TPG * g:TPG * (g + 1), col:col + 4 * hd].rearrange("p t (h d) -> p t h d", h=4),
                src[:, :, :, 0:hd], rden[:, :, :].unsqueeze(3).broadcast_to([P, TPG, 4, hd]),
                ALU.mult).then_inc(A_.o, 1)

        N_SETS = BASE_SET[NG]
        N_UNITS = HKV * NG

        K_L = 2 + 5
        K_B = 2 + 4

        def act_oproj(act, S, n, it, done, last):
            act.wait_ge(done, last)
            wait_past(act, S.oT, n)
            S_.activation(xn_st[:, :, :], grp(o_all, it), ACT.Copy).then_inc(S.ost, 1)
            act.wait_ge(S.oT, n + 1)
            S_.activation(aT_st[:, :], ps[:, 0, :], ACT.Copy).then_inc(S.oTc, 1)

        def pe_oproj(pe, S, n, layer):
            pe.wait_ge(S.ost, n + 1)
            pe_transpose(xn_st, 0, S.oT)
            pe.wait_ge(S.oTc, n + 1)
            wait_past(pe, S.ores, n)
            for t in range(TPG):
                last = PE_.matmul(ps[:, 4, t * P:(t + 1) * P], aT_st[:, t * P:(t + 1) * P], wo[:, layer, :],
                                  start=True, stop=True)
            last.then_inc(S.op, 1)

        def dve_oproj(dve, S, n, it):
            dve.wait_ge(S.op, n + 1)
            V.tensor_tensor(cen, ps[:, 4, :].rearrange("p (t n) -> p t n", t=TPG), grp(s_all, it),
                            ALU.add).then_inc(S.ores, 1)

        def loc_score(pe, t, kv, w, first):
            n = 4 * t + kv
            if not first:
                pe.wait_ge(AL.prob, n - 1)
            for h in range(4):
                last = PE_.matmul(ps[:, 2 * (kv % 2) + h // 2, (h % 2) * w:(h % 2) * w + w],
                                  k0s[0:KS0, kv, ds(P * t, P)], q0s[0:KS0, 4 * kv + h, ds(P * t, w)],
                                  start=True, stop=True)
            last.then_inc(AL.score, 1)

        def loc_exp(act, t, kv, w, late):
            n = 4 * t + kv
            act.wait_ge(AL.score, n + 1)
            if late:
                act.wait_ge(AL.pv, n - 3)
            b = 2 * (kv % 2)
            S_.activation(ring[:, kv, 0:4 * w].rearrange("p (b q) -> p b q", b=2), ps[:, b:b + 2, 0:2 * w],
                          ACT.Exp, scale=float(HD) ** -0.5).then_inc(AL.prob, 1)

        def loc_mask(dve, t, kv, w):
            dve.wait_ge(AL.prob, 4 * t + kv + 1)
            d = ring[:, kv, 0:4 * w].rearrange("p (h q) -> p h q", h=4)
            V.tensor_tensor(d, d, band[:, 0:w].unsqueeze(1).broadcast_to([P, 4, w]), ALU.mult).then_inc(AL.mask, 1)

        def loc_pv(pe, t, par, kv, w, tile0):
            pe.wait_ge(AL.mask, 4 * t + kv + 1)
            if kv == 0:
                pe.wait_ge(AL.vst, t + 1)
            for h in range(4):
                last = PE_.matmul(ps[32 * h:32 * h + 32, 4 + par, kv * P:(kv + 1) * P], vst[:, par, kv, :],
                                  ring[:, kv, h * w:h * w + P], start=(tile0 and kv == 0), stop=True,
                                  skip_group_check=True)
            if w > P:
                if kv == 0 and not tile0:
                    pe.wait_ge(AL.oT, t)
                for h in range(4):
                    last = PE_.matmul(ps[32 * h:32 * h + 32, 5 - par, kv * P:kv * P + WIN], vst[:, par, kv, :],
                                      ring[:, kv, h * w + P:h * w + w], start=(kv == 0), stop=True,
                                      skip_group_check=True)
            last.then_inc(AL.pv, 1)

        def loc_fin(pe, t, par):
            pe.wait_ge(AL.oT, t + 1)
            wait_past(pe, AL.o, t)
            for kv in range(HKV):
                last = PE_.transpose(ps[:, 6, kv * P:(kv + 1) * P], oT[:, par, kv * P:(kv + 1) * P], ident[:, :])
            last.then_inc(AL.fin, 1)

        def loc_out(act, t, par):
            act.wait_ge(AL.pv, 4 * t + 4)
            if not (isinstance(t, int) and t == 0):
                act.wait_ge(AL.fin, t - 1)
            S_.activation(oT[:, par, :], ps[:, 4 + par, :], ACT.Copy).then_inc(AL.oT, 1)

        def loc_normalise(dve, t):
            dve.wait_ge(AL.fin, t + 1)
            src = ps[:, 6, :].rearrange("p (h d) -> p h d", d=32)
            r = rden[:, :, :].rearrange("p a b -> p (a b)")
            wait_past(dve, AL.o, t)
            V.reciprocal(r, src[:, :, HD]).then_inc(AL.och, 1)
            dve.wait_ge(AL.och, t + 1)
            V.tensor_tensor(o_all[:, ds(t, 1), :].rearrange("p o (h d) -> p (o h) d", d=HD), src[:, :, 0:HD],
                            over(r, HD), ALU.mult).then_inc(AL.o, 1)

        def loc_loop(eng, step):
            step(0, 0, True, False)
            step(1, 1, False, False)
            with eng.Fori(1, NT // 2 - 1) as i:
                step(2 * i, 0, False, False)
                step(2 * i + 1, 1, False, False)
            step(NT - 2, 0, False, False)
            step(NT - 1, 1, False, True)

        def route_dve(dve, R, sig):
            link = Chain(dve, R.ch)
            x = lg[:, :, 0:E0]
            link(V.tensor_reduce(rs[:, 0, :], x, AX.X, ALU.max))
            link(V.tensor_tensor(x, x, over(rs[:, 0, :], E0), ALU.subtract))
            V.nop().then_inc(R.ready, 1)
            dve.wait_ge(R.ex, 1)
            link(V.tensor_reduce(rs[:, 1, :], x, AX.X, ALU.add))
            link(V.reciprocal(rs[:, 2, :], rs[:, 1, :]))
            link(V.tensor_tensor(x, x, over(rs[:, 2, :], E0), ALU.mult))
            for t in range(NT):
                V.max(top[:, t, :], lg[:, t, 0:E0]).then_inc(R.ch, 1)
            link.k += NT
            dve.wait_ge(R.ch, link.k)
            link(V.memset(top[:, :, 2:8], -1.0))
            for t in range(NT):
                V.match_replace(pr[:, t, :], top[:, t, :], lg[:, t, 0:E0], 0.0).then_inc(R.ch, 1)
            link.k += NT
            dve.wait_ge(R.ch, link.k)
            link(V.tensor_tensor(gates[:, :, 0:E0], x, pr[:, :, :], ALU.subtract))
            if sig:
                link(V.tensor_scalar(rs[:, 3, :], lg[:, :, E0], 1.0, None, ALU.add))
                link(V.reciprocal(gates[:, :, E0], rs[:, 3, :]))
                link(V.tensor_copy(gates[:, :, E0 + 1], gates[:, :, E0]))
            V.nop().then_inc(R.ready, 1)

        def route_act(act, R, sig):
            act.wait_ge(R.ready, 1)
            last = S_.activation(lg[:, :, 0:E0], lg[:, :, 0:E0], ACT.Exp)
            if sig:
                last = S_.activation(lg[:, :, E0], lg[:, :, E0], ACT.Exp, scale=-1.0)
            last.then_inc(R.ex, 1)

        def moe_down(pe, M, n, par, k, chunks, lhs, slot, first):
            pe.wait_ge(M.hid, 2 * n + 2)
            if not first:
                pe.wait_ge(M.acc, n - 1)
            for t in range(TPG):
                for c in range(chunks):
                    last = PE_.matmul(ps[:, 4 + par, t * P:(t + 1) * P], lhs(c, t),
                                      wdn[0:k, slot, c, :], start=(c == 0), stop=(c == chunks - 1),
                                      skip_group_check=True)
            last.then_inc(M.dn, 1)

        def moe_add(dve, M, n, par, g, gate, late):
            dve.wait_ge(M.dn, n + 1)
            if late:
                dve.wait_ge(M.acc, n)
            for t in range(TPG):
                a = acc[:, TPG * g + t, :]
                y = ps[:, 4 + par, t * P:(t + 1) * P]
                if gate is None:
                    last = V.tensor_tensor(a, y, a, ALU.add)
                else:
                    last = V.scalar_tensor_tensor(out=a, in0=y, scalar=gate(TPG * g + t), in1=a,
                                                  op0=ALU.mult, op1=ALU.add)
            last.then_inc(M.acc, 1)

        def hid0(par, c, lo, n):
            return ring[:, 2 * par + c // 2, (c % 2) * GT + lo:(c % 2) * GT + lo + n]

        def up0(pe, n, g, slot, first):
            for c in range(FC0):
                if c % 2 == 0 and not first:
                    pe.wait_ge(M0.hid, 2 * n - 1 + c // 2)
                last = PE_.matmul(ps[:, c, :], wup[:, slot, c * P:(c + 1) * P], xnT_all[:, g * GT:(g + 1) * GT],
                                  start=True, stop=True)
                if c % 2:
                    last.then_inc(M0.up, 1)

        def gelu0(act, n, par, late):
            for u in range(2):
                act.wait_ge(M0.up, 2 * n + u + 1)
                if u == 0 and late:
                    act.wait_ge(M0.dn, n - 1)
                S_.activation(ring[:, 2 * par + u, :], ps[:, 2 * u:2 * u + 2, :].rearrange("p b n -> p (b n)"),
                              ACT.Gelu).then_inc(M0.hid, 1)

        def down0(pe, n, par, slot, first):
            moe_down(pe, M0, n, par, P, FC0, lambda c, t: hid0(par, c, t * P, P), slot, first)

        def up1(pe, n, g, slot, first):
            for c in range(4):
                if not first and c == 0:
                    pe.wait_ge(M1.act, n)
                if not first and c == 2:
                    pe.wait_ge(M1.hid, 2 * n)
                last = PE_.matmul(ps[0:IC1, c, :], wup[:, slot, c * IC1:(c + 1) * IC1],
                                  xnT_all[:, g * GT:(g + 1) * GT], start=True, stop=True)
                if c % 2:
                    last.then_inc(M1.up, 1)

        def silu1(act, n, par, late):
            act.wait_ge(M1.up, 2 * n + 1)
            if late:
                act.wait_ge(M1.hid, 2 * n - 2)
            S_.activation(ring[0:IC1, 2 * par, :], ps[0:IC1, 0:2, :].rearrange("p b n -> p (b n)"),
                          ACT.Silu).then_inc(M1.act, 1)

        def mult1(dve, n, par, late):
            dve.wait_ge(M1.act, n + 1)
            dve.wait_ge(M1.up, 2 * n + 2)
            if late:
                dve.wait_ge(M1.dn, n - 1)
            V.tensor_tensor(ring[0:IC1, 2 * par + 1, :], ring[0:IC1, 2 * par, :],
                            ps[0:IC1, 2:4, :].rearrange("p b n -> p (b n)"), ALU.mult).then_inc(M1.hid, 2)

        def down1(pe, n, par, slot, first):
            moe_down(pe, M1, n, par, IC1, 2,
                     lambda c, t: ring[0:IC1, 2 * par + 1, c * GT + t * P:c * GT + (t + 1) * P], slot, first)

        NU1 = 2 * NG
        NKB = NT
        ROW = 8 * 16

        def where1(u):
            return 4 * (u // NG), GT * (u % NG)

        def max_item(pe, u, s, j, e, first):
            h0, q0 = where1(u)
            h = h0 + 2 * s + e
            m0 = 64 * u + 32 * s + 8 * j + 4 * e
            for kc in range(NG):
                if not (first and kc < 2):
                    pe.wait_ge(MX.mxr, m0 + kc - 1)
                PE_.matmul(ps[:, 6 + kc % 2, :], q1s[0:KS1, h, ds(q0 + P * j, P)],
                           k1s[0:KS1, h, kc * GT:(kc + 1) * GT], start=True, stop=True).then_inc(MX.mx, 1)

        def max_reduce(dve, u, s, j, e):
            m0 = 64 * u + 32 * s + 8 * j + 4 * e
            for kc in range(NG):
                dve.wait_ge(MX.mx, m0 + kc + 1)
                V.tensor_reduce(mxp[:, ds(4 * (2 * s + e) + j, 1), kc:kc + 1],
                                ps[:, 6 + kc % 2, :].unsqueeze(1), AX.X, ALU.max).then_inc(MX.mxr, 1)

        def max_tail_dve(dve, u):
            dve.wait_ge(MX.mxr, 64 * u + 64)
            if u:
                dve.wait_ge(MX.mnT, u)
            V.tensor_reduce(mneg[:, 0, :], mxp[:, :, :], AX.X, ALU.max).then_inc(MX.mn, 1)
            dve.wait_ge(MX.mn, 4 * u + 1)
            V.tensor_scalar(mneg[:, 1, :], mneg[:, 0, :], -1.0, None, ALU.mult).then_inc(MX.mn, 1)
            dve.wait_ge(MX.mn, 4 * u + 2)
            V.tensor_copy(mparts[:, 0, :], mneg[:, 1, :]).then_inc(MX.mn, 1)
            dve.wait_ge(MX.mn, 4 * u + 3)
            V.tensor_tensor(mparts[:, 1, :], mneg[:, 1, :], mparts[:, 0, :], ALU.subtract).then_inc(MX.mn, 1)

        def max_tail_pe(pe, u, bank):
            pe.wait_ge(MX.mn, 4 * u + 4)
            PE_.transpose(ps_bf[0:32, bank * 1024:bank * 1024 + P], mparts[:, :, :].rearrange("p a m -> p (a m)"),
                          identb[:, :]).then_inc(MX.mnT, 1)

        def max_tail_act(act, u, bank):
            act.wait_ge(MX.mnT, u + 1)
            if u:
                act.wait_ge(MX.row, ROW * u)
            S_.activation(mT[:, :], ps_bf[0:32, bank * 1024:bank * 1024 + P], ACT.Copy).then_inc(MX.mnTc, 1)

        def max_tail_sp(sp, u):
            h0, q0 = where1(u)
            sp.wait_ge(MX.mnTc, u + 1)
            for a in range(2):
                for h in range(4):
                    sp.dma_start(q1s[KS1 + a:KS1 + a + 1, h0 + h, q0:q0 + GT],
                                 mT[16 * a + 4 * h:16 * a + 4 * h + 4, :]).then_inc(MX.row, 16)

        def att1_score(pe, n, u, kb, first):
            h0, q0 = where1(u)
            for w in range(2):
                if not first:
                    pe.wait_ge(AB.prob, 2 * n + w - 1)
                for j in range(2):
                    h = 2 * w + j
                    last = PE_.matmul(ps[:, h, :], k1s[0:KM1, h0 + h, ds(P * kb, P)],
                                      q1s[0:KM1, h0 + h, q0:q0 + GT], start=True, stop=True)
                last.then_inc(AB.score, 1)

        def att1_exp(act, n, par, late):
            for w in range(2):
                act.wait_ge(AB.score, 2 * n + w + 1)
                if late:
                    act.wait_ge(AB.pv, n - 1)
                S_.activation(ring[:, 2 * par + w, :], ps[:, 2 * w:2 * w + 2, :].rearrange("p b n -> p (b n)"),
                              ACT.Exp, scale=float(HD1) ** -0.5).then_inc(AB.prob, 1)

        def att1_pv(pe, n, par, bank):
            pe.wait_ge(AB.vst, n + 1)
            pe.wait_ge(AB.prob, 2 * n + 2)
            for h in range(4):
                last = PE_.matmul(ps[32 * h:32 * h + 32, bank, :], vst[:, par, h, :],
                                  ring[:, 2 * par + h // 2, (h % 2) * GT:(h % 2 + 1) * GT],
                                  start=False, stop=True, skip_group_check=True)
            last.then_inc(AB.pv, 1)

        def att1_clear(pe, bank):
            for h in range(4):
                PE_.matmul(ps[32 * h:32 * h + 32, bank, :], zerob[:, 0:32], zerob[:, :], start=True, stop=False,
                           skip_group_check=True)

        B1 = (1, 2, 3, 5)

        def act_layer1(act, S, it):
            n = NG + it
            act_oproj(act, S, n, it, AL.o, NT)
            act_layernorm(act, S, n)
            act.wait_ge(S.xnT, n + 1)
            S_.activation(aT_st[:, :], ps[:, 0, :], ACT.Copy).then_inc(S.xnTc, 1)
            act.wait_ge(S.xnTc, 2 * n + 1)
            S_.activation(xnT_all[:, cols(it)], aT_st[:, :], ACT.Copy).then_inc(S.xnTc, 1)
            act.wait_ge(S.lg, n + 1)
            S_.activation(lg[:, ds(TPG * it, TPG), :],
                          ps[:, 4, 0:TPG * (E0 + 1)].rearrange("p (t e) -> p t e", t=TPG), ACT.Copy).then_inc(S.lgc, 1)
            act.wait_ge(S.qkvc, 2 * (n + NG) + 2)
            S_.activation(v_all[:, ds(TPG * it, TPG), :, 0:HD1],
                          qkv_st[:, :, 2 * P:3 * P].rearrange("p t (h d) -> p t h d", d=HD1),
                          ACT.Copy).then_inc(S.vc, 1)
            act.wait_ge(S.pT, n + NG)
            S_.activation(parts1[:, :, 0, :], qkv_st[:, :, 0:2 * P], ACT.Copy).then_inc(S.h, 1)
            act.wait_ge(S.r1, n + NG + 1)
            S_.activation(parts1[:, :, 1, :], res1, ACT.Copy).then_inc(S.m, 1)
            act.wait_ge(S.pT, n + NG + 1)
            act.wait_ge(S.scr, 32 * (n + NG))
            for half, bank in ((0, 6), (1, 0)):
                S_.activation(pT[:, 3 * half:3 * half + 3, :].rearrange("p a n -> p (a n)"),
                              ps_bf[:, bank * 1024:bank * 1024 + 3 * GT], ACT.Copy).then_inc(S.pTc, 1)

        def pe_layer1(pe, S, it):
            n = NG + it
            pe.wait_ge(S.pTc, 2 * (n + NG))
            pe_oproj(pe, S, n, 1)
            pe.wait_ge(S.xn, n + 1)
            pe_transpose(xn_st, 0, S.xnT)
            pe.wait_ge(S.xnTc, 2 * n + 1)
            for t in range(TPG):
                last = PE_.matmul(ps[:, B1[t], 0:3 * P], aT_st[:, t * P:(t + 1) * P], wl1[:, :],
                                  start=True, stop=True)
            last.then_inc(S.qkv, 1)
            pe.wait_ge(S.ores, n + 1)
            for t in range(TPG):
                last = PE_.matmul(ps[:, 4, t * (E0 + 1):(t + 1) * (E0 + 1)], aT_st[:, t * P:(t + 1) * P],
                                  rw1[:, :], start=True, stop=True)
            last.then_inc(S.lg, 1)
            pe.wait_ge(S.l, n + NG + 1)
            pe.wait_ge(S.xnTc, 2 * n + 2)
            for half, bank in ((0, 6), (1, 0)):
                for a in range(3):
                    for t in range(TPG):
                        at = bank * 1024 + a * GT + t * P
                        last = PE_.transpose(ps_bf[:, at:at + P], parts1[:, t, a, half * P:(half + 1) * P],
                                             identb[:, :])
            last.then_inc(S.pT, 1)
            pe.wait_ge(S.lgc, n + 1)

        def dve_layer1(dve, S, link, it):
            n = NG + it
            dve_oproj(dve, S, n, it)
            dve.wait_ge(S.ores, n + 1)
            link(V.tensor_tensor(cen, cen, grp(acc, it), ALU.mult))
            link(V.tensor_tensor(cen, grp(x_all, it), cen, ALU.add))
            dve_layernorm(dve, S, link, n, cen, NG, keep=grp(x_all, it))
            dve.wait_ge(S.qkv, n + NG + 1)
            dve.wait_ge(S.h, n + NG)
            dve.wait_ge(S.vc, n + NG)
            for t in range(TPG):
                last = V.tensor_tensor(qkv_st[:, t, :], ps[:, B1[t], 0:3 * P], bias1[:, :], ALU.add)
            last.then_inc(S.qkvc, 2)
            dve.wait_ge(S.h, n + NG + 1)
            dve.wait_ge(S.qkvc, 2 * (n + NG) + 2)
            V.tensor_tensor(res1, qkv_st[:, :, 0:2 * P], parts1[:, :, 0, :], ALU.subtract).then_inc(S.r1, 1)
            dve.wait_ge(S.m, n + NG + 1)
            dve.wait_ge(S.r1, n + NG + 1)
            V.tensor_tensor(parts1[:, :, 2, :], res1, parts1[:, :, 1, :], ALU.subtract).then_inc(S.l, 1)
            dve.wait_ge(S.l, n + NG + 1)

        def sp_tail(sp):
            with sp.Fori(0, NG) as it:
                sp_stack0(sp, SG, NG + it, it, 1, AG.pv, N_SETS)

            def load(w, slot, up_src, dn_src, k, c, n_up):
                sp.dma_start(wup[:, slot, 0:n_up], up_src.rearrange("o d f -> (o d) f")).then_inc(w[slot], 16)
                sp.dma_start(wdn[0:k, slot, 0:c, :], dn_src.rearrange("o f c d -> (o f) c d")).then_inc(w[slot], 16)

            def load0(x, slot):
                load(w0, slot, A.up0[ds(x, 1)], A.dn0[ds(x, 1)], P, FC0, F0)
            load0(0, 1)
            load0(1, 0)
            sp.wait_ge(M0.dn, 4)
            load0(2, 1)
            with sp.Fori(1, E0 // 2) as i:
                sp.wait_ge(M0.dn, 8 * i)
                load0(1 + 2 * i, 0)
                sp.wait_ge(M0.dn, 8 * i + 4)
                load0(2 + 2 * i, 1)
            with sp.Fori(0, NG) as it:
                n = 2 * NG + it
                sp.wait_ge(AL.o, NT)
                sp.wait_ge(SG.pTc, 2 * n + 2)
                for half in range(2):
                    sp.dma_start(scr[2, ds(it, 1), :, 3 * half:3 * half + 3, :].rearrange("o p a t -> p (o a) t"),
                                 pT[:, 3 * half:3 * half + 3, :]).then_inc(SG.scr, 16)
                sp.wait_ge(SG.scr, 32 * n + 32)
                for r, (a, b) in enumerate(PRODUCTS1):
                    for dst, part in ((q1s, a), (k1s, 3 + b)):
                        sp.dma_start(dst[r * HD1:(r + 1) * HD1, :, cols(it)],
                                     scr[2, ds(it, 1), :, part, :].rearrange("o (h d) t -> d (o h) t", d=HD1))\
                            .then_inc(s_stk1, 16)
            for u in range(NU1):
                max_tail_sp(sp, u)

            def load1(x, slot):
                load(w1, slot, A.up1[ds(x, 1)], A.dn1[ds(x, 1)], IC1, 2, 4 * IC1)
            sp.wait_ge(M0.dn, 4 * (E0 + 1))
            load1(0, 0)
            load1(1, 1)
            with sp.Fori(1, E1 // 2) as i:
                for e in range(2):
                    sp.wait_ge(M1.dn, 8 * i + 4 * e - 4)
                    load1(2 * i + e, e)
            with sp.Fori(0, NG) as it:
                sp.wait_ge(s_y, it + 1)
                sp.dma_start(A.out[cols(it), :].rearrange("(t p) d -> p t d", p=P), grp(x_all, it)).then_inc(s_out, 16)
            sp.wait_ge(s_out, 16 * NG)

        def pool_tail(pool):
            G_.memset(zerob[:, :], 0.0).then_inc(s_zero, 1)
            pool.wait_ge(SG.vc, 2 * NG)
            pool.wait_ge(AG.pv, N_SETS)
            pool.wait_ge(s_zero, 1)

            def stage(t, par, first, last):
                if not first:
                    pool.wait_ge(AL.pv, 4 * t - 4)
                G_.tensor_copy(vst[:, par, :, 0:HD + 1],
                               v_all[:, ds(t, 1), 0:HKV, 0:HD + 1].rearrange("p o h d -> p (o h) d")).then_inc(AL.vst, 1)
            loc_loop(pool, stage)
            pool.wait_ge(AL.pv, 4 * NT)
            G_.memset(k1s[KS1:KM1, :, :], 1.0).then_inc(s_zero, 1)
            pool.wait_ge(s_zero, 2)
            pool.wait_ge(SG.vc, 3 * NG)
            for u in range(NU1):
                h0, _ = where1(u)

                def stage1(n, e, kb, late):
                    if late:
                        pool.wait_ge(AB.pv, n - 1)
                    G_.tensor_copy(vst[:, e, :, 0:VW],
                                   v_all[:, ds(kb, 1), h0:h0 + 4, :].rearrange("p o h d -> p (o h) d")).then_inc(AB.vst, 1)
                if u == 0:
                    stage1(0, 0, 0, False)
                    stage1(1, 1, 1, False)
                with pool.Fori(1 if u == 0 else 0, NKB // 2) as j:
                    for e in range(2):
                        stage1(NKB * u + 2 * j + e, e, 2 * j + e, True)

        def act_tail(act):
            def prepare(it):
                act_oproj(act, SG, it, it, AG.o, N_UNITS)
                act_rms(act, SG, NG + it, cen, SG.ores, it + 1)
                S_.activation(grp(s_all, it), cen, ACT.Copy).then_inc(SG.st, 1)
                act_qkv0(act, SG, NG + it, it, 1)
                act_rope_split(act, SG, NG + it)
            over_groups(act, prepare)

            def tile(t, par, first, last):
                w = P if last else LW
                for kv in range(HKV):
                    loc_exp(act, t, kv, w, not first)
                    if kv == 0 and not first:
                        loc_out(act, t - 1, 1 - par)
            loc_loop(act, tile)
            loc_out(act, NT - 1, 1)
            route_act(act, R0, False)
            for g in range(NG):
                gelu0(act, g, g % 2, g >= 2)
            with act.Fori(0, E0 // 2) as i:
                for e in range(2):
                    for g in range(NG):
                        gelu0(act, 4 + 8 * i + 4 * e + g, g % 2, True)
            act.wait_ge(M0.acc, 4 * (E0 + 1))
            S_.activation(acc[:, :, :], acc[:, :, :], ACT.Silu).then_inc(s_silu, 1)
            with act.Fori(0, NG) as it:
                act_layer1(act, SG, it)
            route_act(act, R1, True)
            max_tail_act(act, 0, 4)
            for u in range(NU1):
                n0 = NKB * u

                def pair(j, late):
                    for e in range(2):
                        att1_exp(act, n0 + 2 * j + e, e, late)
                pair(0, u > 0)
                with act.Fori(1, 4) as j:
                    pair(j, True)
                pair(4, True)
                if u + 1 < NU1:
                    max_tail_act(act, u + 1, 4 + (u + 1) % 2)
                with act.Fori(5, 8) as j:
                    pair(j, True)
            silu1(act, 0, 0, False)
            silu1(act, 1, 1, False)
            silu1(act, 2, 0, True)
            silu1(act, 3, 1, True)
            for g in range(NG):
                silu1(act, 4 + g, g % 2, True)
            with act.Fori(1, E1 // 2) as i:
                for e in range(2):
                    for g in range(NG):
                        silu1(act, 8 * i + 4 * e + g, g % 2, True)
            act.wait_ge(M1.acc, 4 * E1)
            with act.Fori(0, NG) as it:
                S_.activation(grp(acc, it), grp(acc, it), ACT.Silu).then_inc(s_silu, 1)

        def pe_moe(units, up, down):
            for k, (n, g, slot, first) in enumerate(units):
                up(n, g, slot, first)
                if k:
                    down(*units[k - 1])
            down(*units[-1])

        def pe_tail(pe):
            def prepare(it):
                pe_oproj(pe, SG, it, 0)
                pe_qkv0(pe, SG, NG + it, 1)
                pe_parts0(pe, SG, NG + it)
            over_groups(pe, prepare)
            pe.wait_ge(SG.stk, 2 * NG * STK0)
            pe.wait_ge(SG.pTc, 4 * NG)
            pe.wait_ge(AG.o, N_UNITS)
            loc_score(pe, 0, 0, LW, True)

            def tile(t, par, first, last):
                w = P if last else LW
                for kv in range(HKV):
                    if kv + 1 < HKV:
                        loc_score(pe, t, kv + 1, w, first and kv == 0)
                    elif not last:
                        loc_score(pe, t + 1, 0, P if isinstance(t, int) and t == NT - 2 else LW, False)
                    loc_pv(pe, t, par, kv, w, first)
                    if kv == 1 and not first:
                        loc_fin(pe, t - 1, 1 - par)
            loc_loop(pe, tile)
            loc_fin(pe, NT - 1, 1)

            pe.wait_ge(AL.oT, NT)
            def up(n, g, slot, first):
                up0(pe, n, g, slot, first)

            def down(n, g, slot, first):
                down0(pe, n, g % 2, slot, first or (isinstance(n, int) and n < 2))
            pe.wait_ge(w0[1], 32)
            pe_moe([(g, g, 1, g == 0) for g in range(NG)], up, down)
            with pe.Fori(0, E0 // 2) as i:
                pe.wait_ge(w0[0], 32 * i + 32)
                units = [(4 + 8 * i + g, g, 0, False) for g in range(NG)]
                more = [(8 + 8 * i + g, g, 1, False) for g in range(NG)]

                def up_(n, g, slot, first):
                    if slot and g == 0:
                        pe.wait_ge(w0[1], 32 * i + 64)
                    up0(pe, n, g, slot, first)
                pe_moe(units + more, up_, down)

            with pe.Fori(0, NG) as it:
                pe_layer1(pe, SG, it)

            pe.wait_ge(s_stk1, 2 * len(PRODUCTS1) * 16 * NG)
            pe.wait_ge(SG.pTc, 6 * NG)
            pe.wait_ge(s_zero, 2)

            def maxima(u, s, lo, hi, first=False):
                if first:
                    for e in range(2):
                        max_item(pe, u, s, 0, e, e == 0)
                    lo += 1
                with pe.Fori(lo, hi) as j:
                    for e in range(2):
                        max_item(pe, u, s, j, e, False)
            maxima(0, 0, 0, 4, True)
            maxima(0, 1, 0, 4)
            max_tail_pe(pe, 0, 4)
            maxima(1, 0, 0, 4)
            pe.wait_ge(MX.row, ROW)
            att1_score(pe, 0, 0, 0, True)
            for u in range(NU1):
                n0, bank, other = NKB * u, 4 + u % 2, 4 + (u + 1) % 2

                def pair(j, half, last=False):
                    for e in range(2):
                        n = n0 + 2 * j + e
                        if last and e:
                            if u + 1 < NU1:
                                pe.wait_ge(MX.row, ROW * (u + 2))
                                att1_score(pe, n + 1, u + 1, 0, False)
                        else:
                            att1_score(pe, n + 1, u, 2 * j + e + 1, False)
                        if half == 0 and u + 1 < NU1:
                            max_item(pe, u + 1, 1, j, e, False)
                        if half == 1 and u + 2 < NU1:
                            max_item(pe, u + 2, 0, j - 4, e, False)
                        att1_pv(pe, n, e, bank)
                pe.wait_ge(MX.mnTc, u + 1)
                if u >= 2:
                    pe.wait_ge(AB.o, u - 1)
                att1_clear(pe, bank)
                with pe.Fori(0, 4) as j:
                    pair(j, 0)
                if u:
                    fin_transposes(pe, AB, u - 1, other)
                pair(4, 1)
                if u + 1 < NU1:
                    if u:
                        pe.wait_ge(AB.o, u)
                    max_tail_pe(pe, u + 1, other)
                with pe.Fori(5, 7) as j:
                    pair(j, 1)
                pair(7, 1, last=True)
            fin_transposes(pe, AB, NU1 - 1, 4 + (NU1 - 1) % 2)

            pe.wait_ge(AB.prob, 2 * NKB * NU1)
            pe.wait_ge(AB.o, NU1)

            def up1_(n, g, slot, first):
                up1(pe, n, g, slot, first)

            def down1_(n, g, slot, first):
                down1(pe, n, g % 2, slot, first or (isinstance(n, int) and n < 2))

            def pair1(i, first):
                pe.wait_ge(w1[0], 32 * i + 32)
                pe.wait_ge(w1[1], 32 * i + 32)
                pe_moe([(8 * i + 4 * e + g, g, e, first and e + g == 0) for e in range(2) for g in range(NG)],
                       up1_, down1_)
            pair1(0, True)
            with pe.Fori(1, E1 // 2) as i:
                pair1(i, False)

        def dve_tail(dve):
            def prepare(it):
                link = Chain(dve, SG.dch, NG * K_G + it * K_L)
                dve_oproj(dve, SG, it, it)
                dve_rms(dve, SG, link, NG + it, cen)
                dve_rope_split(dve, SG, link, NG + it, it, 1)
                assert link.k == K_L, link.k
            over_groups(dve, prepare)

            def tile(t, par, first, last):
                w = P if last else LW
                for kv in range(HKV):
                    loc_mask(dve, t, kv, w)
                    if kv == 1 and not first:
                        loc_normalise(dve, t - 1)
            loc_loop(dve, tile)
            loc_normalise(dve, NT - 1)
            route_dve(dve, R0, False)
            for g in range(NG):
                moe_add(dve, M0, g, g % 2, g, None, g > 0)
            with dve.Fori(0, E0 // 2) as i:
                for e in range(2):
                    for g in range(NG):
                        moe_add(dve, M0, 4 + 8 * i + 4 * e + g, g % 2, g,
                                lambda t: gates[:, t, ds(2 * i + e, 1)], True)
            dve.wait_ge(s_silu, 1)
            with dve.Fori(0, NG) as it:
                link = Chain(dve, SG.dch, NG * (K_G + K_L) + it * K_B)
                dve_layer1(dve, SG, link, it)
                assert link.k == K_B, link.k
            V.memset(acc[:, :, :], 0.0).then_inc(s_cleared, 1)
            route_dve(dve, R1, True)

            def maxima(u, s, lo=0):
                with dve.Fori(lo, 4) as j:
                    for e in range(2):
                        max_reduce(dve, u, s, j, e)
            maxima(0, 0)
            maxima(0, 1)
            max_tail_dve(dve, 0)
            maxima(1, 0)
            for u in range(NU1):
                if u:
                    dve_out(dve, AB, u - 1, 4 + (u - 1) % 2, NKB * u)
                if u + 1 < NU1:
                    maxima(u + 1, 1)
                    max_tail_dve(dve, u + 1)
                if u:
                    dve_normalise(dve, AB, u - 1, 4 + (u - 1) % 2, (u - 1) % NG, 64 * ((u - 1) // NG), HD1)
                if u + 2 < NU1:
                    maxima(u + 2, 0)
            dve_out(dve, AB, NU1 - 1, 4 + (NU1 - 1) % 2, NKB * NU1)
            dve_normalise(dve, AB, NU1 - 1, 4 + (NU1 - 1) % 2, NG - 1, 64, HD1)

            def gate1(x):
                return lambda t: gates[:, t, ds(x, 1)]
            dve.wait_ge(s_cleared, 1)

            def pair1(i, first):
                units = [(8 * i + 4 * e + g, g, e) for e in range(2) for g in range(NG)]
                for k, (n, g, e) in enumerate(units):
                    mult1(dve, n, g % 2, not (first and k < 2))
                    if k:
                        m, mg, me = units[k - 1]
                        moe_add(dve, M1, m, mg % 2, mg, gate1(2 * i + me), not (first and k == 1))
                m, mg, me = units[-1]
                moe_add(dve, M1, m, mg % 2, mg, gate1(2 * i + me), True)
            pair1(0, True)
            with dve.Fori(1, E1 // 2) as i:
                pair1(i, False)
            with dve.Fori(0, NG) as it:
                dve.wait_ge(s_silu, it + 2)
                V.tensor_tensor(cen, grp(o_all, it), grp(acc, it), ALU.mult).then_inc(s_prod, 1)
                dve.wait_ge(s_prod, it + 1)
                V.tensor_tensor(grp(x_all, it), grp(x_all, it), cen, ALU.add).then_inc(s_y, 1)
                dve.wait_ge(s_y, it + 1)

        @block.sync
        def _(sp):
            for g in range(NG):
                sp.dma_start(x_all[:, TPG * g:TPG * (g + 1), :],
                             A.x[GT * g:GT * (g + 1), :].rearrange("(t p) d -> p t d", p=P)).then_inc(s_x, 16)
            for dst, src in consts:
                sp.dma_start(dst, src).then_inc(s_const, 16)
            over_groups(sp, lambda it: sp_stack0(sp, SG, it, it, 0, None, None))
            sp_tail(sp)

        @block.gpsimd
        def _(pool):
            G_.memset(v_all[:, :, :, :], 1.0).then_inc(s_vones, 1)
            G_.memset(vst[:, :, :, :], 0.0).then_inc(s_vones, 1)
            pool.wait_ge(s_vones, 2)
            pool.wait_ge(SG.vc, NG)
            def stage_v(n, par, kb, kv, late):
                if late:
                    pool.wait_ge(AG.pv, n - 1)
                G_.tensor_copy(vst[:, par, 0:1, 0:HD + 1],
                               v_all[:, ds(kb, 1), kv, 0:HD + 1]).then_inc(AG.vst, 1)
            for c, g, kv, n0 in plan0():
                for i in range(4):
                    stage_v(n0 + i, i % 2, TPG * g + i, kv, n0 + i >= 2)
                if g:
                    with pool.Fori(0, 2 * g) as j:
                        for e in range(2):
                            stage_v(n0 + 4 + 2 * j + e, e, 2 * j + e, kv, True)
            pool_tail(pool)

        @block.scalar
        def _(act):
            act.wait_ge(s_const, ALL_CONST)
            S_.activation(identb[:, :], ident[:, :], ACT.Copy).then_inc(s_identb, 1)
            act.wait_ge(s_fold, 1)
            S_.activation(wqkv[:, 0, P:NQKV], ps[:, 5, 0:2 * HKV * HD], ACT.Copy).then_inc(s_foldc, 1)
            act.wait_ge(s_fold, 2)
            S_.activation(wl1[:, :], ps[:, 4, 0:3 * P], ACT.Copy).then_inc(s_foldc, 1)
            act.wait_ge(s_vones, 2)
            def prepare(it):
                act_layernorm(act, SG, it)
                act_rms(act, SG, it, xn_st[:, :, :], SG.xn, it + 1)
                S_.activation(grp(s_all, it), xn_st[:, :, :], ACT.Copy)
                act.wait_ge(SG.xnT, it + 1)
                S_.activation(aT_st[:, :], ps[:, 0, :], ACT.Copy).then_inc(SG.xnTc, 1)
                act.wait_ge(SG.xnTc, 2 * it + 1)
                S_.activation(xnT_all[:, cols(it)], aT_st[:, :], ACT.Copy).then_inc(SG.xnTc, 1)
                S_.activation(grp(acc, it), xn_st[:, :, :], ACT.Copy).then_inc(SG.st, 1)
                act_qkv0(act, SG, it, it, 0)
                act_rope_split(act, SG, it)
                act.wait_ge(SG.lg, it + 1)
                S_.activation(lg[:, ds(TPG * it, TPG), 0:E0],
                              ps[:, 4, 0:TPG * E0].rearrange("p (t e) -> p t e", t=TPG), ACT.Copy).then_inc(SG.lgc, 1)
            over_groups(act, prepare)

            def exps(n, u, par, w, late):
                act.wait_ge(AG.score, 2 * n + u + 1)
                if late:
                    act.wait_ge(AG.pv, n - 1)
                S_.activation(ring[:, 2 * par + u, 0:2 * w].rearrange("p (h q) -> p h q", h=2),
                              ps[:, 2 * u:2 * u + 2, 0:w], ACT.Exp, scale=float(HD) ** -0.5).then_inc(AG.prob, 1)
            for c, g, kv, n0 in plan0():
                for i in range(4):
                    for u in range(2):
                        exps(n0 + i, u, i % 2, GT - P * i, n0 + i >= 2)
                if g:
                    with act.Fori(0, 2 * g) as j:
                        for e in range(2):
                            for u in range(2):
                                exps(n0 + 4 + 2 * j + e, u, e, GT, True)
            act_tail(act)

        @block.tensor
        def _(pe):
            pe.wait_ge(s_const, ALL_CONST)
            PE_.matmul(ps[:, 5, 0:2 * HKV * HD], kvdT[:, :], kvup[:, :], start=True, stop=True).then_inc(s_fold, 1)
            for m in range(3):
                for c in range(2):
                    last = PE_.matmul(ps[:, 4, m * P:(m + 1) * P], lrV[:, m, c, :], lrU[:, m, c, :],
                                      start=(c == 0), stop=(c == 1))
            last.then_inc(s_fold, 1)
            pe.wait_ge(s_foldc, 2)
            pe.wait_ge(s_identb, 1)
            def prepare(it):
                pe.wait_ge(SG.xn, it + 1)
                wait_past(pe, SG.xnTc, 2 * it)
                pe_transpose(xn_st, 0, SG.xnT)
                pe_qkv0(pe, SG, it, 0)
                pe.wait_ge(SG.xnTc, 2 * it + 2)
                wait_past(pe, SG.lgc, it)
                for t in range(TPG):
                    last = PE_.matmul(ps[:, 4, t * E0:(t + 1) * E0], aT_st[:, t * P:(t + 1) * P], rw0[:, :],
                                      start=True, stop=True)
                last.then_inc(SG.lg, 1)
                pe_parts0(pe, SG, it)
            over_groups(pe, prepare)

            pe.wait_ge(SG.stk, NG * STK0)
            pe.wait_ge(SG.pTc, 2 * NG)
            pe.wait_ge(SG.lgc, NG)
            units = list(plan0())
            att0_score(pe, AG, 0, 0, 0, 0, 0, True)
            for c, g, kv, n0 in units:
                bank = 4 + c % 2
                NSET = sets0(g)
                nxt = units[c + 1] if c + 1 < len(units) else None

                def first_of_next():
                    if nxt:
                        att0_score(pe, AG, nxt[3], nxt[1], nxt[2], TPG * nxt[1], 0, False)
                for i in range(4):
                    if i < 3:
                        att0_score(pe, AG, n0 + i + 1, g, kv, TPG * g + i + 1, P * (i + 1), n0 + i + 1 < 1)
                    elif g:
                        att0_score(pe, AG, n0 + 4, g, kv, 0, 0, False)
                    else:
                        first_of_next()
                    if i == 0 and c >= 2:
                        pe.wait_ge(AG.oT, c - 1)
                    att0_pv(pe, AG, n0 + i, i % 2, bank, P * i, 8 * c + 2 * i + 2, i == 0, False)
                    if i == 1 and c:
                        fin_transposes(pe, AG, c - 1, 6)
                if g:
                    if g > 0:
                        with pe.Fori(0, 2 * g - 1) as j:
                            for e in range(2):
                                att0_score(pe, AG, n0 + 4 + 2 * j + e + 1, g, kv, 2 * j + e + 1, 0, False)
                                att0_pv(pe, AG, n0 + 4 + 2 * j + e, e, bank, 0, None, False, False)
                    m = 4 * g - 2
                    att0_score(pe, AG, n0 + 4 + m + 1, g, kv, m + 1, 0, False)
                    att0_pv(pe, AG, n0 + 4 + m, 0, bank, 0, None, False, False)
                    first_of_next()
                    att0_pv(pe, AG, n0 + 4 + m + 1, 1, bank, 0, None, False, True)
            fin_transposes(pe, AG, N_UNITS - 1, 6)
            pe_tail(pe)

        @block.vector
        def _(dve):
            dve.wait_ge(s_x, 16 * NG)
            def prepare(it):
                link = Chain(dve, SG.dch, it * K_G)
                dve_layernorm(dve, SG, link, it, grp(x_all, it), 0)
                dve_rms(dve, SG, link, it, xn_st[:, :, :])
                dve_rope_split(dve, SG, link, it, it, 0)
                assert link.k == K_G, link.k
            over_groups(dve, prepare)
            for c, g, kv, n0 in plan0():
                if c:
                    dve_out(dve, AG, c - 1, 4 + (c - 1) % 2, n0)
                for i in range(4):
                    w = GT - P * i
                    for u in range(2):
                        dve.wait_ge(AG.prob, 2 * (n0 + i) + u + 1)
                        d = ring[:, 2 * (i % 2) + u, 0:2 * w].rearrange("p (h q) -> p h q", h=2)[:, :, 0:P]
                        V.tensor_tensor(d, d, tri[:, :].unsqueeze(1).broadcast_to([P, 2, P]),
                                        ALU.mult).then_inc(AG.mask, 1)
                    if i == 1 and c:
                        dve_normalise(dve, AG, c - 1, 6, (c - 1) // HKV, ((c - 1) % HKV) * 32, HD)
            dve_out(dve, AG, N_UNITS - 1, 4 + (N_UNITS - 1) % 2, N_SETS)
            dve_normalise(dve, AG, N_UNITS - 1, 6, NG - 1, 96, HD)
            dve_tail(dve)


def _arrays(i):
    import numpy as np

    f = {k: np.ascontiguousarray(np.asarray(v)) for k, v in i.items()}
    tok = np.arange(T, dtype=np.float32)
    cos, sin = np.empty((P, 2, NT, HD), np.float32), np.empty((P, 2, NT, HD), np.float32)
    for n, base in enumerate((1000000.0, 10000.0)):
        inv = (1.0 / np.float32(base) ** (np.arange(0, HD, 2, dtype=np.float32) / np.float32(HD))).astype(np.float32)
        fr = (tok[:, None] * inv[None, :]).reshape(NT, P, HD // 2).transpose(1, 0, 2)
        cos[:, n, :, 0::2] = cos[:, n, :, 1::2] = np.cos(fr)
        sin[:, n, :, 0::2], sin[:, n, :, 1::2] = -np.sin(fr), np.sin(fr)
    k, q = np.arange(P)[:, None], np.arange(LW)[None, :]

    def blocks(w):
        h, a, b = w.shape
        out = np.zeros((h * a, h * b), w.dtype)
        for n in range(h):
            out[n * a:(n + 1) * a, n * b:(n + 1) * b] = w[n]
        return out.reshape(2, P, h * b).transpose(1, 0, 2)

    L = "L1_attn_"
    gu = f["L1_ffn_experts_gate_up"]
    sg, su, sd = f["L1_ffn_shared_gate_w"], f["L1_ffn_shared_up_w"], f["L1_ffn_shared_down_w"]
    g1 = np.concatenate([gu[:, :I1], sg.reshape(2, I1, P)])
    u1 = np.concatenate([gu[:, I1:], su.reshape(2, I1, P)])
    up1 = np.concatenate([g1, u1], axis=1).transpose(0, 2, 1)
    dn1 = np.concatenate([f["L1_ffn_experts_down"], sd.reshape(P, 2, I1).transpose(1, 0, 2)])
    dn1 = dn1.transpose(0, 2, 1).reshape(E1, 2, IC1, P).transpose(0, 2, 1, 3)
    dn0 = np.concatenate([f["L0_ffn_shared_down"], f["L0_ffn_routed_down"]])
    a = dict(
        x=f["L0_attn_hidden"][0],
        ident=np.eye(P, dtype=np.float32),
        tri=(q[:, :P] >= k).astype(np.float32), band=((q >= k) & (q - k < WIN)).astype(np.float32),
        cosT=cos, sinT=sin,
        normw=np.stack([f["L0_attn_norm1_w"], f["L0_attn_norm2_w"]], axis=1),
        kvdT=f["L0_attn_g_kv_down"].T, kvup=np.concatenate([f["L0_attn_g_k_up"], f["L0_attn_g_v_up"]], axis=1),
        g_wq=f["L0_attn_g_wq"],
        l_wqkv=np.concatenate([f["L0_attn_l_wq"], f["L0_attn_l_wk"], f["L0_attn_l_wv"]], axis=1),
        wo=np.stack([f["L0_attn_g_wo"], f["L0_attn_l_wo"]], axis=1),
        router0=f["L0_ffn_router_w"],
        router1=np.concatenate([f["L1_ffn_gate_w"], f["L1_ffn_shared_expert_gate_w"]]).T,
        lrV=np.stack([blocks(f[L + "V" + m]) for m in "qkv"], axis=1),
        lrU=np.stack([blocks(f[L + "U" + m].transpose(0, 2, 1)) for m in "qkv"], axis=1),
        bias1=np.broadcast_to(np.concatenate([f[L + "b" + m].reshape(-1) for m in "qkv"]), (P, 3 * P)),
        up0=np.concatenate([f["L0_ffn_shared_up"], f["L0_ffn_routed_up"]]),
        dn0=dn0.reshape(E0 + 1, FC0, P, P).transpose(0, 2, 1, 3),
        up1=up1, dn1=dn1,
    )
    return {k: np.ascontiguousarray(v) for k, v in a.items()}


class Arrays:

    def __init__(self, a):
        self.band, self.bias1, self.cosT, self.dn0, self.dn1, self.g_wq = (a[x] for x in ("band", "bias1", "cosT", "dn0", "dn1", "g_wq"))
        self.ident, self.kvdT, self.kvup, self.l_wqkv, self.lrU, self.lrV = (a[x] for x in ("ident", "kvdT", "kvup", "l_wqkv", "lrU", "lrV"))
        self.normw, self.router0, self.router1, self.sinT, self.tri, self.up0 = (a[x] for x in ("normw", "router0", "router1", "sinT", "tri", "up0"))
        self.up1, self.wo, self.x = (a[x] for x in ("up1", "wo", "x"))


def kernel(**inputs):
    import concourse.bacc as bacc
    from concourse.bass_utils import run_bass_kernel_spmd

    arrays = {f"in_{k}": v for k, v in _arrays(inputs).items()}
    nc = bacc.Bacc("TRN2", target_bir_lowering=False, num_devices=1)
    A = Arrays({name[3:]: nc.dram_tensor(name, a.shape, mybir.dt.from_np(a.dtype), kind="ExternalInput").ap()
                for name, a in arrays.items()})
    A.out = nc.dram_tensor("out_x", (T, P), mybir.dt.float32, kind="ExternalOutput").ap()
    build(nc, A)
    r = run_bass_kernel_spmd(nc, [arrays], core_ids=[0])
    return r.results[0]["out_x"].reshape(1, T, P)
```

```python
from contextlib import ExitStack

import concourse.bass as bass
from concourse import mybir

P = 128
T = 2048
GT = 512
TPG = GT // P
NG = T // GT
NT = T // P
HQ, HKV, HD = 16, 4, 8
HQK = HQ + HKV
H1, HD1 = 8, 16
WIN = 32
LW = P + WIN
NQK = HQK * HD
NQKV = NQK + HKV * HD
KS0 = 9 * HD
KS1 = 6 * HD1
KM1 = KS1 + 2
F0, FC0 = 512, 4
E0 = 8
I1, IC1 = 176, 88
E1 = 10
LN_EPS, RMS_EPS = 1e-5, 1e-6
PRODUCTS1 = ((0, 0), (0, 1), (0, 2), (1, 0), (1, 1), (2, 0))
VW = HD1 + 1


class Chain:

    def __init__(self, eng, sem, start=0):
        self.eng, self.sem, self.start, self.k = eng, sem, start, 0

    def __call__(self, ins):
        ins.then_inc(self.sem, 1)
        self.k += 1
        self.eng.wait_ge(self.sem, self.start + self.k)


def over_groups(eng, step):
    step(0)
    with eng.Fori(1, NG) as it:
        step(it)


def over_rounds(eng, step, peeled):
    step(0, None)
    for r in range(1, peeled):
        step(r, r - 1)
    with eng.Fori(peeled, NG) as r:
        step(r, r - 1)
    step(None, NG - 1)


def wait_past(eng, sem, n):
    if not (isinstance(n, int) and n == 0):
        eng.wait_ge(sem, n)


class PrepSems:

    def __init__(self, sem, prefix):
        self.cen = sem(prefix + "_cen")
        self.sq = sem(prefix + "_sq")
        self.var = sem(prefix + "_var")
        self.std = sem(prefix + "_std")
        self.xn = sem(prefix + "_xn")
        self.st = sem(prefix + "_st")
        self.xnT = sem(prefix + "_xnT")
        self.xnTc = sem(prefix + "_xnTc")
        self.lg = sem(prefix + "_lg")
        self.lgc = sem(prefix + "_lgc")
        self.sq2 = sem(prefix + "_sq2")
        self.var2 = sem(prefix + "_var2")
        self.std2 = sem(prefix + "_std2")
        self.y = sem(prefix + "_y")
        self.yT = sem(prefix + "_yT")
        self.yTc = sem(prefix + "_yTc")
        self.qkv = sem(prefix + "_qkv")
        self.qkvc = sem(prefix + "_qkvc")
        self.vc = sem(prefix + "_vc")
        self.ro = sem(prefix + "_ro")
        self.sq3 = sem(prefix + "_sq3")
        self.var3 = sem(prefix + "_var3")
        self.std3 = sem(prefix + "_std3")
        self.rn = sem(prefix + "_rn")
        self.h = sem(prefix + "_h")
        self.r1 = sem(prefix + "_r1")
        self.m = sem(prefix + "_m")
        self.l = sem(prefix + "_l")
        self.kp = sem(prefix + "_kp")
        self.pT = sem(prefix + "_pT")
        self.pTc = sem(prefix + "_pTc")
        self.scr = sem(prefix + "_scr")
        self.stk = sem(prefix + "_stk")
        self.dch = sem(prefix + "_dch")
        self.ost = sem(prefix + "_ost")
        self.oT = sem(prefix + "_oT")
        self.oTc = sem(prefix + "_oTc")
        self.op = sem(prefix + "_op")
        self.ores = sem(prefix + "_ores")


class AttSems:

    def __init__(self, sem, prefix):
        self.vst = sem(prefix + "_vst")
        self.score = sem(prefix + "_score")
        self.prob = sem(prefix + "_prob")
        self.mask = sem(prefix + "_mask")
        self.pv = sem(prefix + "_pv")
        self.oT = sem(prefix + "_oT")
        self.fin = sem(prefix + "_fin")
        self.och = sem(prefix + "_och")
        self.o = sem(prefix + "_o")


class MaxSems:

    def __init__(self, sem, prefix):
        self.mx = sem(prefix + "_mx")
        self.mxr = sem(prefix + "_mxr")
        self.mn = sem(prefix + "_mn")
        self.mnT = sem(prefix + "_mnT")
        self.mnTc = sem(prefix + "_mnTc")
        self.row = sem(prefix + "_row")


class MoeSems:

    def __init__(self, sem, prefix):
        self.up = sem(prefix + "_up")
        self.act = sem(prefix + "_act")
        self.hid = sem(prefix + "_hid")
        self.dn = sem(prefix + "_dn")
        self.acc = sem(prefix + "_acc")


class RouteSems:

    def __init__(self, sem, prefix):
        self.ch = sem(prefix + "_ch")
        self.ready = sem(prefix + "_ready")
        self.ex = sem(prefix + "_ex")


def build(nc, A):
    F32, BF = mybir.dt.float32, mybir.dt.bfloat16
    ALU, ACT, AX = mybir.AluOpType, mybir.ActivationFunctionType, mybir.AxisListType
    ds = bass.ds
    V, S_, PE_, G_ = nc.vector, nc.scalar, nc.tensor, nc.gpsimd
    ctx = ExitStack()
    with ctx:
        def sb(name, shape, dt=F32):
            return ctx.enter_context(nc.sbuf_tensor("sb_" + name, shape, dt))

        def sem(name):
            return ctx.enter_context(nc.semaphore(name))

        x_all = sb("x_all", [P, NT, P])
        xnT_all = sb("xnT_all", [P, T])
        s_all = sb("s_all", [P, NT, P])
        o_all = sb("o_all", [P, NT, P])
        acc = sb("acc", [P, NT, P])
        v_all = sb("v_all", [P, NT, 8, VW])
        stack = sb("stack", [P, HQK, T], BF)
        ring = sb("ring", [P, 4, 1024])
        gates = sb("gates", [P, NT, E1])
        ident = sb("ident", [P, P])
        identb = sb("identb", [P, P], BF)
        tri = sb("tri", [P, P])
        band = sb("band", [P, LW])
        cosT = sb("cosT", [P, 2, NT, HD])
        sinT = sb("sinT", [P, 2, NT, HD])
        normw = sb("normw", [P, 2])
        kvdT = sb("kvdT", [32, P])
        kvup = sb("kvup", [32, 2 * HKV * HD])
        wqkv = sb("wqkv", [P, 2, NQKV])
        wo = sb("wo", [P, 2, P])
        rw0 = sb("rw0", [P, E0])
        rw1 = sb("rw1", [P, E0 + 1])
        wl1 = sb("wl1", [P, 3 * P])
        bias1 = sb("bias1", [P, 3 * P])
        wup = sb("wup", [P, 2, F0])
        wdn = sb("wdn", [P, 2, FC0, P])
        vst = sb("vst", [P, 2, 4, 32])
        oT = sb("oT", [P, 2, GT])
        sq = sb("sq", [P, TPG, NQK])
        st4 = sb("st4", [P, 4, TPG])
        xn_st = sb("xn_st", [P, TPG, P])
        aT_st = sb("aT_st", [P, GT])
        yT_st = sb("yT_st", [P, GT])
        qkv_st = sb("qkv_st", [P, TPG, 3 * P])
        y_st = qkv_st[:, :, 2 * P:3 * P]
        rr = sb("rr", [P, 2 * TPG * NQK])
        ro = rr[:, 0:TPG * NQK].rearrange("p (t n) -> p t n", t=TPG)
        rt = rr[:, TPG * NQK:].rearrange("p (t n) -> p t n", t=TPG)
        cen = ring[:, 2, 0:GT].rearrange("p (t n) -> p t n", t=TPG)
        sq_ln = ring[:, 2, GT:2 * GT].rearrange("p (t n) -> p t n", t=TPG)
        res1 = rr[:, 0:TPG * 2 * P].rearrange("p (t n) -> p t n", t=TPG)
        st80 = sb("st80", [P, 3, TPG * HQK])
        parts = sb("parts", [P, TPG, 6, P], BF)
        parts0 = parts[:, :, :, :].rearrange("p t a n -> p t (a n)")[:, :, 0:3 * NQK]\
            .rearrange("p t (a n) -> p t a n", a=3)
        parts1 = parts[:, :, :, :].rearrange("p t (a q) n -> p t a (q n)", q=2)
        kparts = sb("kparts", [P, TPG, 3 * 32], BF)
        pT = sb("pT", [P, 6, GT], BF)
        rden = sb("rden", [P, TPG, 4])
        lg = sb("lg", [P, NT, E0 + 1])
        rs = sb("rs", [P, 4, NT])
        top = sb("top", [P, NT, 8])
        pr = sb("pr", [P, NT, 8])
        mxp = sb("mxp", [P, 2, 16, 4])
        mneg = sb("mneg", [P, 2, 16])
        mparts = sb("mparts", [P, 2, 16], BF)
        mT = sb("mT", [32, P], BF)
        zerob = sb("zerob", [P, GT], BF)

        ps = ctx.enter_context(nc.psum_tensor("ps", [P, 8, 512], F32))
        ps_bf = ps[:, :, :].rearrange("p b n -> p (b n)").bitcast(BF)
        scr = nc.dram_tensor("parts_dram", (3, NG, P, 6, GT), BF, kind="Internal").ap()

        q0s, k0s = stack[:, 0:HQ, :], stack[:, HQ:HQK, :]
        q1s, k1s = stack[:, 0:H1, :], stack[:, H1:2 * H1, :]
        lrV = ring[:, 0, 0:3 * 2 * P].rearrange("p (m c n) -> p m c n", m=3, c=2)
        lrU = ring[:, 1, 0:3 * 2 * P].rearrange("p (m c n) -> p m c n", m=3, c=2)

        s_const, s_x, s_identb = sem("s_const"), sem("s_x"), sem("s_identb")
        s_fold, s_foldc, s_vones = sem("s_fold"), sem("s_foldc"), sem("s_vones")
        AG, AL, AB = AttSems(sem, "ag"), AttSems(sem, "al"), AttSems(sem, "ab")
        MX = MaxSems(sem, "mx")
        M0, M1 = MoeSems(sem, "m0"), MoeSems(sem, "m1")
        w0, w1 = [sem("w0_0"), sem("w0_1")], [sem("w1_0"), sem("w1_1")]
        s_stk1, s_zero = sem("s_stk1"), sem("s_zero")
        R0, R1 = RouteSems(sem, "r0"), RouteSems(sem, "r1")
        s_cleared, s_silu, s_prod, s_y, s_out = sem("s_cleared"), sem("s_silu"), sem("s_prod"), sem("s_y"), sem("s_out")

        block = ctx.enter_context(nc.Block())

        consts = [(ident[:, :], A.ident), (tri[:, :], A.tri),
                  (band[:, :], A.band), (cosT[:, :, :, :], A.cosT), (sinT[:, :, :, :], A.sinT),
                  (normw[:, :], A.normw), (kvdT[:, :], A.kvdT), (kvup[:, :], A.kvup),
                  (wqkv[:, 0, 0:P], A.g_wq), (wqkv[:, 1, :], A.l_wqkv), (wo[:, :, :], A.wo),
                  (rw0[:, :], A.router0), (rw1[:, :], A.router1), (lrV, A.lrV), (lrU, A.lrU),
                  (bias1[:, :], A.bias1)]
        ALL_CONST = 16 * len(consts)

        def grp(buf, it):
            return buf[:, ds(TPG * it, TPG), :]

        def cols(it):
            return ds(GT * it, GT)

        S = PrepSems(sem, "p")
        STAT4 = (st4[:, 0, :], st4[:, 1, :], st4[:, 2, :])
        STAT80 = (st80[:, 0, :], st80[:, 1, :], st80[:, 2, :])
        KF0, KB0 = (6, 2), 5
        KF1 = 6

        def heads(x):
            return x.rearrange("p t (h d) -> p t h d", d=HD)

        def flat_heads(x):
            return x.rearrange("p t (h d) -> p (t h) d", d=HD)

        def over(stat, n):
            return stat.unsqueeze(2).broadcast_to([P, stat.shape[1], n])

        def mean_square(link, src, stat, inv_n, eps, done):
            link(V.tensor_reduce(stat[0], src, AX.X, ALU.add))
            V.tensor_scalar(stat[1], stat[0], inv_n, eps, ALU.mult, ALU.add).then_inc(done, 1)

        def act_root(stat, done):
            S_.activation(stat[2], stat[1], ACT.Sqrt).then_inc(done, 1)

        def dve_centre(dve, link, src, keep=None):
            last = V.tensor_reduce(st4[:, 0, :], src, AX.X, ALU.add)
            if keep is not None:
                last = V.tensor_copy(keep, src)
            link(last)
            link(V.tensor_scalar(st4[:, 1, :], st4[:, 0, :], -1.0 / P, None, ALU.mult))
            V.tensor_tensor(cen, src, over(st4[:, 1, :], P), ALU.add).then_inc(S.cen, 1)

        def dve_xn(dve, link, n):
            dve.wait_ge(S.std, n + 1)
            link(V.reciprocal(st4[:, 0, :], st4[:, 2, :]))
            wait_past(dve, S.xnT, n)
            V.tensor_tensor(xn_st[:, :, :], cen, over(st4[:, 0, :], P), ALU.mult).then_inc(S.xn, 1)

        def pe_transpose(src, bank, done):
            for t in range(TPG):
                last = PE_.transpose(ps[:, bank, t * P:(t + 1) * P], src[:, t, :], ident[:, :])
            last.then_inc(done, 1)

        def dve_prep0(dve, f, b, layer):
            link = Chain(dve, S.dch, (NG * (KF0[0] + KB0) if layer else 0)
                         + (NG if f is None else f) * KF0[layer] + (0 if b is None else b) * KB0)
            nf, nb = (None if x is None else layer * NG + x for x in (f, b))
            if b is not None:
                dve.wait_ge(S.qkvc, 2 * nb + 2)
                full, half = [P, TPG, HQK, HD], [P, TPG, HQK, HD // 2]
                x, w = heads(qkv_st[:, :, 0:NQK]), heads(rt)
                cs = cosT[:, layer, ds(TPG * b, TPG), :].unsqueeze(2)
                sn = sinT[:, layer, ds(TPG * b, TPG), :].unsqueeze(2)
                V.tensor_tensor(heads(ro), x, cs.broadcast_to(full), ALU.mult).then_inc(S.dch, 1)
                V.tensor_tensor(w[:, :, :, 0:HD:2], x[:, :, :, 1:HD:2], sn[:, :, :, 0:HD:2].broadcast_to(half),
                                ALU.mult).then_inc(S.dch, 1)
                link.k += 2
                link(V.tensor_tensor(w[:, :, :, 1:HD:2], x[:, :, :, 0:HD:2],
                                     sn[:, :, :, 1:HD:2].broadcast_to(half), ALU.mult))
                V.tensor_tensor(ro, ro, rt, ALU.add).then_inc(S.ro, 1)
            if f is not None and layer == 0:
                dve_centre(dve, link, grp(x_all, f))
            if b is not None:
                dve.wait_ge(S.sq3, nb + 1)
                mean_square(link, flat_heads(sq[:, :, :]), STAT80, 1.0 / HD, RMS_EPS, S.var3)
            if f is not None and layer == 0:
                dve.wait_ge(S.sq, nf + 1)
                mean_square(link, sq_ln, STAT4, 1.0 / P, LN_EPS, S.var)
            if b is not None:
                dve.wait_ge(S.std3, nb + 1)
                link(V.reciprocal(st80[:, 0, :], st80[:, 2, :]))
                V.tensor_tensor(flat_heads(rt), flat_heads(ro), over(st80[:, 0, :], HD), ALU.mult).then_inc(S.rn, 1)
            if f is not None and layer == 0:
                wait_past(dve, S.st, nf)
                dve_xn(dve, link, nf)
            if f is not None and layer == 1:
                dve_oproj(dve, nf - NG, f)
            if b is not None:
                dve.wait_ge(S.h, nb + 1)
                dve.wait_ge(S.rn, nb + 1)
                V.tensor_tensor(ro, rt, parts0[:, :, 0, :], ALU.subtract).then_inc(S.r1, 1)
            if f is not None:
                dve.wait_ge(S.sq2, nf + 1)
                mean_square(link, sq_ln, STAT4, 1.0 / P, RMS_EPS, S.var2)
            if b is not None:
                dve.wait_ge(S.m, nb + 1)
                dve.wait_ge(S.r1, nb + 1)
                V.tensor_tensor(parts0[:, :, 2, :], ro, parts0[:, :, 1, :], ALU.subtract).then_inc(S.l, 1)
                dve.wait_ge(S.l, nb + 1)
                V.tensor_copy(kparts[:, :, :].rearrange("p t (a n) -> p t a n", a=3),
                              parts0[:, :, :, HQ * HD:NQK]).then_inc(S.kp, 1)
            if f is not None:
                dve.wait_ge(S.std2, nf + 1)
                link(V.reciprocal(st4[:, 0, :], st4[:, 2, :]))
                V.tensor_tensor(y_st, cen if layer else xn_st[:, :, :], over(st4[:, 0, :], P), ALU.mult).then_inc(S.y, 1)
            assert link.k == (0 if f is None else KF0[layer]) + (0 if b is None else KB0)

        def act_prep0(act, f, b, layer):
            nf, nb = (None if x is None else layer * NG + x for x in (f, b))
            if f is not None and layer == 1:
                act_ost(act, nf - NG, f, AG.o, N_UNITS)
            if b is not None:
                act.wait_ge(S.ro, nb + 1)
                S_.activation(sq[:, :, :], ro, ACT.Square).then_inc(S.sq3, 1)
            if f is not None and layer == 1:
                act_oT(act, nf - NG)
            if f is not None and layer == 0:
                act.wait_ge(S.cen, nf + 1)
                S_.activation(sq_ln, cen, ACT.Square).then_inc(S.sq, 1)
            if b is not None:
                act.wait_ge(S.var3, nb + 1)
                act_root(STAT80, S.std3)
            if f is not None and layer == 0:
                act.wait_ge(S.var, nf + 1)
                act_root(STAT4, S.std)
            if b is not None:
                act.wait_ge(S.rn, nb + 1)
                wait_past(act, S.pT, nb)
                S_.activation(parts0[:, :, 0, :], rt, ACT.Copy).then_inc(S.h, 1)
            if f is not None:
                src = cen if layer else xn_st[:, :, :]
                if layer:
                    act.wait_ge(S.ores, nf - NG + 1)
                else:
                    act.wait_ge(S.xn, nf + 1)
                S_.activation(sq_ln, src, ACT.Square).then_inc(S.sq2, 1)
                last = S_.activation(grp(s_all, f), src, ACT.Copy)
                if layer == 0:
                    last = S_.activation(grp(acc, f), src, ACT.Copy)
                last.then_inc(S.st, 1)
            if b is not None:
                act.wait_ge(S.r1, nb + 1)
                S_.activation(parts0[:, :, 1, :], ro, ACT.Copy).then_inc(S.m, 1)
            if f is not None:
                act.wait_ge(S.var2, nf + 1)
                act_root(STAT4, S.std2)
            if f is not None and layer == 0:
                act_xnT(act, nf, f)
            if b is not None:
                act.wait_ge(S.pT, nb + 1)
                wait_past(act, S.scr, 32 * nb)
                S_.activation(pT[:, 0:3, :].rearrange("p a n -> p (a n)"), ps_bf[:, 6 * 1024:6 * 1024 + 3 * GT],
                              ACT.Copy).then_inc(S.pTc, 1)
                S_.activation(pT[0:96, 3, :], ps_bf[0:96, 6 * 1024 + 3 * GT:8 * 1024], ACT.Copy).then_inc(S.pTc, 1)
            if f is not None:
                act.wait_ge(S.yT, nf + 1)
                S_.activation(yT_st[:, :], ps[:, 1, :], ACT.Copy, scale=normw[:, layer:layer + 1]).then_inc(S.yTc, 1)
                act.wait_ge(S.qkv, nf + 1)
                wait_past(act, S.ro, nf)
                for k in range(2):
                    S_.activation(qkv_st[:, 2 * k:2 * k + 2, 0:NQKV],
                                  ps[:, 2 + k, 0:2 * NQKV].rearrange("p (t n) -> p t n", t=2),
                                  ACT.Copy).then_inc(S.qkvc, 1)
                act.wait_ge(S.qkvc, 2 * nf + 2)
                S_.activation(v_all[:, ds(TPG * f, TPG), 0:HKV, 0:HD],
                              qkv_st[:, :, NQK:NQKV].rearrange("p t (h d) -> p t h d", d=HD),
                              ACT.Copy).then_inc(S.vc, 1)
            if f is not None and layer == 0:
                act.wait_ge(S.lg, nf + 1)
                S_.activation(lg[:, ds(TPG * f, TPG), 0:E0],
                              ps[:, 4, 0:TPG * E0].rearrange("p (t e) -> p t e", t=TPG), ACT.Copy).then_inc(S.lgc, 1)

        def act_xnT(act, n, f):
            act.wait_ge(S.xnT, n + 1)
            S_.activation(aT_st[:, :], ps[:, 0, :], ACT.Copy).then_inc(S.xnTc, 1)
            act.wait_ge(S.xnTc, 2 * n + 1)
            S_.activation(xnT_all[:, cols(f)], aT_st[:, :], ACT.Copy).then_inc(S.xnTc, 1)

        def pe_prep0(pe, f, b, layer):
            nf, nb = (None if x is None else layer * NG + x for x in (f, b))
            if f is not None and layer == 1:
                pe_oT(pe, nf - NG)
                pe_oproj(pe, nf - NG, 0, 4)
            if f is not None and layer == 0:
                pe.wait_ge(S.xn, nf + 1)
                wait_past(pe, S.xnTc, 2 * nf)
                pe_transpose(xn_st, 0, S.xnT)
            if b is not None:
                pe.wait_ge(S.kp, nb + 1)
                wait_past(pe, S.pTc, 2 * nb)
                for a in range(3):
                    for t in range(TPG):
                        at = 6 * 1024 + a * GT + t * P
                        PE_.transpose(ps_bf[:, at:at + P], parts0[:, t, a, 0:P], identb[:, :])
                for t in range(TPG):
                    at = 6 * 1024 + 3 * GT + t * P
                    last = PE_.transpose(ps_bf[0:96, at:at + P], kparts[:, t, :], identb[:, :])
                last.then_inc(S.pT, 1)
            if f is not None:
                pe.wait_ge(S.y, nf + 1)
                wait_past(pe, S.yTc, nf)
                pe_transpose(y_st, 1, S.yT)
                pe.wait_ge(S.yTc, nf + 1)
                wait_past(pe, S.qkvc, 2 * nf)
                for t in range(TPG):
                    last = PE_.matmul(ps[:, 2 + t // 2, (t % 2) * NQKV:(t % 2 + 1) * NQKV],
                                      yT_st[:, t * P:(t + 1) * P], wqkv[:, layer, :], start=True, stop=True)
                last.then_inc(S.qkv, 1)
            if f is not None and layer == 0:
                pe.wait_ge(S.xnTc, 2 * nf + 2)
                wait_past(pe, S.lgc, nf)
                for t in range(TPG):
                    last = PE_.matmul(ps[:, 4, t * E0:(t + 1) * E0], aT_st[:, t * P:(t + 1) * P], rw0[:, :],
                                      start=True, stop=True)
                last.then_inc(S.lg, 1)

        def sp_stack0(sp, n, it, layer, used, total):
            if used is not None:
                sp.wait_ge(used, total)
            sp.wait_ge(S.pTc, 2 * n + 2)
            sp.dma_start(scr[layer, ds(it, 1), :, 0:3, :].rearrange("o p a t -> p (o a) t"), pT[:, 0:3, :]).then_inc(S.scr, 16)
            sp.dma_start(scr[layer, ds(it, 1), 0:96, 3:4, :].rearrange("o p a t -> p (o a) t"), pT[0:96, 3:4, :]).then_inc(S.scr, 16)
            sp.wait_ge(S.scr, 32 * n + 32)
            for a in range(3):
                for b in range(3):
                    r = (3 * a + b) * HD
                    sp.dma_start(q0s[r:r + HD, :, cols(it)],
                                 scr[layer, ds(it, 1), :, a, :].rearrange("o (h d) t -> d (o h) t", d=HD)).then_inc(S.stk, 16)
                    sp.dma_start(k0s[r:r + HD, :, cols(it)],
                                 scr[layer, ds(it, 1), 32 * b:32 * b + 32, 3, :].rearrange("o (h d) t -> d (o h) t", d=HD)).then_inc(S.stk, 16)

        STK0 = 18 * 16


        def sets0(g):
            return TPG * (g + 1)

        BASE_SET = [0]
        for g in range(NG):
            BASE_SET.append(BASE_SET[-1] + HKV * sets0(g))

        def att0_score(pe, A_, n, g, kv, kb, q0, first):
            w = GT - q0
            for u in range(2):
                if not first:
                    pe.wait_ge(A_.prob, 2 * n + u - 1)
                for j in range(2):
                    h = 4 * kv + 2 * u + j
                    last = PE_.matmul(ps[:, 2 * u + j, 0:w], k0s[0:KS0, kv, bass.ts(kb, P)],
                                      q0s[0:KS0, h, g * GT + q0:(g + 1) * GT], start=True, stop=True)
                last.then_inc(A_.score, 1)

        def att0_pv(pe, A_, n, par, bank, q0, masked, first, last_set):
            w = GT - q0
            pe.wait_ge(A_.vst, n + 1)
            if masked is not None:
                pe.wait_ge(A_.mask, masked)
            else:
                pe.wait_ge(A_.prob, 2 * n + 2)
            for h in range(4):
                last = PE_.matmul(ps[32 * h:32 * h + 32, bank, q0:GT], vst[:, par, 0, :],
                                  ring[:, 2 * par + h // 2, (h % 2) * w:(h % 2) * w + w],
                                  start=first, stop=last_set, skip_group_check=True)
            last.then_inc(A_.pv, 1)

        def plan0():
            for g in range(NG):
                for kv in range(HKV):
                    yield HKV * g + kv, g, kv, BASE_SET[g] + kv * sets0(g)

        def fin_transposes(pe, A_, c, bank):
            pe.wait_ge(A_.oT, c + 1)
            if c >= 1:
                pe.wait_ge(A_.o, c)
            for t in range(TPG):
                last = PE_.transpose(ps[:, bank, t * P:(t + 1) * P], oT[:, c % 2, t * P:(t + 1) * P], ident[:, :])
            last.then_inc(A_.fin, 1)

        def dve_out(dve, A_, c, bank, pv_done):
            dve.wait_ge(A_.pv, pv_done)
            if c >= 2:
                dve.wait_ge(A_.fin, c - 1)
            V.tensor_copy(oT[:, c % 2, :], ps[:, bank, :]).then_inc(A_.oT, 1)

        def dve_normalise(dve, A_, c, bank, g, col, hd):
            dve.wait_ge(A_.fin, c + 1)
            src = ps[:, bank, :].rearrange("p (t h d) -> p t h d", t=TPG, h=4)
            if c:
                dve.wait_ge(A_.o, c)
            V.reciprocal(rden[:, :, :], src[:, :, :, hd]).then_inc(A_.och, 1)
            dve.wait_ge(A_.och, c + 1)
            V.tensor_tensor(
                o_all[:, TPG * g:TPG * (g + 1), col:col + 4 * hd].rearrange("p t (h d) -> p t h d", h=4),
                src[:, :, :, 0:hd], rden[:, :, :].unsqueeze(3).broadcast_to([P, TPG, 4, hd]),
                ALU.mult).then_inc(A_.o, 1)

        N_SETS = BASE_SET[NG]
        N_UNITS = HKV * NG

        def act_ost(act, n, it, done, last):
            act.wait_ge(done, last)
            wait_past(act, S.oT, n)
            S_.activation(xn_st[:, :, :], grp(o_all, it), ACT.Copy).then_inc(S.ost, 1)

        def act_oT(act, n):
            act.wait_ge(S.oT, n + 1)
            S_.activation(aT_st[:, :], ps[:, 0, :], ACT.Copy).then_inc(S.oTc, 1)

        def pe_oT(pe, n):
            pe.wait_ge(S.ost, n + 1)
            pe_transpose(xn_st, 0, S.oT)

        def pe_oproj(pe, n, layer, bank):
            pe.wait_ge(S.oTc, n + 1)
            wait_past(pe, S.ores, n)
            for t in range(TPG):
                last = PE_.matmul(ps[:, bank, t * P:(t + 1) * P], aT_st[:, t * P:(t + 1) * P], wo[:, layer, :],
                                  start=True, stop=True)
            last.then_inc(S.op, 1)

        def dve_oproj(dve, n, it, bank=4):
            dve.wait_ge(S.op, n + 1)
            if bank == 4:
                dve.wait_ge(S.st, NG + n)
            V.tensor_tensor(cen, ps[:, bank, :].rearrange("p (t n) -> p t n", t=TPG), grp(s_all, it),
                            ALU.add).then_inc(S.ores, 1)

        def loc_score(pe, t, kv, w, first):
            n = 4 * t + kv
            if not first:
                pe.wait_ge(AL.prob, n - 1)
            for h in range(4):
                last = PE_.matmul(ps[:, 2 * (kv % 2) + h // 2, (h % 2) * w:(h % 2) * w + w],
                                  k0s[0:KS0, kv, ds(P * t, P)], q0s[0:KS0, 4 * kv + h, ds(P * t, w)],
                                  start=True, stop=True)
            last.then_inc(AL.score, 1)

        def loc_exp(act, t, kv, w, late):
            n = 4 * t + kv
            act.wait_ge(AL.score, n + 1)
            if late:
                act.wait_ge(AL.pv, n - 3)
            b = 2 * (kv % 2)
            S_.activation(ring[:, kv, 0:4 * w].rearrange("p (b q) -> p b q", b=2), ps[:, b:b + 2, 0:2 * w],
                          ACT.Exp, scale=float(HD) ** -0.5).then_inc(AL.prob, 1)

        def loc_mask(dve, t, kv, w):
            dve.wait_ge(AL.prob, 4 * t + kv + 1)
            d = ring[:, kv, 0:4 * w].rearrange("p (h q) -> p h q", h=4)
            V.tensor_tensor(d, d, band[:, 0:w].unsqueeze(1).broadcast_to([P, 4, w]), ALU.mult).then_inc(AL.mask, 1)

        def loc_pv(pe, t, par, kv, w, tile0):
            pe.wait_ge(AL.mask, 4 * t + kv + 1)
            if kv == 0:
                pe.wait_ge(AL.vst, t + 1)
            for h in range(4):
                last = PE_.matmul(ps[32 * h:32 * h + 32, 4 + par, kv * P:(kv + 1) * P], vst[:, par, kv, :],
                                  ring[:, kv, h * w:h * w + P], start=(tile0 and kv == 0), stop=True,
                                  skip_group_check=True)
            if w > P:
                if kv == 0 and not tile0:
                    pe.wait_ge(AL.oT, t)
                for h in range(4):
                    last = PE_.matmul(ps[32 * h:32 * h + 32, 5 - par, kv * P:kv * P + WIN], vst[:, par, kv, :],
                                      ring[:, kv, h * w + P:h * w + w], start=(kv == 0), stop=True,
                                      skip_group_check=True)
            last.then_inc(AL.pv, 1)

        def loc_fin(pe, t, par):
            pe.wait_ge(AL.oT, t + 1)
            wait_past(pe, AL.o, t)
            for kv in range(HKV):
                last = PE_.transpose(ps[:, 6, kv * P:(kv + 1) * P], oT[:, par, kv * P:(kv + 1) * P], ident[:, :])
            last.then_inc(AL.fin, 1)

        def loc_out(act, t, par):
            act.wait_ge(AL.pv, 4 * t + 4)
            if not (isinstance(t, int) and t == 0):
                act.wait_ge(AL.fin, t - 1)
            S_.activation(oT[:, par, :], ps[:, 4 + par, :], ACT.Copy).then_inc(AL.oT, 1)

        def loc_normalise(dve, t):
            dve.wait_ge(AL.fin, t + 1)
            src = ps[:, 6, :].rearrange("p (h d) -> p h d", d=32)
            r = rden[:, :, :].rearrange("p a b -> p (a b)")
            wait_past(dve, AL.o, t)
            V.reciprocal(r, src[:, :, HD]).then_inc(AL.och, 1)
            dve.wait_ge(AL.och, t + 1)
            V.tensor_tensor(o_all[:, ds(t, 1), :].rearrange("p o (h d) -> p (o h) d", d=HD), src[:, :, 0:HD],
                            over(r, HD), ALU.mult).then_inc(AL.o, 1)

        def loc_loop(eng, step):
            step(0, 0, True, False)
            step(1, 1, False, False)
            with eng.Fori(1, NT // 2 - 1) as i:
                step(2 * i, 0, False, False)
                step(2 * i + 1, 1, False, False)
            step(NT - 2, 0, False, False)
            step(NT - 1, 1, False, True)

        def route_dve(dve, R, sig):
            link = Chain(dve, R.ch)
            x = lg[:, :, 0:E0]
            link(V.tensor_reduce(rs[:, 0, :], x, AX.X, ALU.max))
            link(V.tensor_tensor(x, x, over(rs[:, 0, :], E0), ALU.subtract))
            V.nop().then_inc(R.ready, 1)
            dve.wait_ge(R.ex, 1)
            link(V.tensor_reduce(rs[:, 1, :], x, AX.X, ALU.add))
            link(V.reciprocal(rs[:, 2, :], rs[:, 1, :]))
            link(V.tensor_tensor(x, x, over(rs[:, 2, :], E0), ALU.mult))
            for t in range(NT):
                V.max(top[:, t, :], lg[:, t, 0:E0]).then_inc(R.ch, 1)
            link.k += NT
            dve.wait_ge(R.ch, link.k)
            link(V.memset(top[:, :, 2:8], -1.0))
            for t in range(NT):
                V.match_replace(pr[:, t, :], top[:, t, :], lg[:, t, 0:E0], 0.0).then_inc(R.ch, 1)
            link.k += NT
            dve.wait_ge(R.ch, link.k)
            link(V.tensor_tensor(gates[:, :, 0:E0], x, pr[:, :, :], ALU.subtract))
            if sig:
                link(V.tensor_scalar(rs[:, 3, :], lg[:, :, E0], 1.0, None, ALU.add))
                link(V.reciprocal(gates[:, :, E0], rs[:, 3, :]))
                link(V.tensor_copy(gates[:, :, E0 + 1], gates[:, :, E0]))
            V.nop().then_inc(R.ready, 1)

        def route_act(act, R, sig):
            act.wait_ge(R.ready, 1)
            last = S_.activation(lg[:, :, 0:E0], lg[:, :, 0:E0], ACT.Exp)
            if sig:
                last = S_.activation(lg[:, :, E0], lg[:, :, E0], ACT.Exp, scale=-1.0)
            last.then_inc(R.ex, 1)

        def moe_down(pe, M, n, par, k, chunks, lhs, slot, first):
            pe.wait_ge(M.hid, 2 * n + 2)
            if not first:
                pe.wait_ge(M.acc, n - 1)
            for t in range(TPG):
                for c in range(chunks):
                    last = PE_.matmul(ps[:, 4 + par, t * P:(t + 1) * P], lhs(c, t),
                                      wdn[0:k, slot, c, :], start=(c == 0), stop=(c == chunks - 1),
                                      skip_group_check=True)
            last.then_inc(M.dn, 1)

        def moe_add(dve, M, n, par, g, gate, late):
            dve.wait_ge(M.dn, n + 1)
            if late:
                dve.wait_ge(M.acc, n)
            for t in range(TPG):
                a = acc[:, TPG * g + t, :]
                y = ps[:, 4 + par, t * P:(t + 1) * P]
                if gate is None:
                    last = V.tensor_tensor(a, y, a, ALU.add)
                else:
                    last = V.scalar_tensor_tensor(out=a, in0=y, scalar=gate(TPG * g + t), in1=a,
                                                  op0=ALU.mult, op1=ALU.add)
            last.then_inc(M.acc, 1)

        def hid0(par, c, lo, n):
            return ring[:, 2 * par + c // 2, (c % 2) * GT + lo:(c % 2) * GT + lo + n]

        def up0(pe, n, g, slot, first):
            for c in range(FC0):
                if c % 2 == 0 and not first:
                    pe.wait_ge(M0.hid, 2 * n - 1 + c // 2)
                last = PE_.matmul(ps[:, c, :], wup[:, slot, c * P:(c + 1) * P], xnT_all[:, g * GT:(g + 1) * GT],
                                  start=True, stop=True)
                if c % 2:
                    last.then_inc(M0.up, 1)

        def gelu0(act, n, par, late):
            for u in range(2):
                act.wait_ge(M0.up, 2 * n + u + 1)
                if u == 0 and late:
                    act.wait_ge(M0.dn, n - 1)
                S_.activation(ring[:, 2 * par + u, :], ps[:, 2 * u:2 * u + 2, :].rearrange("p b n -> p (b n)"),
                              ACT.Gelu).then_inc(M0.hid, 1)

        def down0(pe, n, par, slot, first):
            moe_down(pe, M0, n, par, P, FC0, lambda c, t: hid0(par, c, t * P, P), slot, first)

        def up1(pe, n, g, slot, first, beside=None):
            for c in range(4):
                if not first and c == 0:
                    pe.wait_ge(M1.act, n)
                if not first and c == 2:
                    pe.wait_ge(M1.hid, 2 * n)
                last = PE_.matmul(ps[0:IC1, c, :], wup[:, slot, c * IC1:(c + 1) * IC1],
                                  xnT_all[:, g * GT:(g + 1) * GT], start=True, stop=True)
                if c % 2:
                    last.then_inc(M1.up, 1)
                if beside:
                    beside(c)

        def silu1(act, n, par, late):
            act.wait_ge(M1.up, 2 * n + 1)
            if late:
                act.wait_ge(M1.hid, 2 * n - 2)
            S_.activation(ring[0:IC1, 2 * par, :], ps[0:IC1, 0:2, :].rearrange("p b n -> p (b n)"),
                          ACT.Silu).then_inc(M1.act, 1)

        def mult1(dve, n, par, late):
            dve.wait_ge(M1.act, n + 1)
            dve.wait_ge(M1.up, 2 * n + 2)
            if late:
                dve.wait_ge(M1.dn, n - 1)
            V.tensor_tensor(ring[0:IC1, 2 * par + 1, :], ring[0:IC1, 2 * par, :],
                            ps[0:IC1, 2:4, :].rearrange("p b n -> p (b n)"), ALU.mult).then_inc(M1.hid, 2)

        def down1(pe, n, par, slot, first):
            moe_down(pe, M1, n, par, IC1, 2,
                     lambda c, t: ring[0:IC1, 2 * par + 1, c * GT + t * P:c * GT + (t + 1) * P], slot, first)

        NU1 = 2 * NG
        NKB = NT
        ROW = 8 * 16

        def where1(u):
            return 4 * (u // NG), GT * (u % NG)

        def max_product(pe, u, s, j, e, kc):
            h0, q0 = where1(u)
            m = 64 * u + 32 * s + 8 * j + 4 * e + kc
            pe.wait_ge(MX.mxr, m + 1)
            PE_.matmul(ps[:, 6 + kc % 2, :], q1s[0:KS1, ds(h0 + e + 2 * s, 1), ds(q0 + P * j, P)].rearrange("p o q -> p (o q)"),
                       k1s[0:KS1, ds(h0 + e + 2 * s, 1), kc * GT:(kc + 1) * GT].rearrange("p o q -> p (o q)"),
                       start=True, stop=True).then_inc(MX.mx, 1)

        def max_reduce(dve, u, s, j, e):
            m0 = 64 * u + 32 * s + 8 * j + 4 * e
            for kc in range(NG):
                dve.wait_ge(MX.mx, m0 + kc + 1)
                V.tensor_reduce(mxp[:, u % 2, ds(4 * e + 8 * s + j, 1), kc:kc + 1],
                                ps[:, 6 + kc % 2, :].unsqueeze(1), AX.X, ALU.max).then_inc(MX.mxr, 1)

        def max_tail_dve(dve, u):
            dve.wait_ge(MX.mxr, 64 * u + 66)
            if u:
                dve.wait_ge(MX.mnT, u)
            V.tensor_reduce(mneg[:, 0, :], mxp[:, u % 2, :, :], AX.X, ALU.max).then_inc(MX.mn, 1)
            dve.wait_ge(MX.mn, 4 * u + 1)
            V.tensor_scalar(mneg[:, 1, :], mneg[:, 0, :], -1.0, None, ALU.mult).then_inc(MX.mn, 1)
            dve.wait_ge(MX.mn, 4 * u + 2)
            V.tensor_copy(mparts[:, 0, :], mneg[:, 1, :]).then_inc(MX.mn, 1)
            dve.wait_ge(MX.mn, 4 * u + 3)
            V.tensor_tensor(mparts[:, 1, :], mneg[:, 1, :], mparts[:, 0, :], ALU.subtract).then_inc(MX.mn, 1)

        def max_tail_pe(pe, u, bank):
            pe.wait_ge(MX.mn, 4 * u + 4)
            PE_.transpose(ps_bf[0:32, bank * 1024:bank * 1024 + P], mparts[:, :, :].rearrange("p a m -> p (a m)"),
                          identb[:, :]).then_inc(MX.mnT, 1)

        def max_tail_act(act, u, bank):
            act.wait_ge(MX.mnT, u + 1)
            if u:
                act.wait_ge(MX.row, ROW * u)
            S_.activation(mT[:, :], ps_bf[0:32, bank * 1024:bank * 1024 + P], ACT.Copy).then_inc(MX.mnTc, 1)

        def max_tail_sp(sp, u):
            h0, q0 = where1(u)
            sp.wait_ge(MX.mnTc, u + 1)
            for a in range(2):
                for h in range(4):
                    sp.dma_start(q1s[KS1 + a:KS1 + a + 1, h0 + h, q0:q0 + GT],
                                 mT[16 * a + 4 * h:16 * a + 4 * h + 4, :]).then_inc(MX.row, 16)

        def att1_score(pe, n, u, kb, w, first=False):
            h0, q0 = where1(u)
            if not first:
                pe.wait_ge(AB.prob, 2 * n + w - 1)
            for h in (2 * w, 2 * w + 1):
                last = PE_.matmul(ps[:, h, :], k1s[0:KM1, h0 + h, ds(P * kb, P)],
                                  q1s[0:KM1, h0 + h, q0:q0 + GT], start=True, stop=True)
            last.then_inc(AB.score, 1)

        def att1_exp(act, n, par, late):
            for w in range(2):
                act.wait_ge(AB.score, 2 * n + w + 1)
                if late:
                    act.wait_ge(AB.pv, n - 1)
                S_.activation(ring[:, 2 * par + w, :], ps[:, 2 * w:2 * w + 2, :].rearrange("p b n -> p (b n)"),
                              ACT.Exp, scale=float(HD1) ** -0.5).then_inc(AB.prob, 1)

        def att1_pv(pe, n, par, bank, w):
            if w == 0:
                pe.wait_ge(AB.vst, n + 1)
            pe.wait_ge(AB.prob, 2 * n + w + 1)
            for h in (2 * w, 2 * w + 1):
                last = PE_.matmul(ps[32 * h:32 * h + 32, bank, :], vst[:, par, h, :],
                                  ring[:, 2 * par + w, (h % 2) * GT:(h % 2 + 1) * GT],
                                  start=False, stop=True, skip_group_check=True)
            if w:
                last.then_inc(AB.pv, 1)

        def att1_clear(pe, bank):
            for h in range(4):
                PE_.matmul(ps[32 * h:32 * h + 32, bank, :], zerob[:, 0:32], zerob[:, :], start=True, stop=False,
                           skip_group_check=True)

        B1 = (1, 2, 3, 4)
        BP = 5

        def act_prep1(act, f, b):
            if b is not None:
                act.wait_ge(S.qkvc, 2 * (2 * NG + b) + 2)
                act.wait_ge(S.pT, 2 * NG + b)
                S_.activation(parts1[:, :, 0, :], qkv_st[:, :, 0:2 * P], ACT.Copy).then_inc(S.h, 1)
                S_.activation(v_all[:, ds(TPG * b, TPG), :, 0:HD1],
                              qkv_st[:, :, 2 * P:3 * P].rearrange("p t (h d) -> p t h d", d=HD1),
                              ACT.Copy).then_inc(S.vc, 1)
            if f is not None:
                act_ost(act, NG + f, f, AL.o, NT)
            if b is not None:
                act.wait_ge(S.r1, 2 * NG + b + 1)
                S_.activation(parts1[:, :, 1, :], res1, ACT.Copy).then_inc(S.m, 1)
            if f is not None:
                act_oT(act, NG + f)
            if b is not None:
                act.wait_ge(S.pT, 2 * NG + b + 1)
                act.wait_ge(S.scr, 32 * (2 * NG + b))
                for half in range(2):
                    S_.activation(pT[:, 3 * half:3 * half + 3, :].rearrange("p a n -> p (a n)"),
                                  ps_bf[:, BP * 1024 + 3 * GT * half:BP * 1024 + 3 * GT * (half + 1)],
                                  ACT.Copy).then_inc(S.pTc, 1)
            if f is not None:
                n = NG + f
                act.wait_ge(S.cen, n + 1)
                S_.activation(sq_ln, cen, ACT.Square).then_inc(S.sq, 1)
                act.wait_ge(S.var, n + 1)
                act_root(STAT4, S.std)
                act_xnT(act, n, f)
                act.wait_ge(S.lg, n + 1)
                S_.activation(lg[:, ds(TPG * f, TPG), :],
                              ps[:, 0, 0:TPG * (E0 + 1)].rearrange("p (t e) -> p t e", t=TPG), ACT.Copy).then_inc(S.lgc, 1)

        def pe_prep1(pe, f, b):
            if f is not None:
                pe.wait_ge(S.lgc, NG + f)
                pe_oT(pe, NG + f)
                pe_oproj(pe, NG + f, 1, 0)
            if b is not None:
                pe.wait_ge(S.l, 2 * NG + b + 1)
                pe.wait_ge(S.pTc, 2 * (2 * NG + b))
                for half in range(2):
                    for a in range(3):
                        for t in range(TPG):
                            at = BP * 1024 + (3 * half + a) * GT + t * P
                            last = PE_.transpose(ps_bf[:, at:at + P], parts1[:, t, a, half * P:(half + 1) * P],
                                                 identb[:, :])
                last.then_inc(S.pT, 1)
            if f is not None:
                n = NG + f
                pe.wait_ge(S.xn, n + 1)
                pe_transpose(xn_st, 0, S.xnT)
                pe.wait_ge(S.xnTc, 2 * n + 1)
                pe.wait_ge(S.qkvc, 2 * (n + NG))
                for t in range(TPG):
                    last = PE_.matmul(ps[:, B1[t], 0:3 * P], aT_st[:, t * P:(t + 1) * P], wl1[:, :],
                                      start=True, stop=True)
                last.then_inc(S.qkv, 1)
                for t in range(TPG):
                    last = PE_.matmul(ps[:, 0, t * (E0 + 1):(t + 1) * (E0 + 1)], aT_st[:, t * P:(t + 1) * P],
                                      rw1[:, :], start=True, stop=True)
                last.then_inc(S.lg, 1)

        def dve_prep1(dve, f, b):
            link = Chain(dve, S.dch, NG * (KF0[0] + KF0[1] + 2 * KB0) + (0 if f is None else f) * KF1)
            if b is not None:
                dve.wait_ge(S.h, 2 * NG + b + 1)
                V.tensor_tensor(res1, qkv_st[:, :, 0:2 * P], parts1[:, :, 0, :], ALU.subtract).then_inc(S.r1, 1)
                dve.wait_ge(S.m, 2 * NG + b + 1)
                dve.wait_ge(S.r1, 2 * NG + b + 1)
                V.tensor_tensor(parts1[:, :, 2, :], res1, parts1[:, :, 1, :], ALU.subtract).then_inc(S.l, 1)
            if f is not None:
                n = NG + f
                dve_oproj(dve, n, f, 0)
                dve.wait_ge(S.ores, n + 1)
                link(V.tensor_tensor(cen, cen, grp(acc, f), ALU.mult))
                link(V.tensor_tensor(cen, grp(x_all, f), cen, ALU.add))
                dve_centre(dve, link, cen, keep=grp(x_all, f))
                dve.wait_ge(S.sq, n + 1)
                mean_square(link, sq_ln, STAT4, 1.0 / P, LN_EPS, S.var)
                dve_xn(dve, link, n)
                dve.wait_ge(S.qkv, n + NG + 1)
                dve.wait_ge(S.h, n + NG)
                dve.wait_ge(S.vc, n + NG)
                for t in range(TPG):
                    last = V.tensor_tensor(qkv_st[:, t, :], ps[:, B1[t], 0:3 * P], bias1[:, :], ALU.add)
                last.then_inc(S.qkvc, 2)
                dve.wait_ge(S.qkvc, 2 * (n + NG) + 2)
                assert link.k == KF1

        def sp_tail(sp):
            with sp.Fori(0, NG) as it:
                sp_stack0(sp, NG + it, it, 1, AG.pv, N_SETS)

            def load(w, slot, up_src, dn_src, k, c, n_up):
                sp.dma_start(wup[:, slot, 0:n_up], up_src.rearrange("o d f -> (o d) f")).then_inc(w[slot], 16)
                sp.dma_start(wdn[0:k, slot, 0:c, :], dn_src.rearrange("o f c d -> (o f) c d")).then_inc(w[slot], 16)

            def load0(x, slot):
                load(w0, slot, A.up0[ds(x, 1)], A.dn0[ds(x, 1)], P, FC0, F0)
            load0(0, 1)
            load0(1, 0)
            sp.wait_ge(M0.dn, 4)
            load0(2, 1)
            with sp.Fori(1, E0 // 2) as i:
                sp.wait_ge(M0.dn, 8 * i)
                load0(1 + 2 * i, 0)
                sp.wait_ge(M0.dn, 8 * i + 4)
                load0(2 + 2 * i, 1)
            def load1(x, slot):
                load(w1, slot, A.up1[ds(x, 1)], A.dn1[ds(x, 1)], IC1, 2, 4 * IC1)
            sp.wait_ge(M0.dn, 4 * (E0 + 1))
            load1(0, 0)
            load1(1, 1)
            with sp.Fori(0, NG) as it:
                n = 2 * NG + it
                sp.wait_ge(AL.o, NT)
                sp.wait_ge(S.pTc, 2 * n + 2)
                for half in range(2):
                    sp.dma_start(scr[2, ds(it, 1), :, 3 * half:3 * half + 3, :].rearrange("o p a t -> p (o a) t"),
                                 pT[:, 3 * half:3 * half + 3, :]).then_inc(S.scr, 16)
                sp.wait_ge(S.scr, 32 * n + 32)
                for r, (a, b) in enumerate(PRODUCTS1):
                    for dst, part in ((q1s, a), (k1s, 3 + b)):
                        sp.dma_start(dst[r * HD1:(r + 1) * HD1, :, cols(it)],
                                     scr[2, ds(it, 1), :, part, :].rearrange("o (h d) t -> d (o h) t", d=HD1))\
                            .then_inc(s_stk1, 16)
            with sp.Fori(1, E1 // 2) as i:
                for e in range(2):
                    sp.wait_ge(M1.dn, 8 * i + 4 * e - 4)
                    load1(2 * i + e, e)
            for u in range(NU1):
                max_tail_sp(sp, u)
            with sp.Fori(0, NG) as it:
                sp.wait_ge(s_y, it + 1)
                sp.dma_start(A.out[cols(it), :].rearrange("(t p) d -> p t d", p=P), grp(x_all, it)).then_inc(s_out, 16)
            sp.wait_ge(s_out, 16 * NG)

        def pool_tail(pool):
            G_.memset(zerob[:, :], 0.0).then_inc(s_zero, 1)
            pool.wait_ge(S.vc, 2 * NG)
            pool.wait_ge(AG.pv, N_SETS)
            pool.wait_ge(s_zero, 1)

            def stage(t, par, first, last):
                if not first:
                    pool.wait_ge(AL.pv, 4 * t - 4)
                G_.tensor_copy(vst[:, par, :, 0:HD + 1],
                               v_all[:, ds(t, 1), 0:HKV, 0:HD + 1].rearrange("p o h d -> p (o h) d")).then_inc(AL.vst, 1)
            loc_loop(pool, stage)
            pool.wait_ge(AL.pv, 4 * NT)
            G_.memset(k1s[KS1:KM1, :, :], 1.0).then_inc(s_zero, 1)
            pool.wait_ge(s_zero, 2)
            pool.wait_ge(S.vc, 3 * NG)
            for u in range(NU1):
                h0, _ = where1(u)

                def stage1(n, e, kb, late):
                    if late:
                        pool.wait_ge(AB.pv, n - 1)
                    G_.tensor_copy(vst[:, e, :, 0:VW],
                                   v_all[:, ds(kb, 1), h0:h0 + 4, :].rearrange("p o h d -> p (o h) d")).then_inc(AB.vst, 1)
                if u == 0:
                    stage1(0, 0, 0, False)
                    stage1(1, 1, 1, False)
                with pool.Fori(1 if u == 0 else 0, NKB // 2) as j:
                    for e in range(2):
                        stage1(NKB * u + 2 * j + e, e, 2 * j + e, True)

        def act_tail(act):
            over_rounds(act, lambda f, b: act_prep0(act, f, b, 1), 1)

            def tile(t, par, first, last):
                w = P if last else LW
                for kv in range(HKV):
                    loc_exp(act, t, kv, w, not first)
                    if kv == 0 and not first:
                        loc_out(act, t - 1, 1 - par)
            loc_loop(act, tile)
            loc_out(act, NT - 1, 1)
            route_act(act, R0, False)
            for g in range(NG):
                gelu0(act, g, g % 2, g >= 2)
            with act.Fori(0, E0 // 2) as i:
                for e in range(2):
                    for g in range(NG):
                        gelu0(act, 4 + 8 * i + 4 * e + g, g % 2, True)
            act.wait_ge(M0.acc, 4 * (E0 + 1))
            S_.activation(acc[:, :, :], acc[:, :, :], ACT.Silu).then_inc(s_silu, 1)
            over_rounds(act, lambda f, b: act_prep1(act, f, b), 1)
            route_act(act, R1, True)
            silu1(act, 0, 0, False)
            silu1(act, 1, 1, False)
            for n in range(2, 8):
                silu1(act, n, n % 2, True)
            with act.Fori(1, E1 // 2) as i:
                for k in range(8):
                    silu1(act, 8 * i + k, k % 2, True)
            act.wait_ge(M1.acc, 4 * E1)
            S_.activation(acc[:, :, :], acc[:, :, :], ACT.Silu).then_inc(s_silu, 1)
            max_tail_act(act, 0, 4)
            for u in range(NU1):
                n0 = NKB * u

                def pair(j, late):
                    for e in range(2):
                        att1_exp(act, n0 + 2 * j + e, e, late)
                pair(0, u > 0)
                with act.Fori(1, 4) as j:
                    pair(j, True)
                pair(4, True)
                if u + 1 < NU1:
                    max_tail_act(act, u + 1, 4 + (u + 1) % 2)
                with act.Fori(5, 8) as j:
                    pair(j, True)

        def pe_moe(units, up, down):
            for k, (n, g, slot, first) in enumerate(units):
                up(n, g, slot, first)
                if k:
                    down(*units[k - 1])
            down(*units[-1])

        def pe_tail(pe):
            over_rounds(pe, lambda f, b: pe_prep0(pe, f, b, 1), 1)
            pe.wait_ge(S.stk, 2 * NG * STK0)
            pe.wait_ge(S.pTc, 4 * NG)
            pe.wait_ge(S.qkvc, 4 * NG)
            pe.wait_ge(AG.o, N_UNITS)
            loc_score(pe, 0, 0, LW, True)

            def tile(t, par, first, last):
                w = P if last else LW
                for kv in range(HKV):
                    if kv + 1 < HKV:
                        loc_score(pe, t, kv + 1, w, first and kv == 0)
                    elif not last:
                        loc_score(pe, t + 1, 0, P if isinstance(t, int) and t == NT - 2 else LW, False)
                    loc_pv(pe, t, par, kv, w, first)
                    if kv == 1 and not first:
                        loc_fin(pe, t - 1, 1 - par)
            loc_loop(pe, tile)
            loc_fin(pe, NT - 1, 1)

            pe.wait_ge(AL.oT, NT)
            def up(n, g, slot, first):
                up0(pe, n, g, slot, first)

            def down(n, g, slot, first):
                down0(pe, n, g % 2, slot, first or (isinstance(n, int) and n < 2))
            pe.wait_ge(w0[1], 32)
            pe_moe([(g, g, 1, g == 0) for g in range(NG)], up, down)
            with pe.Fori(0, E0 // 2) as i:
                pe.wait_ge(w0[0], 32 * i + 32)
                units = [(4 + 8 * i + g, g, 0, False) for g in range(NG)]
                more = [(8 + 8 * i + g, g, 1, False) for g in range(NG)]

                def up_(n, g, slot, first):
                    if slot and g == 0:
                        pe.wait_ge(w0[1], 32 * i + 64)
                    up0(pe, n, g, slot, first)
                pe_moe(units + more, up_, down)

            over_rounds(pe, lambda f, b: pe_prep1(pe, f, b), 1)

            pe.wait_ge(S.pTc, 6 * NG)
            pe.wait_ge(S.lgc, 2 * NG)
            pe.wait_ge(S.qkvc, 6 * NG)

            def down1_(n, g, slot, first):
                down1(pe, n, g % 2, slot, first or (isinstance(n, int) and n < 2))

            def pair1(i, first, beside=None):
                pe.wait_ge(w1[0], 32 * i + 32)
                pe.wait_ge(w1[1], 32 * i + 32)
                pe_moe([(8 * i + 4 * e + g, g, e, first and e + g == 0) for e in range(2) for g in range(NG)],
                       lambda n, g, e, first: up1(pe, n, g, e, first, beside and beside(4 * e + g)), down1_)
            pair1(0, True)
            pe.wait_ge(s_stk1, 2 * len(PRODUCTS1) * 16 * NG)
            for u in range(2):
                with pe.Fori(0, 2) as s:
                    pair1(1 + 2 * u + s, False,
                          lambda k: lambda kc: max_product(pe, u, s, k // 2, k % 2, kc))

            pe.wait_ge(s_zero, 2)
            pe.wait_ge(M1.acc, 4 * E1)
            max_tail_pe(pe, 0, 4)
            pe.wait_ge(MX.row, ROW)
            pe.wait_ge(M1.hid, 2 * 4 * E1)
            for w in range(2):
                att1_score(pe, 0, 0, 0, w, True)
            for u in range(NU1):
                n0, bank, other = NKB * u, 4 + u % 2, 4 + (u + 1) % 2

                def pair(j, half, last=False):
                    for e in range(2):
                        n = n0 + 2 * j + e

                        def score(w):
                            if not (last and e):
                                att1_score(pe, n + 1, u, 2 * j + e + 1, w)
                            elif u + 1 < NU1:
                                if w == 0:
                                    pe.wait_ge(MX.row, ROW * (u + 2))
                                att1_score(pe, n + 1, u + 1, 0, w)

                        def maximum(kc):
                            if u + 2 < NU1:
                                max_product(pe, u + 2, half, j - 4 * half, e, kc)
                        score(0)
                        maximum(0)
                        score(1)
                        maximum(1)
                        att1_pv(pe, n, e, bank, 0)
                        maximum(2)
                        att1_pv(pe, n, e, bank, 1)
                        maximum(3)
                pe.wait_ge(MX.mnTc, u + 1)
                if u >= 2:
                    pe.wait_ge(AB.o, u - 1)
                att1_clear(pe, bank)
                with pe.Fori(0, 4) as j:
                    pair(j, 0)
                if u:
                    fin_transposes(pe, AB, u - 1, other)
                pair(4, 1)
                if u + 1 < NU1:
                    if u:
                        pe.wait_ge(AB.o, u)
                    max_tail_pe(pe, u + 1, other)
                with pe.Fori(5, 7) as j:
                    pair(j, 1)
                pair(7, 1, last=True)
            fin_transposes(pe, AB, NU1 - 1, 4 + (NU1 - 1) % 2)

        def dve_tail(dve):
            over_rounds(dve, lambda f, b: dve_prep0(dve, f, b, 1), 1)

            def tile(t, par, first, last):
                w = P if last else LW
                for kv in range(HKV):
                    loc_mask(dve, t, kv, w)
                    if kv == 1 and not first:
                        loc_normalise(dve, t - 1)
            loc_loop(dve, tile)
            loc_normalise(dve, NT - 1)
            route_dve(dve, R0, False)
            for g in range(NG):
                moe_add(dve, M0, g, g % 2, g, None, g > 0)
            with dve.Fori(0, E0 // 2) as i:
                for e in range(2):
                    for g in range(NG):
                        moe_add(dve, M0, 4 + 8 * i + 4 * e + g, g % 2, g,
                                lambda t: gates[:, t, ds(2 * i + e, 1)], True)
            dve.wait_ge(s_silu, 1)
            over_rounds(dve, lambda f, b: dve_prep1(dve, f, b), 1)
            V.memset(acc[:, :, :], 0.0).then_inc(s_cleared, 1)
            route_dve(dve, R1, True)

            def gate1(x):
                return lambda t: gates[:, t, ds(x, 1)]
            dve.wait_ge(s_cleared, 1)
            for _ in range(2):
                V.nop().then_inc(MX.mxr, 1)

            def pair1(i, first, u=None, s=None):
                units = [(8 * i + 4 * e + g, g, e) for e in range(2) for g in range(NG)]
                for k, (n, g, e) in enumerate(units):
                    if u is not None:
                        max_reduce(dve, u, s, k // 2, k % 2)
                    mult1(dve, n, g % 2, not (first and k < 2))
                    if k:
                        m, mg, me = units[k - 1]
                        moe_add(dve, M1, m, mg % 2, mg, gate1(2 * i + me), not (first and k == 1))
                m, mg, me = units[-1]
                moe_add(dve, M1, m, mg % 2, mg, gate1(2 * i + me), True)
            pair1(0, True)
            for u in range(2):
                with dve.Fori(0, 2) as s:
                    pair1(1 + 2 * u + s, False, u, s)
            max_tail_dve(dve, 0)

            def maxima(u, s):
                with dve.Fori(0, 4) as j:
                    for e in range(2):
                        max_reduce(dve, u, s, j, e)

            def finish(u):
                g = u % NG
                dve_normalise(dve, AB, u, 4 + u % 2, g, 64 * (u // NG), HD1)
                if u < NG:
                    return
                dve.wait_ge(AB.o, u + 1)
                if g == 0:
                    dve.wait_ge(s_silu, 2)
                else:
                    dve.wait_ge(s_y, g)
                V.tensor_tensor(xn_st[:, :, :], grp(o_all, g), grp(acc, g), ALU.mult).then_inc(s_prod, 1)
                dve.wait_ge(s_prod, g + 1)
                V.tensor_tensor(grp(x_all, g), grp(x_all, g), xn_st[:, :, :], ALU.add).then_inc(s_y, 1)
            for u in range(NU1):
                if u + 1 < NU1:
                    max_tail_dve(dve, u + 1)
                if u:
                    dve_out(dve, AB, u - 1, 4 + (u - 1) % 2, NKB * u)
                if u + 2 < NU1:
                    maxima(u + 2, 0)
                if u:
                    finish(u - 1)
                if u + 2 < NU1:
                    maxima(u + 2, 1)
            dve_out(dve, AB, NU1 - 1, 4 + (NU1 - 1) % 2, NKB * NU1)
            finish(NU1 - 1)

        @block.sync
        def _(sp):
            for g in range(NG):
                sp.dma_start(x_all[:, TPG * g:TPG * (g + 1), :],
                             A.x[GT * g:GT * (g + 1), :].rearrange("(t p) d -> p t d", p=P)).then_inc(s_x, 16)
            for dst, src in consts:
                sp.dma_start(dst, src).then_inc(s_const, 16)
            over_groups(sp, lambda it: sp_stack0(sp, it, it, 0, None, None))
            sp_tail(sp)

        @block.gpsimd
        def _(pool):
            G_.memset(v_all[:, :, :, :], 1.0).then_inc(s_vones, 1)
            G_.memset(vst[:, :, :, :], 0.0).then_inc(s_vones, 1)
            pool.wait_ge(s_vones, 2)
            pool.wait_ge(S.vc, NG)
            def stage_v(n, par, kb, kv, late):
                if late:
                    pool.wait_ge(AG.pv, n - 1)
                G_.tensor_copy(vst[:, par, 0:1, 0:HD + 1],
                               v_all[:, ds(kb, 1), kv, 0:HD + 1]).then_inc(AG.vst, 1)
            for c, g, kv, n0 in plan0():
                for i in range(4):
                    stage_v(n0 + i, i % 2, TPG * g + i, kv, n0 + i >= 2)
                if g:
                    with pool.Fori(0, 2 * g) as j:
                        for e in range(2):
                            stage_v(n0 + 4 + 2 * j + e, e, 2 * j + e, kv, True)
            pool_tail(pool)

        @block.scalar
        def _(act):
            act.wait_ge(s_const, ALL_CONST)
            S_.activation(identb[:, :], ident[:, :], ACT.Copy).then_inc(s_identb, 1)
            act.wait_ge(s_fold, 1)
            S_.activation(wqkv[:, 0, P:NQKV], ps[:, 5, 0:2 * HKV * HD], ACT.Copy).then_inc(s_foldc, 1)
            act.wait_ge(s_fold, 2)
            S_.activation(wl1[:, :], ps[:, 4, 0:3 * P], ACT.Copy).then_inc(s_foldc, 1)
            act.wait_ge(s_vones, 2)
            over_rounds(act, lambda f, b: act_prep0(act, f, b, 0), 2)

            def exps(n, u, par, w, late):
                act.wait_ge(AG.score, 2 * n + u + 1)
                if late:
                    act.wait_ge(AG.pv, n - 1)
                S_.activation(ring[:, 2 * par + u, 0:2 * w].rearrange("p (h q) -> p h q", h=2),
                              ps[:, 2 * u:2 * u + 2, 0:w], ACT.Exp, scale=float(HD) ** -0.5).then_inc(AG.prob, 1)
            for c, g, kv, n0 in plan0():
                for i in range(4):
                    for u in range(2):
                        exps(n0 + i, u, i % 2, GT - P * i, n0 + i >= 2)
                if g:
                    with act.Fori(0, 2 * g) as j:
                        for e in range(2):
                            for u in range(2):
                                exps(n0 + 4 + 2 * j + e, u, e, GT, True)
            act_tail(act)

        @block.tensor
        def _(pe):
            pe.wait_ge(s_const, ALL_CONST)
            PE_.matmul(ps[:, 5, 0:2 * HKV * HD], kvdT[:, :], kvup[:, :], start=True, stop=True).then_inc(s_fold, 1)
            for m in range(3):
                for c in range(2):
                    last = PE_.matmul(ps[:, 4, m * P:(m + 1) * P], lrV[:, m, c, :], lrU[:, m, c, :],
                                      start=(c == 0), stop=(c == 1))
            last.then_inc(s_fold, 1)
            pe.wait_ge(s_foldc, 2)
            pe.wait_ge(s_identb, 1)
            over_rounds(pe, lambda f, b: pe_prep0(pe, f, b, 0), 2)

            pe.wait_ge(S.stk, NG * STK0)
            pe.wait_ge(S.pTc, 2 * NG)
            pe.wait_ge(S.lgc, NG)
            pe.wait_ge(S.qkvc, 2 * NG)
            units = list(plan0())
            att0_score(pe, AG, 0, 0, 0, 0, 0, True)
            for c, g, kv, n0 in units:
                bank = 4 + c % 2
                NSET = sets0(g)
                nxt = units[c + 1] if c + 1 < len(units) else None

                def first_of_next():
                    if nxt:
                        att0_score(pe, AG, nxt[3], nxt[1], nxt[2], TPG * nxt[1], 0, False)
                for i in range(4):
                    if i < 3:
                        att0_score(pe, AG, n0 + i + 1, g, kv, TPG * g + i + 1, P * (i + 1), n0 + i + 1 < 1)
                    elif g:
                        att0_score(pe, AG, n0 + 4, g, kv, 0, 0, False)
                    else:
                        first_of_next()
                    if i == 0 and c >= 2:
                        pe.wait_ge(AG.oT, c - 1)
                    att0_pv(pe, AG, n0 + i, i % 2, bank, P * i, 8 * c + 2 * i + 2, i == 0, False)
                    if i == 1 and c:
                        fin_transposes(pe, AG, c - 1, 6)
                if g:
                    if g > 0:
                        with pe.Fori(0, 2 * g - 1) as j:
                            for e in range(2):
                                att0_score(pe, AG, n0 + 4 + 2 * j + e + 1, g, kv, 2 * j + e + 1, 0, False)
                                att0_pv(pe, AG, n0 + 4 + 2 * j + e, e, bank, 0, None, False, False)
                    m = 4 * g - 2
                    att0_score(pe, AG, n0 + 4 + m + 1, g, kv, m + 1, 0, False)
                    att0_pv(pe, AG, n0 + 4 + m, 0, bank, 0, None, False, False)
                    first_of_next()
                    att0_pv(pe, AG, n0 + 4 + m + 1, 1, bank, 0, None, False, True)
            fin_transposes(pe, AG, N_UNITS - 1, 6)
            pe_tail(pe)

        @block.vector
        def _(dve):
            dve.wait_ge(s_x, 16 * NG)
            over_rounds(dve, lambda f, b: dve_prep0(dve, f, b, 0), 2)
            for c, g, kv, n0 in plan0():
                if c:
                    dve_out(dve, AG, c - 1, 4 + (c - 1) % 2, n0)
                for i in range(4):
                    w = GT - P * i
                    for u in range(2):
                        dve.wait_ge(AG.prob, 2 * (n0 + i) + u + 1)
                        d = ring[:, 2 * (i % 2) + u, 0:2 * w].rearrange("p (h q) -> p h q", h=2)[:, :, 0:P]
                        V.tensor_tensor(d, d, tri[:, :].unsqueeze(1).broadcast_to([P, 2, P]),
                                        ALU.mult).then_inc(AG.mask, 1)
                    if i == 1 and c:
                        dve_normalise(dve, AG, c - 1, 6, (c - 1) // HKV, ((c - 1) % HKV) * 32, HD)
            dve_out(dve, AG, N_UNITS - 1, 4 + (N_UNITS - 1) % 2, N_SETS)
            dve_normalise(dve, AG, N_UNITS - 1, 6, NG - 1, 96, HD)
            dve_tail(dve)


def _arrays(i):
    import numpy as np

    f = {k: np.ascontiguousarray(np.asarray(v)) for k, v in i.items()}
    tok = np.arange(T, dtype=np.float32)
    cos, sin = np.empty((P, 2, NT, HD), np.float32), np.empty((P, 2, NT, HD), np.float32)
    for n, base in enumerate((1000000.0, 10000.0)):
        inv = (1.0 / np.float32(base) ** (np.arange(0, HD, 2, dtype=np.float32) / np.float32(HD))).astype(np.float32)
        fr = (tok[:, None] * inv[None, :]).reshape(NT, P, HD // 2).transpose(1, 0, 2)
        cos[:, n, :, 0::2] = cos[:, n, :, 1::2] = np.cos(fr)
        sin[:, n, :, 0::2], sin[:, n, :, 1::2] = -np.sin(fr), np.sin(fr)
    k, q = np.arange(P)[:, None], np.arange(LW)[None, :]

    def blocks(w):
        h, a, b = w.shape
        out = np.zeros((h * a, h * b), w.dtype)
        for n in range(h):
            out[n * a:(n + 1) * a, n * b:(n + 1) * b] = w[n]
        return out.reshape(2, P, h * b).transpose(1, 0, 2)

    L = "L1_attn_"
    gu = f["L1_ffn_experts_gate_up"]
    sg, su, sd = f["L1_ffn_shared_gate_w"], f["L1_ffn_shared_up_w"], f["L1_ffn_shared_down_w"]
    g1 = np.concatenate([gu[:, :I1], sg.reshape(2, I1, P)])
    u1 = np.concatenate([gu[:, I1:], su.reshape(2, I1, P)])
    up1 = np.concatenate([g1, u1], axis=1).transpose(0, 2, 1)
    dn1 = np.concatenate([f["L1_ffn_experts_down"], sd.reshape(P, 2, I1).transpose(1, 0, 2)])
    dn1 = dn1.transpose(0, 2, 1).reshape(E1, 2, IC1, P).transpose(0, 2, 1, 3)
    dn0 = np.concatenate([f["L0_ffn_shared_down"], f["L0_ffn_routed_down"]])
    a = dict(
        x=f["L0_attn_hidden"][0],
        ident=np.eye(P, dtype=np.float32),
        tri=(q[:, :P] >= k).astype(np.float32), band=((q >= k) & (q - k < WIN)).astype(np.float32),
        cosT=cos, sinT=sin,
        normw=np.stack([f["L0_attn_norm1_w"], f["L0_attn_norm2_w"]], axis=1),
        kvdT=f["L0_attn_g_kv_down"].T, kvup=np.concatenate([f["L0_attn_g_k_up"], f["L0_attn_g_v_up"]], axis=1),
        g_wq=f["L0_attn_g_wq"],
        l_wqkv=np.concatenate([f["L0_attn_l_wq"], f["L0_attn_l_wk"], f["L0_attn_l_wv"]], axis=1),
        wo=np.stack([f["L0_attn_g_wo"], f["L0_attn_l_wo"]], axis=1),
        router0=f["L0_ffn_router_w"],
        router1=np.concatenate([f["L1_ffn_gate_w"], f["L1_ffn_shared_expert_gate_w"]]).T,
        lrV=np.stack([blocks(f[L + "V" + m]) for m in "qkv"], axis=1),
        lrU=np.stack([blocks(f[L + "U" + m].transpose(0, 2, 1)) for m in "qkv"], axis=1),
        bias1=np.broadcast_to(np.concatenate([f[L + "b" + m].reshape(-1) for m in "qkv"]), (P, 3 * P)),
        up0=np.concatenate([f["L0_ffn_shared_up"], f["L0_ffn_routed_up"]]),
        dn0=dn0.reshape(E0 + 1, FC0, P, P).transpose(0, 2, 1, 3),
        up1=up1, dn1=dn1,
    )
    return {k: np.ascontiguousarray(v) for k, v in a.items()}


class Arrays:

    def __init__(self, a):
        self.band, self.bias1, self.cosT, self.dn0, self.dn1, self.g_wq = (a[x] for x in ("band", "bias1", "cosT", "dn0", "dn1", "g_wq"))
        self.ident, self.kvdT, self.kvup, self.l_wqkv, self.lrU, self.lrV = (a[x] for x in ("ident", "kvdT", "kvup", "l_wqkv", "lrU", "lrV"))
        self.normw, self.router0, self.router1, self.sinT, self.tri, self.up0 = (a[x] for x in ("normw", "router0", "router1", "sinT", "tri", "up0"))
        self.up1, self.wo, self.x = (a[x] for x in ("up1", "wo", "x"))


def kernel(**inputs):
    import concourse.bacc as bacc
    from concourse.bass_utils import run_bass_kernel_spmd

    arrays = {f"in_{k}": v for k, v in _arrays(inputs).items()}
    nc = bacc.Bacc("TRN2", target_bir_lowering=False, num_devices=1)
    A = Arrays({name[3:]: nc.dram_tensor(name, a.shape, mybir.dt.from_np(a.dtype), kind="ExternalInput").ap()
                for name, a in arrays.items()})
    A.out = nc.dram_tensor("out_x", (T, P), mybir.dt.float32, kind="ExternalOutput").ap()
    build(nc, A)
    r = run_bass_kernel_spmd(nc, [arrays], core_ids=[0])
    return r.results[0]["out_x"].reshape(1, T, P)
```

```python
from contextlib import ExitStack

import concourse.bass as bass
from concourse import mybir

P = 128
T = 2048
GT = 512
TPG = GT // P
NG = T // GT
NT = T // P
HQ, HKV, HD = 16, 4, 8
HQK = HQ + HKV
H1, HD1 = 8, 16
WIN = 32
LW = P + WIN
NQK = HQK * HD
NQKV = NQK + HKV * HD
KS0 = 9 * HD
KS1 = 6 * HD1
KM1 = KS1 + 2
F0, FC0 = 512, 4
E0 = 8
I1 = 176
IR1 = I1 - P
UP_AT = 64
E1 = 10
LN_EPS, RMS_EPS = 1e-5, 1e-6
MASKED = -2.0 ** 15
PRODUCTS1 = ((0, 0), (0, 1), (0, 2), (1, 0), (1, 1), (2, 0))
VW = HD1 + 1


class Chain:

    def __init__(self, eng, sem, start=0):
        self.eng, self.sem, self.start, self.k = eng, sem, start, 0

    def __call__(self, ins):
        ins.then_inc(self.sem, 1)
        self.k += 1
        self.eng.wait_ge(self.sem, self.start + self.k)


def round_of(r):
    return (r if r < NG else None), (r - 1 if r else None)


def over_rounds(eng, step, peeled):
    step(0, None)
    for r in range(1, peeled):
        step(r, r - 1)
    with eng.Fori(peeled, NG) as r:
        step(r, r - 1)
    step(None, NG - 1)


def wait_past(eng, sem, n):
    if not (isinstance(n, int) and n == 0):
        eng.wait_ge(sem, n)


class PrepSems:

    def __init__(self, sem, prefix):
        self.cen = sem(prefix + "_cen")
        self.sq = sem(prefix + "_sq")
        self.var = sem(prefix + "_var")
        self.std = sem(prefix + "_std")
        self.xn = sem(prefix + "_xn")
        self.st = sem(prefix + "_st")
        self.xnT = sem(prefix + "_xnT")
        self.xnTc = sem(prefix + "_xnTc")
        self.lg = sem(prefix + "_lg")
        self.lgc = sem(prefix + "_lgc")
        self.sq2 = sem(prefix + "_sq2")
        self.var2 = sem(prefix + "_var2")
        self.std2 = sem(prefix + "_std2")
        self.y = sem(prefix + "_y")
        self.yT = sem(prefix + "_yT")
        self.yTc = sem(prefix + "_yTc")
        self.qkv = sem(prefix + "_qkv")
        self.qkvc = sem(prefix + "_qkvc")
        self.vc = sem(prefix + "_vc")
        self.ro = sem(prefix + "_ro")
        self.sq3 = sem(prefix + "_sq3")
        self.var3 = sem(prefix + "_var3")
        self.std3 = sem(prefix + "_std3")
        self.rn = sem(prefix + "_rn")
        self.h = sem(prefix + "_h")
        self.r1 = sem(prefix + "_r1")
        self.m = sem(prefix + "_m")
        self.l = sem(prefix + "_l")
        self.kp = sem(prefix + "_kp")
        self.pT = sem(prefix + "_pT")
        self.pTc = sem(prefix + "_pTc")
        self.scr = sem(prefix + "_scr")
        self.stk = sem(prefix + "_stk")
        self.dch = sem(prefix + "_dch")
        self.ost = sem(prefix + "_ost")
        self.oT = sem(prefix + "_oT")
        self.oTc = sem(prefix + "_oTc")
        self.op = sem(prefix + "_op")
        self.ores = sem(prefix + "_ores")


class AttSems:

    def __init__(self, sem, prefix):
        self.vst = sem(prefix + "_vst")
        self.score = sem(prefix + "_score")
        self.prob = sem(prefix + "_prob")
        self.pv = sem(prefix + "_pv")
        self.oT = sem(prefix + "_oT")
        self.fin = sem(prefix + "_fin")
        self.och = sem(prefix + "_och")
        self.o = sem(prefix + "_o")


class MaxSems:

    def __init__(self, sem, prefix):
        self.mx = sem(prefix + "_mx")
        self.mxr = sem(prefix + "_mxr")
        self.mn = sem(prefix + "_mn")
        self.mnT = sem(prefix + "_mnT")
        self.mnTc = sem(prefix + "_mnTc")
        self.row = sem(prefix + "_row")


class MoeSems:

    def __init__(self, sem, prefix):
        self.up = sem(prefix + "_up")
        self.act = sem(prefix + "_act")
        self.hid = sem(prefix + "_hid")
        self.dn = sem(prefix + "_dn")
        self.acc = sem(prefix + "_acc")


class RouteSems:

    def __init__(self, sem, prefix):
        self.ch = sem(prefix + "_ch")
        self.ready = sem(prefix + "_ready")
        self.ex = sem(prefix + "_ex")


def build(nc, A):
    F32, BF = mybir.dt.float32, mybir.dt.bfloat16
    ALU, ACT, AX = mybir.AluOpType, mybir.ActivationFunctionType, mybir.AxisListType
    ds = bass.ds
    V, S_, PE_, G_ = nc.vector, nc.scalar, nc.tensor, nc.gpsimd
    ctx = ExitStack()
    with ctx:
        def sb(name, shape, dt=F32):
            return ctx.enter_context(nc.sbuf_tensor("sb_" + name, shape, dt))

        def sem(name):
            return ctx.enter_context(nc.semaphore(name))

        x_all = sb("x_all", [P, NT, P])
        xnT_all = sb("xnT_all", [P, T])
        s_all = sb("s_all", [P, NT, P])
        o_all = sb("o_all", [P, NT, P])
        acc = sb("acc", [P, NT, P])
        v_all = sb("v_all", [P, NT, 8, VW])
        stack = sb("stack", [P, HQK, T], BF)
        ring = sb("ring", [P, 4, 2 * GT])
        gates = sb("gates", [P, NT, E1])
        ident = sb("ident", [P, P])
        identb = sb("identb", [P, P], BF)
        tri = sb("tri", [P, P], BF)
        band = sb("band", [P, LW], BF)
        cosT = sb("cosT", [P, 2, NT, HD])
        sinT = sb("sinT", [P, 2, NT, HD])
        normw = sb("normw", [P, 2])
        kvdT = sb("kvdT", [32, P])
        kvup = sb("kvup", [32, 2 * HKV * HD])
        wqkv = sb("wqkv", [P, 2, NQKV])
        wo = sb("wo", [P, 2, P])
        rw0 = sb("rw0", [P, E0])
        rw1 = sb("rw1", [P, E0 + 1])
        wl1 = sb("wl1", [P, 3 * P])
        bias1 = sb("bias1", [P, 3 * P])
        wup = sb("wup", [P, 2, F0])
        wdn = sb("wdn", [P, 2, FC0, P])
        vst = sb("vst", [P, 2, 4, 32])
        oT = sb("oT", [P, 2, GT])
        sq = sb("sq", [P, TPG, NQK])
        st4 = sb("st4", [P, 4, TPG])
        xn_st = sb("xn_st", [P, TPG, P])
        aT_st = sb("aT_st", [P, GT])
        yT_st = sb("yT_st", [P, GT])
        qkv_st = sb("qkv_st", [P, TPG, 3 * P])
        y_st = qkv_st[:, :, 2 * P:3 * P]
        rr = sb("rr", [P, 2 * TPG * NQK])
        ro = rr[:, 0:TPG * NQK].rearrange("p (t n) -> p t n", t=TPG)
        rt = rr[:, TPG * NQK:].rearrange("p (t n) -> p t n", t=TPG)
        cen = ring[:, 2, 0:GT].rearrange("p (t n) -> p t n", t=TPG)
        sq_ln = ring[:, 2, GT:2 * GT].rearrange("p (t n) -> p t n", t=TPG)
        res1 = rr[:, 0:TPG * 2 * P].rearrange("p (t n) -> p t n", t=TPG)
        st80 = sb("st80", [P, 3, TPG * HQK])
        parts = sb("parts", [P, TPG, 6, P], BF)
        parts0 = parts[:, :, :, :].rearrange("p t a n -> p t (a n)")[:, :, 0:3 * NQK]\
            .rearrange("p t (a n) -> p t a n", a=3)
        parts1 = parts[:, :, :, :].rearrange("p t (a q) n -> p t a (q n)", q=2)
        kparts = sb("kparts", [P, TPG, 3 * 32], BF)
        pT = sb("pT", [P, 6, GT], BF)
        rden = sb("rden", [P, TPG, 4])
        lg = sb("lg", [P, NT, E0 + 1])
        rs = sb("rs", [P, 4, NT])
        top = sb("top", [P, NT, 8])
        pr = sb("pr", [P, NT, 8])
        mxp = sb("mxp", [P, 2, 16, 4])
        mneg = sb("mneg", [P, 2, 16])
        mparts = sb("mparts", [P, 2, 16], BF)
        mT = sb("mT", [32, P], BF)
        zerob = sb("zerob", [P, GT], BF)

        ps = ctx.enter_context(nc.psum_tensor("ps", [P, 8, 512], F32))
        ps_bf = ps[:, :, :].rearrange("p b n -> p (b n)").bitcast(BF)
        scr = nc.dram_tensor("parts_dram", (3, NG, P, 6, GT), BF, kind="Internal").ap()

        q0s, k0s = stack[:, 0:HQ, :], stack[:, HQ:HQK, :]
        q1s, k1s = stack[:, 0:H1, :], stack[:, H1:2 * H1, :]
        lrV = ring[:, 0, 0:3 * 2 * P].rearrange("p (m c n) -> p m c n", m=3, c=2)
        tri_in, band_in = ring[:, 3, 0:P], ring[:, 3, P:P + LW]
        lrU = ring[:, 1, 0:3 * 2 * P].rearrange("p (m c n) -> p m c n", m=3, c=2)

        s_x0, s_x = sem("s_x0"), sem("s_x")
        s_first, s_const = sem("s_first"), sem("s_const")
        s_identb = sem("s_identb")
        s_fold, s_foldc = sem("s_fold"), sem("s_foldc")
        s_vones = sem("s_vones")
        AG, AL, AB = AttSems(sem, "ag"), AttSems(sem, "al"), AttSems(sem, "ab")
        MX = MaxSems(sem, "mx")
        M0, M1 = MoeSems(sem, "m0"), MoeSems(sem, "m1")
        w0, w1 = [sem("w0_0"), sem("w0_1")], [sem("w1_0"), sem("w1_1")]
        s_stk1 = sem("s_stk1")
        s_zero = sem("s_zero")
        R0, R1 = RouteSems(sem, "r0"), RouteSems(sem, "r1")
        s_cleared = sem("s_cleared")
        s_silu = sem("s_silu")
        s_prod, s_y = sem("s_prod"), sem("s_y")
        s_out = sem("s_out")

        block = ctx.enter_context(nc.Block())

        first = [(ident[:, :], A.ident), (kvdT[:, :], A.kvdT), (kvup[:, :], A.kvup),
                 (wqkv[:, 0, 0:P], A.g_wq), (normw[:, :], A.normw), (rw0[:, :], A.router0)]
        consts = [(cosT[:, :, :, :], A.cosT), (sinT[:, :, :, :], A.sinT), (tri_in, A.tri), (band_in, A.band),
                  (lrV, A.lrV), (lrU, A.lrU), (wqkv[:, 1, :], A.l_wqkv), (wo[:, :, :], A.wo),
                  (rw1[:, :], A.router1), (bias1[:, :], A.bias1)]
        ALL_FIRST, ALL_CONST = 16 * len(first), 16 * len(consts)

        def grp(buf, it):
            return buf[:, ds(TPG * it, TPG), :]

        def cols(it):
            return ds(GT * it, GT)

        S = PrepSems(sem, "p")
        STAT4 = (st4[:, 0, :], st4[:, 1, :], st4[:, 2, :])
        STAT80 = (st80[:, 0, :], st80[:, 1, :], st80[:, 2, :])
        KF0, KB0 = (6, 2), 5
        KF1 = 6
        BP0 = 3 * 1024

        def heads(x):
            return x.rearrange("p t (h d) -> p t h d", d=HD)

        def flat_heads(x):
            return x.rearrange("p t (h d) -> p (t h) d", d=HD)

        def over(stat, n):
            return stat.unsqueeze(2).broadcast_to([P, stat.shape[1], n])

        def mean_square(link, src, stat, inv_n, eps, done):
            link(V.tensor_reduce(stat[0], src, AX.X, ALU.add))
            V.tensor_scalar(stat[1], stat[0], inv_n, eps, ALU.mult, ALU.add).then_inc(done, 1)

        def act_root(stat, done):
            S_.activation(stat[2], stat[1], ACT.Sqrt).then_inc(done, 1)

        def dve_centre(dve, link, src, keep=None):
            last = V.tensor_reduce(st4[:, 0, :], src, AX.X, ALU.add)
            if keep is not None:
                last = V.tensor_copy(keep, src)
            link(last)
            link(V.tensor_scalar(st4[:, 1, :], st4[:, 0, :], -1.0 / P, None, ALU.mult))
            V.tensor_tensor(cen, src, over(st4[:, 1, :], P), ALU.add).then_inc(S.cen, 1)

        def dve_xn(dve, link, n):
            dve.wait_ge(S.std, n + 1)
            link(V.reciprocal(st4[:, 0, :], st4[:, 2, :]))
            wait_past(dve, S.xnT, n)
            V.tensor_tensor(xn_st[:, :, :], cen, over(st4[:, 0, :], P), ALU.mult).then_inc(S.xn, 1)

        def pe_transpose(src, bank, done):
            for t in range(TPG):
                last = PE_.transpose(ps[:, bank, t * P:(t + 1) * P], src[:, t, :], ident[:, :])
            last.then_inc(done, 1)

        def dve_prep0(dve, f, b, layer, beside=None):
            link = Chain(dve, S.dch, (NG * (KF0[0] + KB0) if layer else 0)
                         + (NG if f is None else f) * KF0[layer] + (0 if b is None else b) * KB0)
            nf, nb = (None if x is None else layer * NG + x for x in (f, b))
            if b is not None:
                dve.wait_ge(S.qkvc, 2 * nb + 2)
                full, half = [P, TPG, HQK, HD], [P, TPG, HQK, HD // 2]
                x, w = heads(qkv_st[:, :, 0:NQK]), heads(rt)
                cs = cosT[:, layer, ds(TPG * b, TPG), :].unsqueeze(2)
                sn = sinT[:, layer, ds(TPG * b, TPG), :].unsqueeze(2)
                V.tensor_tensor(heads(ro), x, cs.broadcast_to(full), ALU.mult).then_inc(S.dch, 1)
                V.tensor_tensor(w[:, :, :, 0:HD:2], x[:, :, :, 1:HD:2], sn[:, :, :, 0:HD:2].broadcast_to(half),
                                ALU.mult).then_inc(S.dch, 1)
                link.k += 2
                link(V.tensor_tensor(w[:, :, :, 1:HD:2], x[:, :, :, 0:HD:2],
                                     sn[:, :, :, 1:HD:2].broadcast_to(half), ALU.mult))
                V.tensor_tensor(ro, ro, rt, ALU.add).then_inc(S.ro, 1)
            if f is not None and layer == 0:
                dve_centre(dve, link, grp(x_all, f))
            if b is not None:
                dve.wait_ge(S.sq3, nb + 1)
                mean_square(link, flat_heads(sq[:, :, :]), STAT80, 1.0 / HD, RMS_EPS, S.var3)
            if beside:
                beside(0)
            if f is not None and layer == 0:
                dve.wait_ge(S.sq, nf + 1)
                mean_square(link, sq_ln, STAT4, 1.0 / P, LN_EPS, S.var)
            if b is not None:
                dve.wait_ge(S.std3, nb + 1)
                link(V.reciprocal(st80[:, 0, :], st80[:, 2, :]))
                V.tensor_tensor(flat_heads(rt), flat_heads(ro), over(st80[:, 0, :], HD), ALU.mult).then_inc(S.rn, 1)
            if f is not None and layer == 0:
                wait_past(dve, S.st, nf)
                dve_xn(dve, link, nf)
            if f is not None and layer == 1:
                dve_oproj(dve, nf - NG, f, 0, grp(s_all, f))
            if b is not None:
                dve.wait_ge(S.h, nb + 1)
                dve.wait_ge(S.rn, nb + 1)
                V.tensor_tensor(ro, rt, parts0[:, :, 0, :], ALU.subtract).then_inc(S.r1, 1)
            if f is not None:
                dve.wait_ge(S.sq2, nf + 1)
                mean_square(link, xn_st[:, :, :] if layer else sq_ln, STAT4, 1.0 / P, RMS_EPS, S.var2)
            if beside:
                beside(1)
            if b is not None:
                dve.wait_ge(S.m, nb + 1)
                dve.wait_ge(S.r1, nb + 1)
                V.tensor_tensor(parts0[:, :, 2, :], ro, parts0[:, :, 1, :], ALU.subtract).then_inc(S.l, 1)
                dve.wait_ge(S.l, nb + 1)
                V.tensor_copy(kparts[:, :, :].rearrange("p t (a n) -> p t a n", a=3),
                              parts0[:, :, :, HQ * HD:NQK]).then_inc(S.kp, 1)
            if f is not None:
                dve.wait_ge(S.std2, nf + 1)
                link(V.reciprocal(st4[:, 0, :], st4[:, 2, :]))
                V.tensor_tensor(y_st, grp(s_all, f) if layer else xn_st[:, :, :], over(st4[:, 0, :], P),
                                ALU.mult).then_inc(S.y, 1)
            if beside:
                beside(2)
            assert link.k == (0 if f is None else KF0[layer]) + (0 if b is None else KB0)

        def act_prep0(act, f, b, layer, beside=None):
            nf, nb = (None if x is None else layer * NG + x for x in (f, b))
            if f is not None and layer == 1:
                if f:
                    act.wait_ge(S.var2, nf)
                act_ost(act, nf - NG, f, AG.o, N_UNITS)
            if beside:
                beside(0)
            if b is not None:
                act.wait_ge(S.ro, nb + 1)
                S_.activation(sq[:, :, :], ro, ACT.Square).then_inc(S.sq3, 1)
            if f is not None and layer == 1:
                act_oT(act, nf - NG)
            if f is not None and layer == 0:
                act.wait_ge(S.cen, nf + 1)
                S_.activation(sq_ln, cen, ACT.Square).then_inc(S.sq, 1)
            if beside:
                beside(1)
            if b is not None:
                act.wait_ge(S.var3, nb + 1)
                act_root(STAT80, S.std3)
            if f is not None and layer == 0:
                act.wait_ge(S.var, nf + 1)
                act_root(STAT4, S.std)
            if b is not None:
                act.wait_ge(S.rn, nb + 1)
                wait_past(act, S.pT, nb)
                S_.activation(parts0[:, :, 0, :], rt, ACT.Copy).then_inc(S.h, 1)
            if beside:
                beside(2)
            if f is not None and layer == 1:
                act.wait_ge(S.ores, nf - NG + 1)
                S_.activation(xn_st[:, :, :], grp(s_all, f), ACT.Square).then_inc(S.sq2, 1)
            if f is not None and layer == 0:
                act.wait_ge(S.xn, nf + 1)
                S_.activation(sq_ln, xn_st[:, :, :], ACT.Square).then_inc(S.sq2, 1)
                S_.activation(grp(s_all, f), xn_st[:, :, :], ACT.Copy)
                S_.activation(grp(acc, f), xn_st[:, :, :], ACT.Copy).then_inc(S.st, 1)
            if b is not None:
                act.wait_ge(S.r1, nb + 1)
                S_.activation(parts0[:, :, 1, :], ro, ACT.Copy).then_inc(S.m, 1)
            if beside:
                beside(3)
            if f is not None:
                act.wait_ge(S.var2, nf + 1)
                act_root(STAT4, S.std2)
            if f is not None and layer == 0:
                act_xnT(act, nf, f)
            if b is not None:
                act.wait_ge(S.pT, nb + 1)
                wait_past(act, S.scr, 32 * nb)
                S_.activation(pT[:, 0:3, :].rearrange("p a n -> p (a n)"), ps_bf[:, BP0:BP0 + 3 * GT],
                              ACT.Copy).then_inc(S.pTc, 1)
                S_.activation(pT[0:96, 3, :], ps_bf[0:96, BP0 + 3 * GT:BP0 + 4 * GT], ACT.Copy).then_inc(S.pTc, 1)
            if beside:
                beside(4)
            if f is not None:
                act.wait_ge(S.yT, nf + 1)
                S_.activation(yT_st[:, :], ps[:, 0, :], ACT.Copy, scale=normw[:, layer:layer + 1]).then_inc(S.yTc, 1)
                act.wait_ge(S.qkv, nf + 1)
                wait_past(act, S.ro, nf)
                for k in range(2):
                    S_.activation(qkv_st[:, 2 * k:2 * k + 2, 0:NQKV],
                                  ps[:, 1 + k, 0:2 * NQKV].rearrange("p (t n) -> p t n", t=2),
                                  ACT.Copy).then_inc(S.qkvc, 1)
                act.wait_ge(S.qkvc, 2 * nf + 2)
                S_.activation(v_all[:, ds(TPG * f, TPG), 0:HKV, 0:HD],
                              qkv_st[:, :, NQK:NQKV].rearrange("p t (h d) -> p t h d", d=HD),
                              ACT.Copy).then_inc(S.vc, 1)
            if f is not None and layer == 0:
                act.wait_ge(S.lg, nf + 1)
                S_.activation(lg[:, ds(TPG * f, TPG), 0:E0],
                              ps[:, 1, 2 * NQKV:2 * NQKV + TPG * E0].rearrange("p (t e) -> p t e", t=TPG),
                              ACT.Copy).then_inc(S.lgc, 1)
            if beside:
                beside(5)

        def act_xnT(act, n, f):
            act.wait_ge(S.xnT, n + 1)
            S_.activation(aT_st[:, :], ps[:, 0, :], ACT.Copy).then_inc(S.xnTc, 1)
            act.wait_ge(S.xnTc, 2 * n + 1)
            S_.activation(xnT_all[:, cols(f)], aT_st[:, :], ACT.Copy).then_inc(S.xnTc, 1)

        def pe_prep0(pe, f, b, layer, beside=None):
            def also(k):
                if beside:
                    beside(k)
            nf, nb = (None if x is None else layer * NG + x for x in (f, b))
            also(0)
            if f is not None:
                wait_past(pe, S.yTc, nf)
            if f is not None and layer == 1:
                pe_oT(pe, nf - NG)
            if f is not None and layer == 0:
                pe.wait_ge(S.xn, nf + 1)
                pe_transpose(xn_st, 0, S.xnT)
            also(1)
            if f is not None and layer == 1:
                pe_oproj(pe, nf - NG, 0, 0)
            also(2)
            also(3)
            if b is not None:
                pe.wait_ge(S.kp, nb + 1)
                wait_past(pe, S.pTc, 2 * nb)
                for a in range(3):
                    for t in range(TPG):
                        at = BP0 + a * GT + t * P
                        PE_.transpose(ps_bf[:, at:at + P], parts0[:, t, a, 0:P], identb[:, :])
                for t in range(TPG):
                    at = BP0 + 3 * GT + t * P
                    last = PE_.transpose(ps_bf[0:96, at:at + P], kparts[:, t, :], identb[:, :])
                last.then_inc(S.pT, 1)
            also(4)
            if f is not None:
                pe.wait_ge(S.y, nf + 1)
                if layer == 0:
                    pe.wait_ge(S.xnTc, 2 * nf + 1)
                pe_transpose(y_st, 0, S.yT)
                wait_past(pe, S.qkvc, 2 * nf)
            if f is not None and layer == 0:
                pe.wait_ge(S.xnTc, 2 * nf + 2)
                wait_past(pe, S.lgc, nf)
                for t in range(TPG):
                    at = 2 * NQKV + t * E0
                    last = PE_.matmul(ps[:, 1, at:at + E0], aT_st[:, t * P:(t + 1) * P], rw0[:, :],
                                      start=True, stop=True)
                last.then_inc(S.lg, 1)
            if f is not None:
                pe.wait_ge(S.yTc, nf + 1)
                for t in range(TPG):
                    last = PE_.matmul(ps[:, 1 + t // 2, (t % 2) * NQKV:(t % 2 + 1) * NQKV],
                                      yT_st[:, t * P:(t + 1) * P], wqkv[:, layer, :], start=True, stop=True)
                last.then_inc(S.qkv, 1)
            also(5)

        def sp_stack0(sp, n, it, layer, used, total):
            if used is not None:
                sp.wait_ge(used, total)
            sp.wait_ge(S.pTc, 2 * n + 2)
            sp.dma_start(scr[layer, ds(it, 1), :, 0:3, :].rearrange("o p a t -> p (o a) t"),
                         pT[:, 0:3, :]).then_inc(S.scr, 16)
            sp.dma_start(scr[layer, ds(it, 1), 0:96, 3:4, :].rearrange("o p a t -> p (o a) t"),
                         pT[0:96, 3:4, :]).then_inc(S.scr, 16)
            sp.wait_ge(S.scr, 32 * n + 32)
            for a in range(3):
                for b in range(3):
                    r = (3 * a + b) * HD
                    sp.dma_start(q0s[r:r + HD, :, cols(it)],
                                 scr[layer, ds(it, 1), :, a, :].rearrange("o (h d) t -> d (o h) t", d=HD)
                                 ).then_inc(S.stk, 16)
                    sp.dma_start(k0s[r:r + HD, :, cols(it)],
                                 scr[layer, ds(it, 1), 32 * b:32 * b + 32, 3, :].rearrange(
                                     "o (h d) t -> d (o h) t", d=HD)).then_inc(S.stk, 16)

        STK0 = 18 * 16


        def sets0(g):
            return TPG * (g + 1)

        BASE_SET = [0]
        for g in range(NG):
            BASE_SET.append(BASE_SET[-1] + HKV * sets0(g))

        def att0_score(pe, n, g, kv, kb, q0, diag, first=False):
            w = GT - q0
            for u in range(2):
                if not first:
                    pe.wait_ge(AG.prob, 2 * n + u - 1)
                for j in range(2):
                    h = 4 * kv + 2 * u + j
                    last = PE_.matmul(ps[:, 2 * u + j, 0:w], k0s[0:KS0, kv, bass.ts(kb, P)],
                                      q0s[0:KS0, h, g * GT + q0:(g + 1) * GT], start=True, stop=not diag)
                    if diag:
                        last = PE_.matmul(ps[:, 2 * u + j, 0:P], identb[:, :], tri[:, :], start=False, stop=True)
                last.then_inc(AG.score, 1)

        def att0_pv(pe, n, par, bank, q0, first, last_set):
            w = GT - q0
            pe.wait_ge(AG.vst, n + 1)
            pe.wait_ge(AG.prob, 2 * n + 2)
            for h in range(4):
                last = PE_.matmul(ps[32 * h:32 * h + 32, bank, q0:GT], vst[:, par, 0, :],
                                  ring[:, 2 * par + h // 2, (h % 2) * w:(h % 2) * w + w],
                                  start=first, stop=last_set, skip_group_check=True)
            last.then_inc(AG.pv, 1)

        def plan0():
            for g in range(NG):
                for kv in range(HKV):
                    yield HKV * g + kv, g, kv, BASE_SET[g] + kv * sets0(g)

        def fin_transposes(pe, A_, c, bank):
            pe.wait_ge(A_.oT, c + 1)
            if c >= 1:
                pe.wait_ge(A_.o, c)
            for t in range(TPG):
                last = PE_.transpose(ps[:, bank, t * P:(t + 1) * P], oT[:, c % 2, t * P:(t + 1) * P], ident[:, :])
            last.then_inc(A_.fin, 1)

        def dve_out(dve, A_, c, bank, pv_done):
            dve.wait_ge(A_.pv, pv_done)
            if c >= 2:
                dve.wait_ge(A_.fin, c - 1)
            V.tensor_copy(oT[:, c % 2, :], ps[:, bank, :]).then_inc(A_.oT, 1)

        def dve_normalise(dve, A_, c, bank, g, col, hd):
            dve.wait_ge(A_.fin, c + 1)
            src = ps[:, bank, :].rearrange("p (t h d) -> p t h d", t=TPG, h=4)
            if c:
                dve.wait_ge(A_.o, c)
            V.reciprocal(rden[:, :, :], src[:, :, :, hd]).then_inc(A_.och, 1)
            dve.wait_ge(A_.och, c + 1)
            V.tensor_tensor(
                o_all[:, TPG * g:TPG * (g + 1), col:col + 4 * hd].rearrange("p t (h d) -> p t h d", h=4),
                src[:, :, :, 0:hd], rden[:, :, :].unsqueeze(3).broadcast_to([P, TPG, 4, hd]),
                ALU.mult).then_inc(A_.o, 1)

        N_SETS = BASE_SET[NG]
        N_UNITS = HKV * NG

        def act_ost(act, n, it, done, last):
            act.wait_ge(done, last)
            wait_past(act, S.oT, n)
            S_.activation(xn_st[:, :, :], grp(o_all, it), ACT.Copy).then_inc(S.ost, 1)

        def act_oT(act, n, bank=0):
            act.wait_ge(S.oT, n + 1)
            S_.activation(aT_st[:, :], ps[:, bank, :], ACT.Copy).then_inc(S.oTc, 1)

        def pe_oT(pe, n, bank=0):
            pe.wait_ge(S.ost, n + 1)
            pe_transpose(xn_st, bank, S.oT)

        def pe_oproj(pe, n, layer, bank):
            pe.wait_ge(S.oTc, n + 1)
            wait_past(pe, S.ores, n)
            for t in range(TPG):
                last = PE_.matmul(ps[:, bank, t * P:(t + 1) * P], aT_st[:, t * P:(t + 1) * P], wo[:, layer, :],
                                  start=True, stop=True)
            last.then_inc(S.op, 1)

        def dve_oproj(dve, n, it, bank, out):
            dve.wait_ge(S.op, n + 1)
            V.tensor_tensor(out, ps[:, bank, :].rearrange("p (t n) -> p t n", t=TPG), grp(s_all, it),
                            ALU.add).then_inc(S.ores, 1)

        def loc_score(pe, t, kv, w, first):
            n = 4 * t + kv
            if not first:
                pe.wait_ge(AL.prob, n - 1)
            for h in range(4):
                last = PE_.matmul(ps[:, 2 * (kv % 2) + h // 2, (h % 2) * w:(h % 2) * w + w],
                                  k0s[0:KS0, kv, ds(P * t, P)], q0s[0:KS0, 4 * kv + h, ds(P * t, w)],
                                  start=True, stop=False, skip_group_check=True)
                last = PE_.matmul(ps[:, 2 * (kv % 2) + h // 2, (h % 2) * w:(h % 2) * w + w],
                                  identb[:, :], band[:, 0:w], start=False, stop=True, skip_group_check=True)
            last.then_inc(AL.score, 1)

        def loc_exp(act, t, kv, w, late):
            n = 4 * t + kv
            act.wait_ge(AL.score, n + 1)
            if late:
                act.wait_ge(AL.pv, n - 3)
            b = 2 * (kv % 2)
            S_.activation(ring[:, kv, 0:4 * w].rearrange("p (b q) -> p b q", b=2), ps[:, b:b + 2, 0:2 * w],
                          ACT.Exp, scale=float(HD) ** -0.5).then_inc(AL.prob, 1)

        def loc_pv(pe, t, par, kv, w, tile0):
            pe.wait_ge(AL.prob, 4 * t + kv + 1)
            if kv == 0:
                pe.wait_ge(AL.vst, t + 1)
            for h in range(4):
                last = PE_.matmul(ps[32 * h:32 * h + 32, 4 + par, kv * P:(kv + 1) * P], vst[:, par, kv, :],
                                  ring[:, kv, h * w:h * w + P], start=(tile0 and kv == 0), stop=True,
                                  skip_group_check=True)
            if w > P:
                if kv == 0 and not tile0:
                    pe.wait_ge(AL.oT, t)
                for h in range(4):
                    last = PE_.matmul(ps[32 * h:32 * h + 32, 5 - par, kv * P:kv * P + WIN], vst[:, par, kv, :],
                                      ring[:, kv, h * w + P:h * w + w], start=(kv == 0), stop=True,
                                      skip_group_check=True)
            last.then_inc(AL.pv, 1)

        def loc_fin(pe, t, par):
            pe.wait_ge(AL.oT, t + 1)
            wait_past(pe, AL.o, t)
            for kv in range(HKV):
                last = PE_.transpose(ps[:, 6, kv * P:(kv + 1) * P], oT[:, par, kv * P:(kv + 1) * P], ident[:, :])
            last.then_inc(AL.fin, 1)

        def loc_out(act, t, par):
            act.wait_ge(AL.pv, 4 * t + 4)
            if not (isinstance(t, int) and t == 0):
                act.wait_ge(AL.fin, t - 1)
            S_.activation(oT[:, par, :], ps[:, 4 + par, :], ACT.Copy).then_inc(AL.oT, 1)

        def loc_normalise(dve, t):
            dve.wait_ge(AL.fin, t + 1)
            src = ps[:, 6, :].rearrange("p (h d) -> p h d", d=32)
            r = rden[:, :, :].rearrange("p a b -> p (a b)")
            wait_past(dve, AL.o, t)
            V.reciprocal(r, src[:, :, HD]).then_inc(AL.och, 1)
            dve.wait_ge(AL.och, t + 1)
            V.tensor_tensor(o_all[:, ds(t, 1), :].rearrange("p o (h d) -> p (o h) d", d=HD), src[:, :, 0:HD],
                            over(r, HD), ALU.mult).then_inc(AL.o, 1)

        def loc_loop(eng, step):
            step(0, 0, True, False)
            step(1, 1, False, False)
            with eng.Fori(1, NT // 2 - 1) as i:
                step(2 * i, 0, False, False)
                step(2 * i + 1, 1, False, False)
            step(NT - 2, 0, False, False)
            step(NT - 1, 1, False, True)

        def route_dve(dve, R, sig):
            link = Chain(dve, R.ch)
            x = lg[:, :, 0:E0]
            link(V.tensor_reduce(rs[:, 0, :], x, AX.X, ALU.max))
            link(V.tensor_tensor(x, x, over(rs[:, 0, :], E0), ALU.subtract))
            V.nop().then_inc(R.ready, 1)
            dve.wait_ge(R.ex, 1)
            link(V.tensor_reduce(rs[:, 1, :], x, AX.X, ALU.add))
            link(V.reciprocal(rs[:, 2, :], rs[:, 1, :]))
            link(V.tensor_tensor(x, x, over(rs[:, 2, :], E0), ALU.mult))
            for t in range(NT):
                V.max(top[:, t, :], lg[:, t, 0:E0]).then_inc(R.ch, 1)
            link.k += NT
            dve.wait_ge(R.ch, link.k)
            link(V.memset(top[:, :, 2:8], -1.0))
            for t in range(NT):
                V.match_replace(pr[:, t, :], top[:, t, :], lg[:, t, 0:E0], 0.0).then_inc(R.ch, 1)
            link.k += NT
            dve.wait_ge(R.ch, link.k)
            link(V.tensor_tensor(gates[:, :, 0:E0], x, pr[:, :, :], ALU.subtract))
            if sig:
                link(V.tensor_scalar(rs[:, 3, :], lg[:, :, E0], 1.0, None, ALU.add))
                link(V.reciprocal(gates[:, :, E0], rs[:, 3, :]))
                link(V.tensor_copy(gates[:, :, E0 + 1], gates[:, :, E0]))
            V.nop().then_inc(R.ready, 1)

        def route_act(act, R, sig):
            act.wait_ge(R.ready, 1)
            last = S_.activation(lg[:, :, 0:E0], lg[:, :, 0:E0], ACT.Exp)
            if sig:
                last = S_.activation(lg[:, :, E0], lg[:, :, E0], ACT.Exp, scale=-1.0)
            last.then_inc(R.ex, 1)

        def moe_down(pe, M, n, par, k, lhs, slot, first, midway=None):
            pe.wait_ge(M.hid, 2 * n + 2)
            if not first:
                pe.wait_ge(M.acc, n - 1)
            for t in range(TPG):
                for c in range(len(k)):
                    last = PE_.matmul(ps[:, 4 + par, t * P:(t + 1) * P], lhs(c, t),
                                      wdn[0:k[c], slot, c, :], start=(c == 0), stop=(c == len(k) - 1),
                                      skip_group_check=True)
                if midway and t == 1:
                    midway()
            last.then_inc(M.dn, 1)

        def moe_add(dve, M, n, bank, g, gate, late):
            dve.wait_ge(M.dn, n + 1)
            if late:
                dve.wait_ge(M.acc, n)
            for t in range(TPG):
                a = acc[:, ds(TPG * g + t, 1), :].rearrange("p o d -> p (o d)")
                y = ps[:, bank, t * P:(t + 1) * P]
                if gate is None:
                    last = V.tensor_tensor(a, y, a, ALU.add)
                else:
                    last = V.scalar_tensor_tensor(out=a, in0=y, scalar=gate(TPG * g + t), in1=a,
                                                  op0=ALU.mult, op1=ALU.add)
            last.then_inc(M.acc, 1)

        def hid0(par, c, lo, n):
            return ring[:, 2 * par + c // 2, (c % 2) * GT + lo:(c % 2) * GT + lo + n]

        def up0(pe, n, g, slot, first):
            for c in range(FC0):
                if c % 2 == 0 and not first:
                    pe.wait_ge(M0.hid, 2 * n - 1 + c // 2)
                last = PE_.matmul(ps[:, c, :], wup[:, slot, c * P:(c + 1) * P], xnT_all[:, g * GT:(g + 1) * GT],
                                  start=True, stop=True)
                if c % 2:
                    last.then_inc(M0.up, 1)

        def gelu0(act, n, par, late):
            for u in range(2):
                act.wait_ge(M0.up, 2 * n + u + 1)
                if u == 0 and late:
                    act.wait_ge(M0.dn, n - 1)
                S_.activation(ring[:, 2 * par + u, :], ps[:, 2 * u:2 * u + 2, :].rearrange("p b n -> p (b n)"),
                              ACT.Gelu).then_inc(M0.hid, 1)

        def down0(pe, n, par, slot, first):
            moe_down(pe, M0, n, par, [P] * FC0, lambda c, t: hid0(par, c, t * P, P), slot, first)

        NL = 4

        def slot0(x):
            return (x + 1) % 2

        def up_half(pe, n, g, u, slot):
            wait_past(pe, M0.hid, 2 * n + u)
            for c in (2 * u, 2 * u + 1):
                last = PE_.matmul(ps[:, 5 + c % 2, :], wup[:, slot, c * P:(c + 1) * P], xnT_all[:, cols(g)],
                                  start=True, stop=True)
            last.then_inc(M0.up, 1)

        def gelu_half(act, n, u, par, used):
            act.wait_ge(M0.up, 2 * n + u + 1)
            if u == 0:
                wait_past(act, M0.dn, used)
            S_.activation(ring[:, 2 * par + u, :], ps[:, 5:7, :].rearrange("p b n -> p (b n)"),
                          ACT.Gelu).then_inc(M0.hid, 1)

        def down_half(pe, n, par, slot, u):
            if u == 0:
                pe.wait_ge(M0.hid, 2 * n + 2)
                wait_past(pe, M0.acc, n)
            for t in (2 * u, 2 * u + 1):
                for c in range(FC0):
                    last = PE_.matmul(ps[:, 7, t * P:(t + 1) * P], hid0(par, c, t * P, P), wdn[:, slot, c, :],
                                      start=(c == 0), stop=(c == FC0 - 1), skip_group_check=True)
            if u:
                last.then_inc(M0.dn, 1)

        def shared_pe(pe, b):
            def at(k):
                if k == 0:
                    if isinstance(b, int) and b == 0:
                        pe.wait_ge(w0[1], 32)
                    up_half(pe, b, b, 0, 1)
                    up_half(pe, b, b, 1, 1)
                if k == 2:
                    down_half(pe, b, 0, 1, 0)
                    down_half(pe, b, 0, 1, 1)
            return None if b is None else at

        def shared_act(act, b):
            def at(k):
                if k < 2:
                    gelu_half(act, b, k, 0, b)
            return None if b is None else at

        def shared_dve(dve, b):
            def at(k):
                if k == 2:
                    moe_add(dve, M0, b, 7, b, None, not (isinstance(b, int) and b == 0))
            return None if b is None else at

        def halves(r, k):
            if r < NG:
                return [6 * r + k]
            return [6 * r + k] if k < 4 else ([6 * r + 4, 6 * r + 5] if k == 4 else [6 * r + 6, 6 * r + 7])

        def routed_pe(pe, r):
            def at(k):
                for h in halves(r, k):
                    n, u = NG + h // 2, h % 2
                    if n % NG == 0 and u == 0:
                        x = n // NG
                        pe.wait_ge(w0[slot0(x)], 32 * (x // 2 + 1))
                    up_half(pe, n, n % NG, u, slot0(n // NG))
                    if n > NG:
                        down_half(pe, n - 1, (n - 1) % 2, slot0((n - 1) // NG), u)
                if r == NG and k == 5:
                    n = NG * (NL + 1) - 1
                    for u in range(2):
                        down_half(pe, n, n % 2, slot0(n // NG), u)
            return at

        def routed_act(act, r):
            def at(k):
                for h in halves(r, k):
                    n, u = NG + h // 2, h % 2
                    gelu_half(act, n, u, n % 2, n - 1)
            return at

        def routed_dve(dve, r):
            def add(n):
                moe_add(dve, M0, n, 7, n % NG, lambda t: gates[:, t, n // NG - 1:n // NG], True)

            def at(k):
                for h in halves(r, 2 * k) + halves(r, 2 * k + 1):
                    n, u = NG + h // 2, h % 2
                    if u and n > NG:
                        add(n - 1)
                if r == NG and k == 2:
                    add(NG * (NL + 1) - 1)
            return at

        def up1(pe, n, g, slot, first, beside=None):
            for c in range(3):
                if not first:
                    if c != 1:
                        pe.wait_ge(M1.act, 2 * n - 1 + c // 2)
                    if c:
                        pe.wait_ge(M1.hid, 2 * n - 2 + c)
                m = (P, P, UP_AT + IR1)[c]
                last = PE_.matmul(ps[0:m, c, :], wup[:, slot, c * P:c * P + m],
                                  xnT_all[:, g * GT:(g + 1) * GT], start=True, stop=True)
                if c:
                    last.then_inc(M1.up, 1)
                if beside:
                    beside(c)

        def silu1(act, n, par, late):
            act.wait_ge(M1.up, 2 * n + 1)
            if late:
                act.wait_ge(M1.hid, 2 * n - 2)
            S_.activation(ring[:, 2 * par, 0:GT], ps[:, 0, :], ACT.Silu).then_inc(M1.act, 1)
            act.wait_ge(M1.up, 2 * n + 2)
            S_.activation(ring[UP_AT:UP_AT + IR1, 2 * par, GT:2 * GT], ps[0:IR1, 2, :], ACT.Silu).then_inc(M1.act, 1)

        def mult1(dve, n, par, late):
            if late:
                dve.wait_ge(M1.dn, n - 1)
            for c, (lo, hi) in enumerate(((0, P), (UP_AT, UP_AT + IR1))):
                dve.wait_ge(M1.act, 2 * n + 1 + c)
                dve.wait_ge(M1.up, 2 * n + 1 + c)
                V.tensor_tensor(ring[lo:hi, 2 * par + 1, c * GT:(c + 1) * GT],
                                ring[lo:hi, 2 * par, c * GT:(c + 1) * GT], ps[lo:hi, 1 + c, :],
                                ALU.mult).then_inc(M1.hid, 1)

        def down1(pe, n, par, slot, first, midway=None):
            moe_down(pe, M1, n, par, (P, UP_AT + IR1),
                     lambda c, t: ring[0:(P, UP_AT + IR1)[c], 2 * par + 1, c * GT + t * P:c * GT + (t + 1) * P],
                     slot, first, midway)

        NU1 = 2 * NG
        NKB = NT
        ROW = 8 * 16

        def where1(u):
            return 4 * (u // NG), GT * (u % NG)

        def max_bank(t, kc, spare):
            if spare is None:
                return 6 + kc % 2, 2
            i = 4 * (t % 2) + kc
            return (6, 7, 6, 7, spare, 6, 7, spare)[i], (3, 3, 2, 2, 5, 3, 3, 3)[i]

        def max_product(pe, u, hd, t, kc, spare=None):
            h0, q0 = where1(u)
            bank, ago = max_bank(t, kc, spare)
            pe.wait_ge(MX.mxr, 64 * u + 16 * hd + 4 * t + kc + 3 - ago)
            PE_.matmul(ps[:, bank, :],
                       q1s[0:KS1, ds(hd + h0, 1), q0 + P * t:q0 + P * (t + 1)].rearrange("p o q -> p (o q)"),
                       k1s[0:KS1, ds(hd + h0, 1), kc * GT:(kc + 1) * GT].rearrange("p o q -> p (o q)"),
                       start=True, stop=True).then_inc(MX.mx, 1)

        def max_reduce(dve, u, hd, t, spare=None):
            m0 = 64 * u + 16 * hd + 4 * t
            for kc in range(NG):
                dve.wait_ge(MX.mx, m0 + kc + 1)
                V.tensor_reduce(mxp[:, u % 2, ds(4 * hd + t, 1), kc:kc + 1],
                                ps[:, max_bank(t, kc, spare)[0], :].unsqueeze(1), AX.X, ALU.max).then_inc(MX.mxr, 1)

        def max_tail_dve(dve, u):
            dve.wait_ge(MX.mxr, 64 * u + 66)
            if u:
                dve.wait_ge(MX.mnT, u)
            V.tensor_reduce(mneg[:, 0, :], mxp[:, u % 2, :, :], AX.X, ALU.max).then_inc(MX.mn, 1)
            dve.wait_ge(MX.mn, 4 * u + 1)
            V.tensor_scalar(mneg[:, 1, :], mneg[:, 0, :], -1.0, None, ALU.mult).then_inc(MX.mn, 1)
            dve.wait_ge(MX.mn, 4 * u + 2)
            V.tensor_copy(mparts[:, 0, :], mneg[:, 1, :]).then_inc(MX.mn, 1)
            dve.wait_ge(MX.mn, 4 * u + 3)
            V.tensor_tensor(mparts[:, 1, :], mneg[:, 1, :], mparts[:, 0, :], ALU.subtract).then_inc(MX.mn, 1)

        def max_tail_pe(pe, u, bank):
            pe.wait_ge(MX.mn, 4 * u + 4)
            PE_.transpose(ps_bf[0:32, bank * 1024:bank * 1024 + P], mparts[:, :, :].rearrange("p a m -> p (a m)"),
                          identb[:, :]).then_inc(MX.mnT, 1)

        def max_tail_act(act, u, bank):
            act.wait_ge(MX.mnT, u + 1)
            if u:
                act.wait_ge(MX.row, ROW * u)
            S_.activation(mT[:, :], ps_bf[0:32, bank * 1024:bank * 1024 + P], ACT.Copy).then_inc(MX.mnTc, 1)

        def max_tail_sp(sp, u):
            h0, q0 = where1(u)
            sp.wait_ge(MX.mnTc, u + 1)
            for a in range(2):
                for h in range(4):
                    sp.dma_start(q1s[KS1 + a:KS1 + a + 1, h0 + h, q0:q0 + GT],
                                 mT[16 * a + 4 * h:16 * a + 4 * h + 4, :]).then_inc(MX.row, 16)

        def att1_score(pe, n, u, kb, w, first=False):
            h0, q0 = where1(u)
            if not first:
                pe.wait_ge(AB.prob, 2 * n + w - 1)
            for h in (2 * w, 2 * w + 1):
                last = PE_.matmul(ps[:, h, :], k1s[0:KM1, h0 + h, ds(P * kb, P)],
                                  q1s[0:KM1, h0 + h, q0:q0 + GT], start=True, stop=True)
            last.then_inc(AB.score, 1)

        def att1_exp(act, n, par, late):
            for w in range(2):
                act.wait_ge(AB.score, 2 * n + w + 1)
                if late:
                    act.wait_ge(AB.pv, n - 1)
                S_.activation(ring[:, 2 * par + w, :], ps[:, 2 * w:2 * w + 2, :].rearrange("p b n -> p (b n)"),
                              ACT.Exp, scale=float(HD1) ** -0.5).then_inc(AB.prob, 1)

        def att1_pv(pe, n, par, bank, w):
            if w == 0:
                pe.wait_ge(AB.vst, n + 1)
            pe.wait_ge(AB.prob, 2 * n + w + 1)
            for h in (2 * w, 2 * w + 1):
                last = PE_.matmul(ps[32 * h:32 * h + 32, bank, :], vst[:, par, h, :],
                                  ring[:, 2 * par + w, (h % 2) * GT:(h % 2 + 1) * GT],
                                  start=False, stop=True, skip_group_check=True)
            if w:
                last.then_inc(AB.pv, 1)

        def att1_clear(pe, bank):
            for h in range(4):
                PE_.matmul(ps[32 * h:32 * h + 32, bank, :], zerob[:, 0:32], zerob[:, :], start=True, stop=False,
                           skip_group_check=True)

        B1 = (1, 2, 3, 4)
        BP = 5

        def act_prep1(act, f, b):
            if b is not None:
                act.wait_ge(S.qkvc, 2 * (2 * NG + b) + 2)
                act.wait_ge(S.pT, 2 * NG + b)
                S_.activation(parts1[:, :, 0, :], qkv_st[:, :, 0:2 * P], ACT.Copy).then_inc(S.h, 1)
                act.wait_ge(S.r1, 2 * NG + b + 1)
                S_.activation(parts1[:, :, 1, :], res1, ACT.Copy).then_inc(S.m, 1)
            if f is not None:
                n = NG + f
                act.wait_ge(S.cen, n + 1)
                S_.activation(sq_ln, cen, ACT.Square).then_inc(S.sq, 1)
                act.wait_ge(S.var, n + 1)
                act_root(STAT4, S.std)
            if b is not None:
                S_.activation(v_all[:, ds(TPG * b, TPG), :, 0:HD1],
                              qkv_st[:, :, 2 * P:3 * P].rearrange("p t (h d) -> p t h d", d=HD1),
                              ACT.Copy).then_inc(S.vc, 1)
            if f is not None:
                act_xnT(act, n, f)
            if b is not None:
                act.wait_ge(S.pT, 2 * NG + b + 1)
                act.wait_ge(S.scr, 32 * (2 * NG + b))
                for half in range(2):
                    S_.activation(pT[:, 3 * half:3 * half + 3, :].rearrange("p a n -> p (a n)"),
                                  ps_bf[:, BP * 1024 + 3 * GT * half:BP * 1024 + 3 * GT * (half + 1)],
                                  ACT.Copy).then_inc(S.pTc, 1)
            if f is not None:
                act.wait_ge(S.lg, n + 1)
                S_.activation(lg[:, ds(TPG * f, TPG), :],
                              ps[:, 0, 0:TPG * (E0 + 1)].rearrange("p (t e) -> p t e", t=TPG),
                              ACT.Copy).then_inc(S.lgc, 1)

        def pe_prep1(pe, f, b):
            if b is not None:
                pe.wait_ge(S.l, 2 * NG + b + 1)
                pe.wait_ge(S.pTc, 2 * (2 * NG + b))
                for half in range(2):
                    for a in range(3):
                        for t in range(TPG):
                            at = BP * 1024 + (3 * half + a) * GT + t * P
                            last = PE_.transpose(ps_bf[:, at:at + P], parts1[:, t, a, half * P:(half + 1) * P],
                                                 identb[:, :])
                last.then_inc(S.pT, 1)
            if f is not None:
                n = NG + f
                pe.wait_ge(S.xn, n + 1)
                pe.wait_ge(S.lgc, n)
                pe_transpose(xn_st, 0, S.xnT)
                pe.wait_ge(S.xnTc, 2 * n + 1)
                pe.wait_ge(S.qkvc, 2 * (n + NG))
                for t in range(TPG):
                    last = PE_.matmul(ps[:, B1[t], 0:3 * P], aT_st[:, t * P:(t + 1) * P], wl1[:, :],
                                      start=True, stop=True)
                    if t % 2:
                        last.then_inc(S.qkv, 1)
                for t in range(TPG):
                    last = PE_.matmul(ps[:, 0, t * (E0 + 1):(t + 1) * (E0 + 1)], aT_st[:, t * P:(t + 1) * P],
                                      rw1[:, :], start=True, stop=True)
                last.then_inc(S.lg, 1)

        def dve_prep1(dve, f, b):
            link = Chain(dve, S.dch, NG * (KF0[0] + KF0[1] + 2 * KB0) + (0 if f is None else f) * KF1)
            if f is not None:
                n = NG + f
                link(V.tensor_tensor(cen, grp(s_all, f), grp(acc, f), ALU.mult))
                link(V.tensor_tensor(cen, grp(x_all, f), cen, ALU.add))
            if b is not None:
                dve.wait_ge(S.h, 2 * NG + b + 1)
                V.tensor_tensor(res1, qkv_st[:, :, 0:2 * P], parts1[:, :, 0, :], ALU.subtract).then_inc(S.r1, 1)
            if f is not None:
                dve_centre(dve, link, cen, keep=grp(x_all, f))
            if b is not None:
                dve.wait_ge(S.m, 2 * NG + b + 1)
                dve.wait_ge(S.r1, 2 * NG + b + 1)
                V.tensor_tensor(parts1[:, :, 2, :], res1, parts1[:, :, 1, :], ALU.subtract).then_inc(S.l, 1)
            if f is not None:
                dve.wait_ge(S.sq, n + 1)
                mean_square(link, sq_ln, STAT4, 1.0 / P, LN_EPS, S.var)
                dve_xn(dve, link, n)
                dve.wait_ge(S.h, n + NG)
                dve.wait_ge(S.vc, n + NG)
                for t in range(TPG):
                    if t % 2 == 0:
                        dve.wait_ge(S.qkv, 2 * NG + 2 * f + 1 + t // 2)
                    last = V.tensor_tensor(qkv_st[:, t, :], ps[:, B1[t], 0:3 * P], bias1[:, :], ALU.add)
                last.then_inc(S.qkvc, 2)
                dve.wait_ge(S.qkvc, 2 * (n + NG) + 2)
                assert link.k == KF1

        def load(sp, w, slot, up_src, dn_src, k, c, n_up):
            sp.dma_start(wup[:, slot, 0:n_up], up_src.rearrange("o d f -> (o d) f")).then_inc(w[slot], 16)
            sp.dma_start(wdn[0:k, slot, 0:c, :], dn_src.rearrange("o f c d -> (o f) c d")).then_inc(w[slot], 16)

        def load0(sp, x):
            if x >= 2:
                sp.wait_ge(M0.dn, NG * (x - 1))
            load(sp, w0, slot0(x), A.up0[x:x + 1], A.dn0[x:x + 1], P, FC0, F0)

        def sp_tail(sp):
            for it in range(NG):
                if 2 + it <= NL:
                    load0(sp, 2 + it)
                sp_stack0(sp, NG + it, it, 1, AG.pv, N_SETS)
            for x in range(NL + 1, E0 + 1):
                load0(sp, x)

            def load1(x, slot):
                load(sp, w1, slot, A.up1[ds(x, 1)], A.dn1[ds(x, 1)], P, 2, 2 * P + UP_AT + IR1)
            sp.wait_ge(M0.dn, 4 * (E0 + 1))
            load1(0, 0)
            load1(1, 1)
            with sp.Fori(0, NG) as it:
                n = 2 * NG + it
                sp.wait_ge(AL.o, NT)
                sp.wait_ge(S.pTc, 2 * n + 2)
                for half in range(2):
                    sp.dma_start(scr[2, ds(it, 1), :, 3 * half:3 * half + 3, :].rearrange("o p a t -> p (o a) t"),
                                 pT[:, 3 * half:3 * half + 3, :]).then_inc(S.scr, 16)
                sp.wait_ge(S.scr, 32 * n + 32)
                for r, (a, b) in enumerate(PRODUCTS1):
                    for dst, part in ((q1s, a), (k1s, 3 + b)):
                        sp.dma_start(dst[r * HD1:(r + 1) * HD1, :, cols(it)],
                                     scr[2, ds(it, 1), :, part, :].rearrange("o (h d) t -> d (o h) t", d=HD1))\
                            .then_inc(s_stk1, 16)
            with sp.Fori(1, E1 // 2) as i:
                for e in range(2):
                    sp.wait_ge(M1.dn, 8 * i + 4 * e - 4)
                    load1(2 * i + e, e)
            for u in range(NU1):
                max_tail_sp(sp, u)
            with sp.Fori(0, NG) as it:
                sp.wait_ge(s_y, it + 1)
                sp.dma_start(A.out[cols(it), :].rearrange("(t p) d -> p t d", p=P),
                             grp(x_all, it)).then_inc(s_out, 16)
            sp.wait_ge(s_out, 16 * NG)

        def pool_tail(pool):
            G_.memset(zerob[:, :], 0.0).then_inc(s_zero, 1)
            pool.wait_ge(S.vc, 2 * NG)
            pool.wait_ge(AG.pv, N_SETS)
            pool.wait_ge(s_zero, 1)

            def stage(t, par, first, last):
                if not first:
                    pool.wait_ge(AL.pv, 4 * t - 4)
                G_.tensor_copy(vst[:, par, :, 0:HD + 1],
                               v_all[:, ds(t, 1), 0:HKV, 0:HD + 1].rearrange("p o h d -> p (o h) d")
                               ).then_inc(AL.vst, 1)
            loc_loop(pool, stage)
            pool.wait_ge(AL.pv, 4 * NT)
            G_.memset(k1s[KS1:KM1, :, :], 1.0).then_inc(s_zero, 1)
            pool.wait_ge(s_zero, 2)
            pool.wait_ge(M0.acc, NG * (E0 + 1))
            for par in range(2):
                G_.memset(ring[0:UP_AT, 2 * par + 1, GT:2 * GT], 0.0).then_inc(s_zero, 1)
            pool.wait_ge(s_zero, 4)
            pool.wait_ge(S.vc, 3 * NG)
            for u in range(NU1):
                h0, _ = where1(u)

                def stage1(n, e, kb, late):
                    if late:
                        pool.wait_ge(AB.pv, n - 1)
                    G_.tensor_copy(vst[:, e, :, 0:VW],
                                   v_all[:, ds(kb, 1), h0:h0 + 4, :].rearrange("p o h d -> p (o h) d")
                                   ).then_inc(AB.vst, 1)
                if u == 0:
                    stage1(0, 0, 0, False)
                    stage1(1, 1, 1, False)
                with pool.Fori(1 if u == 0 else 0, NKB // 2) as j:
                    for e in range(2):
                        stage1(NKB * u + 2 * j + e, e, 2 * j + e, True)

        def act_out(act, u):
            act.wait_ge(AB.pv, NKB * (u + 1))
            if u >= 2:
                act.wait_ge(AB.fin, u - 1)
            S_.activation(oT[:, u % 2, :], ps[:, 4 + u % 2, :], ACT.Copy).then_inc(AB.oT, 1)

        def act_tail(act):
            for r in range(NG + 1):
                act_prep0(act, *round_of(r), 1, routed_act(act, r))
            act.wait_ge(M0.dn, NG * (NL + 1))

            def tile(t, par, first, last):
                w = P if last else LW
                for kv in range(HKV):
                    loc_exp(act, t, kv, w, not first)
                    if kv == 0 and not first:
                        loc_out(act, t - 1, 1 - par)
            loc_loop(act, tile)
            loc_out(act, NT - 1, 1)
            with act.Fori(0, (E0 - NL) // 2) as i:
                for k in range(2 * NG):
                    f = 2 * i + k // NG
                    if k % NG == 0:
                        act_ost(act, NG + f, f, AL.o, NT)
                    gelu0(act, NG * (NL + 1) + 8 * i + k, k % 2, True)
                    if k % NG == 1:
                        act_oT(act, NG + f, 6)
            act.wait_ge(M0.acc, 4 * (E0 + 1))
            S_.activation(acc[:, :, :], acc[:, :, :], ACT.Silu).then_inc(s_silu, 1)
            over_rounds(act, lambda f, b: act_prep1(act, f, b), 1)
            route_act(act, R1, True)
            silu1(act, 0, 0, False)
            silu1(act, 1, 1, False)
            for n in range(2, 8):
                silu1(act, n, n % 2, True)
            with act.Fori(1, E1 // 2) as i:
                for k in range(8):
                    silu1(act, 8 * i + k, k % 2, True)
            max_tail_act(act, 0, 3)
            act.wait_ge(M1.acc, 4 * E1)
            S_.activation(acc[:, :, :], acc[:, :, :], ACT.Silu).then_inc(s_silu, 1)
            for u in range(NU1):
                n0 = NKB * u

                def pair(j, late):
                    for e in range(2):
                        att1_exp(act, n0 + 2 * j + e, e, late)
                pair(0, u > 0)
                if u:
                    act_out(act, u - 1)
                pair(1, True)
                pair(2, True)
                att1_exp(act, n0 + 6, 0, True)
                if u + 1 < NU1:
                    max_tail_act(act, u + 1, 4 + (u + 1) % 2)
                att1_exp(act, n0 + 7, 1, True)
                with act.Fori(4, 8) as j:
                    pair(j, True)
            act_out(act, NU1 - 1)

        def pe_moe(units, up, down):
            for k, (n, g, slot, first) in enumerate(units):
                up(n, g, slot, first)
                if k:
                    down(*units[k - 1])
            down(*units[-1])

        def pe_tail(pe):
            pe.wait_ge(AG.o, N_UNITS)
            for r in range(NG + 1):
                pe_prep0(pe, *round_of(r), 1, routed_pe(pe, r))
            pe.wait_ge(M0.acc, NG * (NL + 1))
            pe.wait_ge(M0.hid, 2 * NG * (NL + 1))
            pe.wait_ge(S.stk, 2 * NG * STK0)
            pe.wait_ge(S.pTc, 4 * NG)
            pe.wait_ge(S.qkvc, 4 * NG)
            pe.wait_ge(AG.o, N_UNITS)
            loc_score(pe, 0, 0, LW, True)

            def tile(t, par, first, last):
                w = P if last else LW
                for kv in range(HKV):
                    if kv + 1 < HKV:
                        loc_score(pe, t, kv + 1, w, first and kv == 0)
                    elif not last:
                        loc_score(pe, t + 1, 0, P if isinstance(t, int) and t == NT - 2 else LW, False)
                    loc_pv(pe, t, par, kv, w, first)
                    if kv == 1 and not first:
                        loc_fin(pe, t - 1, 1 - par)
            loc_loop(pe, tile)
            loc_fin(pe, NT - 1, 1)

            pe.wait_ge(AL.oT, NT)
            with pe.Fori(0, (E0 - NL) // 2) as i:
                pe.wait_ge(w0[0], 32 * (NL // 2) + 32 * i + 32)

                def up(n, g, slot, first):
                    if slot and g == 0:
                        pe.wait_ge(w0[1], 32 * (NL // 2 + 1) + 32 * i + 32)
                    up0(pe, n, g, slot, first)
                    if g == 1:
                        pe_oT(pe, NG + 2 * i + slot, 6)
                    if g == 3:
                        pe_oproj(pe, NG + 2 * i + slot, 1, 7)
                pe_moe([(NG * (NL + 1) + 8 * i + 4 * e + g, g, e, False) for e in range(2) for g in range(NG)],
                       up, lambda n, g, slot, first: down0(pe, n, g % 2, slot, first))

            over_rounds(pe, lambda f, b: pe_prep1(pe, f, b), 1)

            pe.wait_ge(S.pTc, 6 * NG)
            pe.wait_ge(S.lgc, 2 * NG)
            pe.wait_ge(S.qkvc, 6 * NG)

            pe.wait_ge(s_zero, 4)

            def pair1(i, first, beside=None):
                pe.wait_ge(w1[0], 32 * i + 32)
                for k in range(2 * NG):
                    e, g = k // NG, k % NG
                    if k == NG:
                        pe.wait_ge(w1[1], 32 * i + 32)
                    last = (lambda: beside(k)(3)) if beside else None
                    up1(pe, 8 * i + k, g, e, first and k == 0, beside and beside(k))
                    if k or not first:
                        down1(pe, 8 * i + k - 1, (k - 1) % 2, (k - 1) // NG % 2, first and k <= 2, last)
                    elif last:
                        last()
            pair1(0, True)
            pe.wait_ge(s_stk1, 2 * len(PRODUCTS1) * 16 * NG)
            for u in range(2):
                with pe.Fori(0, 2) as s:
                    pair1(1 + 2 * u + s, False,
                          lambda k: lambda kc: max_product(pe, u, 2 * s + k // 4, k % 4, kc))

            max_tail_pe(pe, 0, 3)
            down1(pe, 4 * E1 - 1, 1, 1, False)

            pe.wait_ge(s_zero, 2)
            pe.wait_ge(M1.acc, 4 * E1)
            pe.wait_ge(MX.row, ROW)
            pe.wait_ge(M1.hid, 2 * 4 * E1)
            for w in range(2):
                att1_score(pe, 0, 0, 0, w, True)
            for u in range(NU1):
                n0, bank, other = NKB * u, 4 + u % 2, 4 + (u + 1) % 2

                def pair(j, hd, t0, spare=None, last=False):
                    for e in range(2):
                        n = n0 + 2 * j + e

                        def score(w):
                            if not (last and e):
                                att1_score(pe, n + 1, u, 2 * j + e + 1, w)
                            elif u + 1 < NU1:
                                if w == 0:
                                    pe.wait_ge(MX.row, ROW * (u + 2))
                                att1_score(pe, n + 1, u + 1, 0, w)

                        def maximum(kc):
                            if u + 2 < NU1:
                                if spare is not None and e == 1 and kc == 0:
                                    pe.wait_ge(MX.mnTc, u + 2)
                                max_product(pe, u + 2, hd, t0 + e, kc, spare)
                        score(0)
                        maximum(0)
                        score(1)
                        maximum(1)
                        if isinstance(j, int) and j + e == 0:
                            pe.wait_ge(MX.mnTc, u + 1)
                            if u >= 2:
                                pe.wait_ge(AB.o, u - 1)
                            if 0 < u and u + 1 < NU1:
                                pe.wait_ge(MX.mxr, 64 * (u + 2) + 2)
                            att1_clear(pe, bank)
                        att1_pv(pe, n, e, bank, 0)
                        att1_pv(pe, n, e, bank, 1)
                        maximum(2)
                        maximum(3)
                pair(0, 0, 0)
                pair(1, 0, 2)
                if u:
                    fin_transposes(pe, AB, u - 1, other)
                pair(2, 1, 0)
                if u + 1 < NU1:
                    if u:
                        pe.wait_ge(AB.o, u)
                    max_tail_pe(pe, u + 1, other)
                if u + 2 < NU1:
                    pe.wait_ge(MX.mxr, 64 * (u + 2) + 24 + 2)
                with pe.Fori(1, 3) as i:
                    pair(2 * i + 1, i, 2, other)
                    pair(2 * i + 2, i + 1, 0, other)
                pair(7, 3, 2, other, last=True)
            fin_transposes(pe, AB, NU1 - 1, 4 + (NU1 - 1) % 2)

        def dve_tail(dve):
            for r in range(NG + 1):
                dve_prep0(dve, *round_of(r), 1, routed_dve(dve, r))

            def tile(t, par, first, last):
                if not first:
                    loc_normalise(dve, t - 1)
            loc_loop(dve, tile)
            loc_normalise(dve, NT - 1)
            with dve.Fori(0, (E0 - NL) // 2) as i:
                for e in range(2):
                    for g in range(NG):
                        if g == 3:
                            dve_oproj(dve, NG + 2 * i + e, 2 * i + e, 7, grp(s_all, 2 * i + e))
                        moe_add(dve, M0, NG * (NL + 1) + 8 * i + 4 * e + g, 4 + g % 2, g,
                                lambda t: gates[:, t, ds(NL + 2 * i + e, 1)], True)
            dve.wait_ge(s_silu, 1)
            over_rounds(dve, lambda f, b: dve_prep1(dve, f, b), 1)
            V.memset(acc[:, :, :], 0.0).then_inc(s_cleared, 1)
            route_dve(dve, R1, True)

            def gate1(x):
                return lambda t: gates[:, t, ds(x, 1)]
            dve.wait_ge(s_cleared, 1)
            for _ in range(2):
                V.nop().then_inc(MX.mxr, 1)

            def pair1(i, first, u=None, s=None):
                for k in range(2 * NG):
                    if u is not None:
                        max_reduce(dve, u, 2 * s + k // 4, k % 4)
                    mult1(dve, 8 * i + k, k % 2, not (first and k < 2))
                    if k or not first:
                        moe_add(dve, M1, 8 * i + k - 1, 4 + (k - 1) % 2, (k - 1) % NG,
                                gate1(2 * i + (k - 1) // NG), not (first and k == 1))
            pair1(0, True)
            for u in range(2):
                with dve.Fori(0, 2) as s:
                    pair1(1 + 2 * u + s, False, u, s)
                if u == 0:
                    max_tail_dve(dve, 0)
            moe_add(dve, M1, 4 * E1 - 1, 5, NG - 1, gate1(E1 - 1), True)

            def finish(u):
                g = u % NG
                dve_normalise(dve, AB, u, 4 + u % 2, g, 64 * (u // NG), HD1)
                if u < NG:
                    return
                dve.wait_ge(AB.o, u + 1)
                if g == 0:
                    dve.wait_ge(s_silu, 2)
                else:
                    dve.wait_ge(s_y, g)
                V.tensor_tensor(xn_st[:, :, :], grp(o_all, g), grp(acc, g), ALU.mult).then_inc(s_prod, 1)
                dve.wait_ge(s_prod, g + 1)
                V.tensor_tensor(grp(x_all, g), grp(x_all, g), xn_st[:, :, :], ALU.add).then_inc(s_y, 1)
            def items(u, hd, tiles, spare=None):
                if u < NU1:
                    for t in tiles:
                        max_reduce(dve, u, hd, t, spare)
            for u in range(NU1):
                items(u + 2, 0, (0, 1))
                if u + 1 < NU1:
                    max_tail_dve(dve, u + 1)
                items(u + 2, 0, (2, 3))
                if u:
                    finish(u - 1)
                items(u + 2, 1, (0, 1))
                items(u + 2, 1, (2, 3), 4 + (u + 1) % 2)
                if u + 2 < NU1:
                    with dve.Fori(2, NG) as hd:
                        items(u + 2, hd, range(4), 4 + (u + 1) % 2)
            finish(NU1 - 1)

        @block.sync
        def _(sp):
            def load_x(g, done):
                sp.dma_start(x_all[:, TPG * g:TPG * (g + 1), :],
                             A.x[GT * g:GT * (g + 1), :].rearrange("(t p) d -> p t d", p=P)).then_inc(done, 16)
            load_x(0, s_x0)
            for dst, src in first:
                sp.dma_start(dst, src).then_inc(s_first, 16)
            for g in range(1, NG):
                load_x(g, s_x)
            for dst, src in consts:
                sp.dma_start(dst, src).then_inc(s_const, 16)
            load0(sp, 0)
            load0(sp, 1)
            for it in range(NG):
                sp_stack0(sp, it, it, 0, None, None)
                sp.wait_ge(S.stk, STK0 * (it + 1))
            sp_tail(sp)

        @block.gpsimd
        def _(pool):
            G_.memset(v_all[:, :, :, :], 1.0).then_inc(s_vones, 1)
            G_.memset(vst[:, :, :, :], 0.0).then_inc(s_vones, 1)
            pool.wait_ge(s_vones, 2)
            pool.wait_ge(S.vc, NG)
            def stage_v(n, par, kb, kv, late):
                if late:
                    pool.wait_ge(AG.pv, n - 1)
                G_.tensor_copy(vst[:, par, 0:1, 0:HD + 1],
                               v_all[:, ds(kb, 1), kv, 0:HD + 1]).then_inc(AG.vst, 1)
            for c, g, kv, n0 in plan0():
                for i in range(4):
                    stage_v(n0 + i, i % 2, TPG * g + i, kv, n0 + i >= 2)
                if g:
                    with pool.Fori(0, g) as j:
                        for e in range(4):
                            stage_v(n0 + 4 + 4 * j + e, e % 2, 4 * j + e, kv, True)
            pool_tail(pool)

        @block.scalar
        def _(act):
            act.wait_ge(s_first, ALL_FIRST)
            S_.activation(identb[:, :], ident[:, :], ACT.Copy).then_inc(s_identb, 1)
            act.wait_ge(s_fold, 1)
            S_.activation(wqkv[:, 0, P:NQKV], ps[:, 5, 0:2 * HKV * HD], ACT.Copy).then_inc(s_foldc, 1)
            act.wait_ge(s_vones, 2)

            def step(f, b):
                if isinstance(b, int) and b == 0:
                    act.wait_ge(s_const, ALL_CONST)
                    S_.activation(tri[:, :], tri_in, ACT.Copy)
                    S_.activation(band[:, :], band_in, ACT.Copy)
                    act.wait_ge(s_fold, 2)
                    S_.activation(wl1[:, :], ps[:, 4, 0:3 * P], ACT.Copy).then_inc(s_foldc, 1)
                act_prep0(act, f, b, 0, shared_act(act, b))
            over_rounds(act, step, 2)
            route_act(act, R0, False)
            act.wait_ge(M0.dn, NG)

            def exps(n, u, par, w, late):
                act.wait_ge(AG.score, 2 * n + u + 1)
                if late:
                    act.wait_ge(AG.pv, n - 1)
                S_.activation(ring[:, 2 * par + u, 0:2 * w].rearrange("p (h q) -> p h q", h=2),
                              ps[:, 2 * u:2 * u + 2, 0:w], ACT.Exp, scale=float(HD) ** -0.5).then_inc(AG.prob, 1)
            for c, g, kv, n0 in plan0():
                for i in range(4):
                    for u in range(2):
                        exps(n0 + i, u, i % 2, GT - P * i, n0 + i >= 2)
                if g:
                    with act.Fori(0, g) as j:
                        for e in range(4):
                            for u in range(2):
                                exps(n0 + 4 + 4 * j + e, u, e % 2, GT, True)
            act_tail(act)

        @block.tensor
        def _(pe):
            pe.wait_ge(s_first, ALL_FIRST)
            PE_.matmul(ps[:, 5, 0:2 * HKV * HD], kvdT[:, :], kvup[:, :], start=True, stop=True).then_inc(s_fold, 1)
            pe.wait_ge(s_foldc, 1)
            pe.wait_ge(s_identb, 1)

            def step(f, b):
                if isinstance(b, int) and b == 0:
                    pe.wait_ge(s_const, ALL_CONST)
                    for m in range(3):
                        for c in range(2):
                            last = PE_.matmul(ps[:, 4, m * P:(m + 1) * P], lrV[:, m, c, :], lrU[:, m, c, :],
                                              start=(c == 0), stop=(c == 1))
                    last.then_inc(s_fold, 1)
                    pe.wait_ge(s_foldc, 2)
                pe_prep0(pe, f, b, 0, shared_pe(pe, b))
            over_rounds(pe, step, 2)
            pe.wait_ge(M0.acc, NG)
            pe.wait_ge(M0.hid, 2 * NG)

            pe.wait_ge(S.stk, STK0)
            pe.wait_ge(S.pTc, 2 * NG)
            pe.wait_ge(S.lgc, NG)
            pe.wait_ge(S.qkvc, 2 * NG)
            units = list(plan0())
            att0_score(pe, 0, 0, 0, 0, 0, True, first=True)
            for c, g, kv, n0 in units:
                bank = 4 + c % 2
                nxt = units[c + 1] if c + 1 < len(units) else None

                def first_of_next():
                    if nxt:
                        if nxt[1] > g:
                            pe.wait_ge(S.stk, STK0 * (nxt[1] + 1))
                        att0_score(pe, nxt[3], nxt[1], nxt[2], TPG * nxt[1], 0, True)
                for i in range(4):
                    if i < 3:
                        att0_score(pe, n0 + i + 1, g, kv, TPG * g + i + 1, P * (i + 1), True)
                    elif g:
                        att0_score(pe, n0 + 4, g, kv, 0, 0, False)
                    else:
                        first_of_next()
                    if i == 0 and c >= 2:
                        pe.wait_ge(AG.oT, c - 1)
                    att0_pv(pe, n0 + i, i % 2, bank, P * i, i == 0, False)
                    if i == 1 and c:
                        fin_transposes(pe, AG, c - 1, 6)
                if g > 1:
                    with pe.Fori(0, g - 1) as j:
                        for e in range(4):
                            att0_score(pe, n0 + 4 + 4 * j + e + 1, g, kv, 4 * j + e + 1, 0, False)
                            att0_pv(pe, n0 + 4 + 4 * j + e, e % 2, bank, 0, False, False)
                if g:
                    for kb in range(4 * g - 4, 4 * g):
                        if kb + 1 < 4 * g:
                            att0_score(pe, n0 + 4 + kb + 1, g, kv, kb + 1, 0, False)
                        else:
                            first_of_next()
                        att0_pv(pe, n0 + 4 + kb, kb % 2, bank, 0, False, kb + 1 == 4 * g)
            fin_transposes(pe, AG, N_UNITS - 1, 6)
            pe_tail(pe)

        @block.vector
        def _(dve):
            dve.wait_ge(s_x0, 16)

            def step(f, b):
                if isinstance(b, int) and b == 0:
                    dve.wait_ge(s_x, 16 * (NG - 1))
                    dve.wait_ge(s_const, ALL_CONST)
                dve_prep0(dve, f, b, 0, shared_dve(dve, b))
            over_rounds(dve, step, 2)
            route_dve(dve, R0, False)
            for c, g, kv, n0 in plan0():
                if c:
                    dve_out(dve, AG, c - 1, 4 + (c - 1) % 2, n0)
                if c:
                    dve_normalise(dve, AG, c - 1, 6, (c - 1) // HKV, ((c - 1) % HKV) * 32, HD)
            dve_out(dve, AG, N_UNITS - 1, 4 + (N_UNITS - 1) % 2, N_SETS)
            dve_normalise(dve, AG, N_UNITS - 1, 6, NG - 1, 96, HD)
            dve_tail(dve)


def _arrays(i):
    import numpy as np

    f = {k: np.ascontiguousarray(np.asarray(v)) for k, v in i.items()}
    tok = np.arange(T, dtype=np.float32)
    cos, sin = np.empty((P, 2, NT, HD), np.float32), np.empty((P, 2, NT, HD), np.float32)
    for n, base in enumerate((1000000.0, 10000.0)):
        pair = np.arange(0, HD, 2, dtype=np.float32) / np.float32(HD)
        inv = (1.0 / np.float32(base) ** pair).astype(np.float32)
        fr = (tok[:, None] * inv[None, :]).reshape(NT, P, HD // 2).transpose(1, 0, 2)
        cos[:, n, :, 0::2] = cos[:, n, :, 1::2] = np.cos(fr)
        sin[:, n, :, 0::2], sin[:, n, :, 1::2] = -np.sin(fr), np.sin(fr)
    k, q = np.arange(P)[:, None], np.arange(LW)[None, :]
    zero, masked = np.float32(0), np.float32(MASKED)

    def blocks(w):
        h, a, b = w.shape
        out = np.zeros((h * a, h * b), w.dtype)
        for n in range(h):
            out[n * a:(n + 1) * a, n * b:(n + 1) * b] = w[n]
        return out.reshape(2, P, h * b).transpose(1, 0, 2)

    L = "L1_attn_"
    gu = f["L1_ffn_experts_gate_up"]
    sg, su, sd = f["L1_ffn_shared_gate_w"], f["L1_ffn_shared_up_w"], f["L1_ffn_shared_down_w"]
    g1 = np.concatenate([gu[:, :I1], sg.reshape(2, I1, P)])
    u1 = np.concatenate([gu[:, I1:], su.reshape(2, I1, P)])
    gap = np.zeros((E1, UP_AT - IR1, P), np.float32)
    up1 = np.concatenate([g1[:, :P], u1[:, :P], g1[:, P:], gap, u1[:, P:]], axis=1).transpose(0, 2, 1)
    dn1 = np.concatenate([f["L1_ffn_experts_down"], sd.reshape(P, 2, I1).transpose(1, 0, 2)])
    dn1 = dn1.transpose(0, 2, 1)
    short = np.zeros((E1, P, P), np.float32)
    short[:, UP_AT:UP_AT + IR1] = dn1[:, P:]
    dn1 = np.stack([dn1[:, :P], short], axis=2)
    dn0 = np.concatenate([f["L0_ffn_shared_down"], f["L0_ffn_routed_down"]])
    a = dict(
        x=f["L0_attn_hidden"][0],
        ident=np.eye(P, dtype=np.float32),
        tri=np.where(q[:, :P] >= k, zero, masked), band=np.where((q >= k) & (q - k < WIN), zero, masked),
        cosT=cos, sinT=sin,
        normw=np.stack([f["L0_attn_norm1_w"], f["L0_attn_norm2_w"]], axis=1),
        kvdT=f["L0_attn_g_kv_down"].T, kvup=np.concatenate([f["L0_attn_g_k_up"], f["L0_attn_g_v_up"]], axis=1),
        g_wq=f["L0_attn_g_wq"],
        l_wqkv=np.concatenate([f["L0_attn_l_wq"], f["L0_attn_l_wk"], f["L0_attn_l_wv"]], axis=1),
        wo=np.stack([f["L0_attn_g_wo"], f["L0_attn_l_wo"]], axis=1),
        router0=f["L0_ffn_router_w"],
        router1=np.concatenate([f["L1_ffn_gate_w"], f["L1_ffn_shared_expert_gate_w"]]).T,
        lrV=np.stack([blocks(f[L + "V" + m]) for m in "qkv"], axis=1),
        lrU=np.stack([blocks(f[L + "U" + m].transpose(0, 2, 1)) for m in "qkv"], axis=1),
        bias1=np.broadcast_to(np.concatenate([f[L + "b" + m].reshape(-1) for m in "qkv"]), (P, 3 * P)),
        up0=np.concatenate([f["L0_ffn_shared_up"], f["L0_ffn_routed_up"]]),
        dn0=dn0.reshape(E0 + 1, FC0, P, P).transpose(0, 2, 1, 3),
        up1=up1, dn1=dn1,
    )
    return {k: np.ascontiguousarray(v) for k, v in a.items()}


class Arrays:

    def __init__(self, a):
        self.band, self.bias1, self.cosT, self.dn0 = (
            a[x] for x in ("band", "bias1", "cosT", "dn0"))
        self.dn1, self.g_wq, self.ident, self.kvdT = (
            a[x] for x in ("dn1", "g_wq", "ident", "kvdT"))
        self.kvup, self.l_wqkv, self.lrU, self.lrV = (
            a[x] for x in ("kvup", "l_wqkv", "lrU", "lrV"))
        self.normw, self.router0, self.router1, self.sinT = (
            a[x] for x in ("normw", "router0", "router1", "sinT"))
        self.tri, self.up0, self.up1, self.wo = (
            a[x] for x in ("tri", "up0", "up1", "wo"))
        self.x = a["x"]


def kernel(**inputs):
    import concourse.bacc as bacc
    from concourse.bass_utils import run_bass_kernel_spmd

    arrays = {f"in_{k}": v for k, v in _arrays(inputs).items()}
    nc = bacc.Bacc("TRN2", target_bir_lowering=False, num_devices=1)
    A = Arrays({name[3:]: nc.dram_tensor(name, a.shape, mybir.dt.from_np(a.dtype), kind="ExternalInput").ap()
                for name, a in arrays.items()})
    A.out = nc.dram_tensor("out_x", (T, P), mybir.dt.float32, kind="ExternalOutput").ap()
    build(nc, A)
    r = run_bass_kernel_spmd(nc, [arrays], core_ids=[0])
    return r.results[0]["out_x"].reshape(1, T, P)
```
